# Optimizing a Trainium2 kernel written in Bass

```python
import numpy as np
import jax
import jax.numpy as jnp

def _softmax(x, axis=-1):
    return jax.nn.softmax(x, axis=axis)

def _gelu(x):
    return jax.nn.gelu(x, approximate=True)

def _silu(x):
    return jax.nn.silu(x)

def _sigmoid(x):
    return jax.nn.sigmoid(x)

def _layernorm(x, axis=-1, eps=1e-05):
    m = jnp.mean(x, axis=axis, keepdims=True)
    v = jnp.var(x, axis=axis, keepdims=True)
    return (x - m) / jnp.sqrt(v + eps)

def _scatter_add(tgt, idx, src, axis=0):
    return tgt.at[idx].add(src)

def _segment_sum(src, seg, n):
    return jax.ops.segment_sum(src, seg, n)
kernel_name = 'mk_seq_postln_d2_jaxref_r8_0a9ecb'

def setup_inputs(seed: int=0):
    np.random.seed(seed)
    _w = jnp.asarray

    def _L0_attn_setup():
        import jax, jax.numpy as jnp
        import numpy as np
        H = 128
        I = 512
        TAU = 9
        LN_EPS = 1e-12

        def _l2_normalize(x):
            n = jnp.sqrt(jnp.sum(x * x, axis=-1, keepdims=True))
            return x / jnp.maximum(n, 1e-12)
        key = jax.random.key(seed)
        k1, k2, k3, k4 = jax.random.split(key, 4)
        return {'hidden_states': jax.random.normal(k1, (4, 256, H), jnp.float32), 'ln_weight': jnp.ones((H,), jnp.float32), 'ln_bias': jnp.zeros((H,), jnp.float32), 'k_weight': 0.02 * jax.random.normal(k2, (I, H), jnp.float32), 'q_weight': 0.02 * jax.random.normal(k3, (I, H), jnp.float32), 'bias': 0.001 * jax.random.normal(k4, (H,), jnp.float32)}
    _L0_attn_in = _L0_attn_setup()

    def _L0_ffn_setup():
        import jax, jax.numpy as jnp
        import numpy as np
        HIDDEN = 128
        NUM_EXPERTS = 8
        TOP_K = 2
        B, S = (4, 128)
        key = jax.random.key(seed)
        ks = jax.random.split(key, 8)
        H, E = (HIDDEN, NUM_EXPERTS)
        sc = lambda fan_in: 1.0 / np.sqrt(fan_in)
        x = jax.random.normal(ks[0], (B, S, H), dtype=jnp.float32)
        Wr = jax.random.uniform(ks[1], (H, E), minval=-sc(H), maxval=sc(H), dtype=jnp.float32)
        br = jax.random.uniform(ks[2], (E,), minval=-sc(H), maxval=sc(H), dtype=jnp.float32)
        W1 = jax.random.uniform(ks[3], (E, H, 2 * H), minval=-sc(H), maxval=sc(H), dtype=jnp.float32)
        b1 = jax.random.uniform(ks[4], (E, 2 * H), minval=-sc(H), maxval=sc(H), dtype=jnp.float32)
        W2 = jax.random.uniform(ks[5], (E, 2 * H, H), minval=-sc(2 * H), maxval=sc(2 * H), dtype=jnp.float32)
        b2 = jax.random.uniform(ks[6], (E, H), minval=-sc(2 * H), maxval=sc(2 * H), dtype=jnp.float32)
        return {'x': x, 'Wr': Wr, 'br': br, 'W1': W1, 'b1': b1, 'W2': W2, 'b2': b2}
    _L0_ffn_in = _L0_ffn_setup()

    def _L1_attn_setup():
        import jax, jax.numpy as jnp
        import numpy as np
        D_MODEL, D_STATE, D_CONV, EXPAND = (128, 16, 4, 2)
        D_INNER = EXPAND * D_MODEL
        BATCH, SEQ = (4, 512)
        DT_MIN, DT_MAX = (0.001, 0.1)
        key = jax.random.key(seed)
        ks = jax.random.split(key, 7)
        s = 0.02
        x = jax.random.normal(ks[0], (BATCH, SEQ, D_MODEL), jnp.float32)
        W_in = jax.random.normal(ks[1], (D_MODEL, 2 * D_INNER), jnp.float32) * s
        conv_w = jax.random.normal(ks[2], (D_INNER, 1, D_CONV), jnp.float32) * 0.3
        conv_b = jnp.zeros((D_INNER,), jnp.float32)
        A_log = jnp.log(jnp.arange(1, D_STATE + 1, dtype=jnp.float32) * jnp.pi) + DT_MIN
        A_log = jnp.broadcast_to(A_log[None, :], (D_INNER, D_STATE)).copy()
        D = jnp.ones((D_INNER,), jnp.float32).at[::2].set(-1.0)
        W_x = jax.random.normal(ks[3], (D_INNER, D_STATE), jnp.float32) * s
        W_dt = jax.random.normal(ks[4], (D_INNER, D_INNER), jnp.float32) * s
        dt = jnp.exp(jax.random.uniform(ks[5], (D_INNER,)) * (np.log(DT_MAX) - np.log(DT_MIN)) + np.log(DT_MIN))
        b_dt = dt + jnp.log(-jnp.expm1(-dt))
        W_out = jax.random.normal(ks[6], (D_INNER, D_MODEL), jnp.float32) * s
        return dict(x=x, W_in=W_in, conv_w=conv_w, conv_b=conv_b, A_log=A_log, D=D, W_x=W_x, W_dt=W_dt, b_dt=b_dt, W_out=W_out)
    _L1_attn_in = _L1_attn_setup()

    def _L1_ffn_setup():
        import jax, jax.numpy as jnp
        import numpy as np
        CAPACITY_FACTOR = 1.0

        def _route(token_inputs, Wg, capacity):
            dt = token_inputs.dtype
            logits = jnp.einsum('bnd,de->bne', token_inputs, Wg)
            gates = jax.nn.softmax(logits, axis=-1)
            expert_idx = jnp.argmax(gates, axis=-1)
            mask = jax.nn.one_hot(expert_idx, Wg.shape[1], dtype=dt)
            gate = jnp.sum(gates * mask, axis=-1)
            pos = jnp.cumsum(mask, axis=1) * mask - mask
            keep = mask * (pos < capacity).astype(dt)
            pos_oh = jax.nn.one_hot(pos.astype(jnp.int32), capacity, dtype=dt)
            dispatch = keep[..., None] * pos_oh
            combine = dispatch * gate[:, :, None, None]
            return (dispatch, combine)
        key = jax.random.key(seed)
        k1, k2, k3, k4 = jax.random.split(key, 4)
        B, N, D, E, H = (8, 256, 128, 8, 512)
        return {'token_inputs': jax.random.normal(k1, (B, N, D), dtype=jnp.float32), 'Wg': jax.random.normal(k2, (D, E), dtype=jnp.float32) * 0.02, 'W1': jax.random.normal(k3, (E, D, H), dtype=jnp.float32) * 0.02, 'W2': jax.random.normal(k4, (E, H, D), dtype=jnp.float32) * 0.02}
    _L1_ffn_in = _L1_ffn_setup()
    _d = {'L0_attn_hidden_states': _L0_attn_in['hidden_states'], 'L0_attn_ln_weight': _L0_attn_in['ln_weight'], 'L0_attn_ln_bias': _L0_attn_in['ln_bias'], 'L0_attn_k_weight': _L0_attn_in['k_weight'], 'L0_attn_q_weight': _L0_attn_in['q_weight'], 'L0_attn_bias': _L0_attn_in['bias'], 'L0_ffn_Wr': _L0_ffn_in['Wr'], 'L0_ffn_br': _L0_ffn_in['br'], 'L0_ffn_W1': _L0_ffn_in['W1'], 'L0_ffn_b1': _L0_ffn_in['b1'], 'L0_ffn_W2': _L0_ffn_in['W2'], 'L0_ffn_b2': _L0_ffn_in['b2'], 'L1_attn_W_in': _L1_attn_in['W_in'], 'L1_attn_conv_w': _L1_attn_in['conv_w'], 'L1_attn_conv_b': _L1_attn_in['conv_b'], 'L1_attn_A_log': _L1_attn_in['A_log'], 'L1_attn_D': _L1_attn_in['D'], 'L1_attn_W_x': _L1_attn_in['W_x'], 'L1_attn_W_dt': _L1_attn_in['W_dt'], 'L1_attn_b_dt': _L1_attn_in['b_dt'], 'L1_attn_W_out': _L1_attn_in['W_out'], 'L1_ffn_Wg': _L1_ffn_in['Wg'], 'L1_ffn_W1': _L1_ffn_in['W1'], 'L1_ffn_W2': _L1_ffn_in['W2']}
    _x0 = _d['L0_attn_hidden_states']
    _d['L0_attn_hidden_states'] = jax.random.normal(jax.random.fold_in(jax.random.key(seed), 1), (8, 1024, 128), dtype=_x0.dtype)
    del _x0
    return _d

def reference(L0_attn_hidden_states, L0_attn_ln_weight, L0_attn_ln_bias, L0_attn_k_weight, L0_attn_q_weight, L0_attn_bias, L0_ffn_Wr, L0_ffn_br, L0_ffn_W1, L0_ffn_b1, L0_ffn_W2, L0_ffn_b2, L1_attn_W_in, L1_attn_conv_w, L1_attn_conv_b, L1_attn_A_log, L1_attn_D, L1_attn_W_x, L1_attn_W_dt, L1_attn_b_dt, L1_attn_W_out, L1_ffn_Wg, L1_ffn_W1, L1_ffn_W2):

    def _L0_attn_ref(hidden_states, ln_weight, ln_bias, k_weight, q_weight, bias):
        import jax, jax.numpy as jnp
        import numpy as np
        H = 128
        I = 512
        TAU = 9
        LN_EPS = 1e-12

        def _l2_normalize(x):
            n = jnp.sqrt(jnp.sum(x * x, axis=-1, keepdims=True))
            return x / jnp.maximum(n, 1e-12)
        lead_shape = hidden_states.shape[:-1]
        x = hidden_states.reshape(-1, H)
        mu = jnp.mean(x, axis=-1, keepdims=True)
        var = jnp.mean(jnp.square(x - mu), axis=-1, keepdims=True)
        x = (x - mu) * jax.lax.rsqrt(var + LN_EPS) * ln_weight + ln_bias
        Q = _l2_normalize(x)
        K = _l2_normalize(k_weight)
        s = jnp.clip(jnp.einsum('nh,ih->ni', Q, K), -1.0 + 1e-06, 1.0 - 1e-06)
        B = jnp.power(1.0 - jnp.arccos(s) / jnp.pi, TAU)
        X = jnp.einsum('ni,ih->nh', B, q_weight)
        X = _l2_normalize(X) + bias
        return X.reshape(*lead_shape, H)

    def _L0_ffn_ref(x, Wr, br, W1, b1, W2, b2):
        import jax, jax.numpy as jnp
        import numpy as np
        HIDDEN = 128
        NUM_EXPERTS = 8
        TOP_K = 2
        B, S = (4, 128)
        B_, S_, H = x.shape
        xf = x.reshape(-1, H)
        logits = xf @ Wr + br
        topk_w, topk_idx = jax.lax.top_k(logits, TOP_K)
        topk_w = jax.nn.softmax(topk_w, axis=-1)
        gate = jnp.sum(jax.nn.one_hot(topk_idx, NUM_EXPERTS, dtype=xf.dtype) * topk_w[..., None], axis=1)
        h = jax.nn.relu(jnp.einsum('th,ehf->etf', xf, W1) + b1[:, None, :])
        y = jnp.einsum('etf,efh->eth', h, W2) + b2[:, None, :]
        out = jnp.einsum('te,eth->th', gate, y)
        return out.reshape(B_, S_, H)

    def _L1_attn_ref(x, W_in, conv_w, conv_b, A_log, D, W_x, W_dt, b_dt, W_out):
        import jax, jax.numpy as jnp
        import numpy as np
        D_MODEL, D_STATE, D_CONV, EXPAND = (128, 16, 4, 2)
        D_INNER = EXPAND * D_MODEL
        BATCH, SEQ = (4, 512)
        DT_MIN, DT_MAX = (0.001, 0.1)
        B, L, _ = x.shape
        d_inner = W_in.shape[1] // 2
        K = conv_w.shape[-1]
        xz = x @ W_in
        xs, z = (xz[..., :d_inner], xz[..., d_inner:])
        xc = jax.lax.conv_general_dilated(xs.transpose(0, 2, 1), conv_w, window_strides=(1,), padding=[(K - 1, 0)], feature_group_count=d_inner, dimension_numbers=('NCH', 'OIH', 'NCH'))
        xc = xc + conv_b[None, :, None]
        xs = jax.nn.silu(xc.transpose(0, 2, 1))
        dt = jax.nn.softplus(xs @ W_dt + b_dt)
        Bs = xs @ W_x
        A_exp = jnp.exp(A_log)

        def step(h, inp):
            dt_t, Bs_t, x_t = inp
            h = h * jnp.exp(-A_exp[None] * dt_t[..., None]) + Bs_t[:, None, :]
            return (h, jnp.sum(h, axis=-1) + D * x_t)
        h0 = jnp.zeros((B, d_inner, A_exp.shape[1]), x.dtype)
        _, ys = jax.lax.scan(step, h0, (dt.transpose(1, 0, 2), Bs.transpose(1, 0, 2), xs.transpose(1, 0, 2)))
        y = ys.transpose(1, 0, 2) * jax.nn.silu(z)
        return y @ W_out

    def _L1_ffn_ref(token_inputs, Wg, W1, W2):
        import jax, jax.numpy as jnp
        import numpy as np
        CAPACITY_FACTOR = 1.0

        def _route(token_inputs, Wg, capacity):
            dt = token_inputs.dtype
            logits = jnp.einsum('bnd,de->bne', token_inputs, Wg)
            gates = jax.nn.softmax(logits, axis=-1)
            expert_idx = jnp.argmax(gates, axis=-1)
            mask = jax.nn.one_hot(expert_idx, Wg.shape[1], dtype=dt)
            gate = jnp.sum(gates * mask, axis=-1)
            pos = jnp.cumsum(mask, axis=1) * mask - mask
            keep = mask * (pos < capacity).astype(dt)
            pos_oh = jax.nn.one_hot(pos.astype(jnp.int32), capacity, dtype=dt)
            dispatch = keep[..., None] * pos_oh
            combine = dispatch * gate[:, :, None, None]
            return (dispatch, combine)
        B, N, D = token_inputs.shape
        E = Wg.shape[1]
        capacity = int(N * CAPACITY_FACTOR // E)
        dispatch, combine = _route(token_inputs, Wg, capacity)
        expert_inputs = jnp.einsum('bnd,bnec->becd', token_inputs, dispatch)
        h = jax.nn.gelu(jnp.einsum('becd,edh->bech', expert_inputs, W1))
        expert_outputs = jnp.einsum('bech,ehd->becd', h, W2)
        output = jnp.einsum('becd,bnec->bnd', expert_outputs, combine)
        return output
    x = L0_attn_hidden_states
    x = _layernorm(x + _L0_attn_ref(x, L0_attn_ln_weight, L0_attn_ln_bias, L0_attn_k_weight, L0_attn_q_weight, L0_attn_bias), axis=-1)
    x = _layernorm(x + _L0_ffn_ref(x, L0_ffn_Wr, L0_ffn_br, L0_ffn_W1, L0_ffn_b1, L0_ffn_W2, L0_ffn_b2), axis=-1)
    x = _layernorm(x + _L1_attn_ref(x, L1_attn_W_in, L1_attn_conv_w, L1_attn_conv_b, L1_attn_A_log, L1_attn_D, L1_attn_W_x, L1_attn_W_dt, L1_attn_b_dt, L1_attn_W_out), axis=-1)
    x = _layernorm(x + _L1_ffn_ref(x, L1_ffn_Wg, L1_ffn_W1, L1_ffn_W2), axis=-1)
    return x

_drawn_inputs = setup_inputs


def setup_inputs(seed=0):
    import zlib

    import numpy as np

    out = dict(_drawn_inputs(seed))
    spreads = {'L0_attn_ln_weight': (1.0, 0.6),
     'L0_attn_ln_bias': (0.0, 0.8),
     'L1_attn_conv_b': (0.0, 0.1)}
    factors = {'L0_attn_bias': 8.0,
     'L0_ffn_b1': 3.914,
     'L1_attn_conv_w': 6.359,
     'L1_attn_W_x': 3.377,
     'L1_attn_W_dt': 8.0,
     'L1_ffn_Wg': 6.757,
     'L1_ffn_W1': 6.454,
     'L1_ffn_W2': 6.37}
    for name, (base, spread) in spreads.items():
        noise = np.random.default_rng([zlib.crc32(name.encode()), seed]).standard_normal(out[name].shape)
        drawn = base * np.exp(spread * noise) if base else spread * noise
        out[name] = jnp.asarray(drawn.astype(out[name].dtype))
    for name, factor in factors.items():
        out[name] = (out[name] * factor).astype(out[name].dtype)
    return out
```

```python
import math
from contextlib import ExitStack

import concourse.bass as bass
from concourse import mybir


V_STEPS = 59
A_STEPS = 15
P_STEPS = 2
CONSTS = 17


def build_layer_stack(
    nc: bass.Bass,
    x_in, ln_w, ln_b, k_w, q_w, l0_bias,
    wr, br, w1b, b1b, w2b, b2b,
    w_in, conv_w, conv_b, a_log, d_skip, w_x, w_dt, b_dt, w_out,
    wg, w1d, w2d,
    out,
):
    fp32, bf16, u32 = mybir.dt.float32, mybir.dt.bfloat16, mybir.dt.uint32
    ACT = mybir.ActivationFunctionType
    ALU = mybir.AluOpType
    AX = mybir.AxisListType.X

    P = 128
    NB, T, H = x_in.shape
    NT = T // P
    CH = 512
    NC_ = T // CH
    TPC = CH // P
    I = k_w.shape[0]
    NI = I // P
    E = wr.shape[1]
    FB = w1b.shape[2]
    NFB = FB // P
    DI = w_in.shape[1] // 2
    ND = DI // P
    NS = a_log.shape[1]
    TAPS = conv_w.shape[2]
    FD = w1d.shape[2]
    NFD = FD // P
    CAP = T // E
    SLOTS = E * CAP
    assert CAP == P and H == P and NC_ == 2

    S_MAX = 1.0 - 1e-6
    N2_SCALE = 2.0 ** 16
    RN_BIAS = 0.5 * math.log(N2_SCALE)

    slot_x = nc.dram_tensor("slot_x", (SLOTS, H), fp32, kind="Internal").ap()
    slot_y = nc.dram_tensor("slot_y", (SLOTS, H), fp32, kind="Internal").ap()

    ctx = ExitStack()
    with ctx:
        def sb(name, shape, dt=fp32):
            return ctx.enter_context(nc.sbuf_tensor(name, shape, dt))

        per, sems = {}, {}

        def sem(name, per_row=0):
            sems[name] = ctx.enter_context(nc.semaphore(name))
            per[name] = per_row
            return sems[name]

        def need(eng, name, b, k):
            if k or not isinstance(b, int) or b:
                eng.wait_ge(sems[name], b * per[name] + k)

        ident = sb("ident", [P, P])
        identb = sb("identb", [P, P], bf16)
        onesb = sb("onesb", [P, P], bf16)
        before = sb("before", [P, P], bf16)
        sel_gate = sb("sel_gate", [3 * E, E, P], bf16)
        sel_bs = sb("sel_bs", [3 * NS, NS, P], bf16)
        first = sb("first", [P, E])
        base128 = sb("base128", [P, E])
        lnw_bc = sb("lnw_bc", [P, H])
        lnb_bc = sb("lnb_bc", [P, H])
        bias_bc = sb("bias_bc", [P, H])
        br_bc = sb("br_bc", [P, E])
        kn = sb("kn", [P, NI, H])
        knT = sb("knT", [P, I])
        qw = sb("qw", [P, NI, H])
        wr_s = sb("wr_s", [P, E])
        w1b_s = sb("w1b_s", [P, E, FB])
        b1_s = sb("b1_s", [P, E, NFB])
        w2b_s = sb("w2b_s", [P, E, NFB, H])
        b2_f = sb("b2_f", [3 * E, H])
        b2_r = sb("b2_r", [3 * E, H])
        b2_p = sb("b2_p", [3 * E, 3, H], bf16)
        win_s = sb("win_s", [P, 2 * DI])
        cw_s = sb("cw_s", [P, ND, TAPS])
        cb_s = sb("cb_s", [P, ND])
        nega = sb("nega", [P, ND, NS])
        dsk = sb("dsk", [P, ND])
        wx_s = sb("wx_s", [P, ND, NS])
        wdt_s = sb("wdt_s", [P, ND, DI])
        bdt_s = sb("bdt_s", [P, ND])
        wout_s = sb("wout_s", [P, ND, H])
        wg_s = sb("wg_s", [P, E])
        w1d_s = sb("w1d_s", [P, E, FD])
        w2d_s = sb("w2d_s", [P, E, NFD, H])
        X = sb("X", [P, NT, H])
        XB = sb("XB", [P, NT, H])
        XL = sb("XL", [P, NT, H])
        SQ = sb("SQ", [P, NT, H])
        Y = sb("Y", [P, NT, H])
        XN = sb("XN", [P, NT, H])
        YG = sb("YG", [P, NT, H])
        XT = sb("XT", [P, T])
        SC = sb("SC", [P, NC_, NI, CH])
        L1 = sb("L1", [P, NC_, NI, CH])
        L2 = sb("L2", [P, NC_, NI, CH])
        bst = sb("bst", [P, NT, 6])
        mv = sb("mv", [P, NT, 2])
        lnv = sb("lnv", [P, NT])
        rstd = sb("rstd", [P, NT])
        n2 = sb("n2", [P, NT])
        ln2 = sb("ln2", [P, NT])
        rn = sb("rn", [P, NT])
        eps_a = sb("eps_a", [P, 1])
        eps_l = sb("eps_l", [P, 1])
        half = sb("half", [P, 1])
        held = sb("held", [P, 1])
        rnb = sb("rnb", [P, 1])
        lg = sb("lg", [P, NT, E])
        t8a = sb("t8a", [P, NT, E])
        t8b = sb("t8b", [P, NT, E])
        oh1 = sb("oh1", [P, NT, E])
        oh2 = sb("oh2", [P, NT, E])
        m1 = sb("m1", [P, NT])
        m2 = sb("m2", [P, NT])
        ms = sb("ms", [P, NT])
        gw1 = sb("gw1", [P, NT])
        gw2 = sb("gw2", [P, NT])
        ex = sb("ex", [P, NT, E])
        g3 = sb("g3", [P, NT, 3, E], bf16)
        g3T = sb("g3T", [3 * E, T], bf16)
        maskb = sb("maskb", [P, NT, E], bf16)
        pos = sb("pos", [P, NT])
        slot = sb("slot", [P, NT])
        over = sb("over", [P, NT])
        gk = sb("gk", [P, NT])
        put_i = sb("put_i", [P, NT], u32)
        get_i = sb("get_i", [P, NT], u32)
        HR = sb("HR", [P, 2, CH])
        HG = sb("HG", [P, 2, CH])
        OT = SQ[:, :, :].rearrange("p (c r) h -> p c (r h)", c=NC_)
        XS = sb("XS", [P, ND, TAPS - 1 + T])
        ZS = sb("ZS", [P, ND, T])
        XC = sb("XC", [P, ND, T])
        XA = sb("XA", [P, ND, T])
        DT = sb("DT", [P, ND, T])
        SP_ = L1[:, 0, :, :].rearrange("p a b -> p (a b)").rearrange("p (n t) -> p n t", n=ND)
        bs3 = sb("bs3", [P, NT, 3, NS], bf16)
        bsr = sb("bsr", [P, NT, NS])
        bs3T = sb("bs3T", [3 * NS, T], bf16)
        dA = L2[:, 0, :, :].rearrange("p a b -> p (a b)").rearrange("p (n t) -> p n t", n=2)
        HS = L2[:, 1, :, :].rearrange("p a b -> p (a b)").rearrange("p (n t) -> p n t", n=2)
        GE = L2[:, 1, :, :].rearrange("p a b -> p (a b)")[:, 0:2 * FD].rearrange("p (k f s) -> p k f s", k=2, f=NFD)
        XD = SC[:, 0, :, :].rearrange("p a b -> p (a b)")[:, 0:SLOTS].rearrange("p (e d) -> p e d", e=E)
        XDT = L1[:, 0, :, :].rearrange("p a b -> p (a b)")[:, 0:SLOTS]
        YD = L2[:, 0, :, :].rearrange("p a b -> p (a b)")[:, 0:SLOTS].rearrange("p (e d) -> p e d", e=E)

        PS = ctx.enter_context(nc.psum_tensor("PS", [P, 8, CH], fp32))
        g3T_ps = PS[:, 7, :].bitcast(bf16)
        bs3T_ps = PS[:, 7, :].bitcast(bf16)

        for name, n in (
            ("x_loaded", 16), ("out_stored", 16),
            ("v_step", V_STEPS), ("a_step", A_STEPS), ("p_step", P_STEPS),
            ("xh_done", 1), ("xln_done", 1), ("sqA_done", 1),
            ("n2_done", 2), ("rn_done", 2), ("qn_done", 1), ("qT_ps_done", 2), ("qT_done", 2),
            ("s_ps_done", 2), ("clip_done", 2), ("logs_done", 2), ("dlog_done", 2), ("atan_done", 2),
            ("t4_done", 2), ("bpow_done", 2), ("xo_ps_done", 2), ("sqX_done", 2),
            ("mv_done", 5), ("rstd_done", 5), ("ln_done", 4),
            ("xT_ps_done", 6), ("xT_done", 6),
            ("lg_ps_done", 2), ("lg_done", 2), ("m_done", 2), ("ex_done", 2),
            ("g3_done", 1), ("g3T_ps_done", 1), ("g3T_done", 1),
            ("z_ps_done", 2 * E * NFB), ("relu_done", 2 * E * NFB), ("gate_ps_done", 2 * E),
            ("hg_done", 2 * E * NFB), ("oB_acc_done", 2 * E * NFB), ("oT_done", 2), ("oB_ps_done", 2), ("yB_done", 1),
            ("xz_ps_done", 8), ("xs_done", 4), ("silz_done", 4), ("conv_done", ND), ("xa_done", ND),
            ("dt_ps_done", 4), ("abs_done", 4), ("vrel_done", 4), ("sp_done", ND), ("dt_done", ND),
            ("bs_ps_done", 1), ("bs3_done", 1), ("bs3T_ps_done", 1), ("bs3T_done", 1),
            ("bc_ps_done", ND * NS), ("dA_done", ND * NS), ("scan_done", ND * NS), ("y_acc_done", ND * NS),
            ("yx_done", ND), ("yz_done", ND), ("oC_ps_done", 2), ("yC_done", 1),
            ("mask_done", 1), ("pos_ps_done", 1), ("put_done", 1), ("get_done", 1),
            ("scattered", 16 * NT), ("slots_loaded", 16), ("xdT_ps_done", 2), ("xdT_done", 2),
            ("g_ps_done", E), ("gelu_done", E), ("yD_ps_done", E), ("yD_done", 2), ("slots_stored", 16),
            ("gathered", 16 * NT), ("yF_done", 1),
        ):
            sem(name, n)
        consts_done = sem("consts_done")
        weights_in = sem("weights_in")
        setup_v = sem("setup_v")
        setup_a = sem("setup_a")
        setup_pe = sem("setup_pe")
        slots_zeroed = sem("slots_zeroed")
        N_WEIGHTS = 23 + 2 * E
        W_ALL = 16 * N_WEIGHTS
        N_CONST = 13

        block = ctx.enter_context(nc.Block())

        def need_apart(eng, name, b, k):
            eng.wait_ge(consts_done, CONSTS)
            need(eng, name, b, k)

        def per_tile(ap):
            return ap[:, :].unsqueeze(2).to_broadcast([P, NT, E])

        @block.sync
        def _(sp):
            loads = [
                (lnw_bc[:, :], ln_w.partition_broadcast(P)), (lnb_bc[:, :], ln_b.partition_broadcast(P)),
                (bias_bc[:, :], l0_bias.partition_broadcast(P)), (br_bc[:, :], br.partition_broadcast(P)),
                (kn[:, :, :], k_w.rearrange("(n p) h -> p n h", p=P)),
                (qw[:, :, :], q_w.rearrange("(n p) h -> p n h", p=P)),
                (wr_s[:, :], wr), (w1b_s[:, :, :], w1b.rearrange("e d f -> d e f")),
                (b1_s[:, :, :], b1b.rearrange("e (n p) -> p e n", p=P)),
                (b2_f[0:E, :], b2b), (b2_f[E:2 * E, :], b2b), (b2_f[2 * E:3 * E, :], b2b),
                (win_s[:, :], w_in), (cw_s[:, :, :], conv_w.rearrange("(n p) o k -> p n (o k)", p=P)),
                (cb_s[:, :], conv_b.rearrange("(n p) -> p n", p=P)),
                (nega[:, :, :], a_log.rearrange("(n p) s -> p n s", p=P)),
                (dsk[:, :], d_skip.rearrange("(n p) -> p n", p=P)),
                (wx_s[:, :, :], w_x.rearrange("(n p) s -> p n s", p=P)),
                (wdt_s[:, :, :], w_dt.rearrange("(n p) s -> p n s", p=P)),
                (bdt_s[:, :], b_dt.rearrange("(n p) -> p n", p=P)),
                (wout_s[:, :, :], w_out.rearrange("(n p) h -> p n h", p=P)),
                (wg_s[:, :], wg), (w1d_s[:, :, :], w1d.rearrange("e d f -> d e f")),
            ]
            for dst, src in ((w2b_s, w2b), (w2d_s, w2d)):
                loads += [(dst[:, e], src[e].rearrange("(n p) h -> p n h", p=P)) for e in range(E)]
            assert len(loads) == N_WEIGHTS
            for dst, src in loads:
                sp.dma_start(dst, src, allow_slow_non_contiguous=True).then_inc(weights_in, 16)
            sp.wait_ge(consts_done, 1)
            sp.dma_start(slot_x.rearrange("(e p) d -> p e d", p=P), YG[:, :, :]).then_inc(slots_zeroed, 16)

            def row(b):
                need(sp, "xln_done", b, 0)
                sp.dma_start(X[:, :, :],
                             x_in[bass.ds(b, 1), :, :].rearrange("o (k p) d -> p (o k) d", p=P))\
                    .then_inc(sems["x_loaded"], 16)
                need(sp, "scattered", b, 16 * NT)
                need(sp, "atan_done", b, 2)
                sp.dma_start(XD, slot_x.rearrange("(e p) d -> p e d", p=P)).then_inc(sems["slots_loaded"], 16)
                need(sp, "yD_done", b, 2)
                sp.dma_start(slot_y.rearrange("(e p) d -> p e d", p=P), YD).then_inc(sems["slots_stored"], 16)
                need(sp, "ln_done", b, 4)
                sp.dma_start(out[bass.ds(b, 1), :, :].rearrange("o (k p) d -> p (o k) d", p=P),
                             XN[:, :, :]).then_inc(sems["out_stored"], 16)

            row(0)
            with sp.Fori(1, NB) as b:
                row(b)
            sp.wait_ge(sems["out_stored"], 16 * NB)

        @block.gpsimd
        def _(pool):
            g = nc.gpsimd
            n = 0

            def const(ins):
                nonlocal n
                n += 1
                ins.then_inc(consts_done, 1)
                pool.wait_ge(consts_done, n)

            const(g.memset(YG[:, :, :], 0.0))
            const(g.memset(ident[:, :], 0.0))
            const(g.affine_select(out=ident[:, :], in_=ident[:, :], compare_op=ALU.not_equal, fill=1.0,
                                  base=0, pattern=[[-1, P]], channel_multiplier=1))
            const(g.tensor_copy(identb[:, :], ident[:, :]))
            const(g.memset(onesb[:, :], 1.0))
            const(g.affine_select(out=before[:, :], in_=onesb[:, :], compare_op=ALU.is_gt, fill=0.0,
                                  base=0, pattern=[[1, P]], channel_multiplier=-1))
            for tile, count in ((sel_gate, E), (sel_bs, NS)):
                const(g.memset(tile[:, :, :], 0.0))
                for part in range(3):
                    ins = g.affine_select(out=tile[:, :, :], in_=tile[:, :, :], compare_op=ALU.not_equal,
                                          fill=1.0, base=-part * count, pattern=[[-1, count], [0, P]],
                                          channel_multiplier=1)
                    ins.then_inc(consts_done, 1)
                    n += 1
                    pool.wait_ge(consts_done, n)
            const(g.iota(first[:, :], pattern=[[-1, E]], base=E, channel_multiplier=0,
                         allow_small_or_imprecise_dtypes=True))
            const(g.iota(base128[:, :], pattern=[[CAP, E]], base=0, channel_multiplier=0,
                         allow_small_or_imprecise_dtypes=True))
            g.memset(XS[:, :, 0:TAPS - 1], 0.0).then_inc(consts_done, 1)
            n += 1
            assert n == CONSTS
            pool.wait_ge(consts_done, n)
            pool.wait_ge(weights_in, W_ALL)

            def row(b):
                need(pool, "x_loaded", b, 16)
                need(pool, "ln_done", b, 0)
                g.tensor_tensor(out=XB[:, :, :], in0=X[:, :, :],
                                in1=bias_bc[:, :].unsqueeze(1).to_broadcast([P, NT, H]), op=ALU.add)\
                    .then_inc(sems["p_step"], 1)
                need(pool, "xh_done", b, 1)
                g.tensor_tensor(out=XL[:, :, :], in0=XL[:, :, :],
                                in1=lnw_bc[:, :].unsqueeze(1).to_broadcast([P, NT, H]), op=ALU.mult)\
                    .then_inc(sems["p_step"], 1)
                need(pool, "p_step", b, 2)
                g.tensor_tensor(out=XL[:, :, :], in0=XL[:, :, :],
                                in1=lnb_bc[:, :].unsqueeze(1).to_broadcast([P, NT, H]), op=ALU.add)\
                    .then_inc(sems["xln_done"], 1)
                for d in range(ND):
                    need(pool, "sp_done", b, d + 1)
                    need(pool, "vrel_done", b, 2 * (d + 1))
                    g.tensor_tensor(out=DT[:, d, :], in0=DT[:, d, :], in1=SP_[:, d, :], op=ALU.add)\
                        .then_inc(sems["dt_done"], 1)
                for d in range(ND):
                    need(pool, "yx_done", b, d + 1)
                    g.tensor_tensor(out=XC[:, d, :], in0=XC[:, d, :], in1=ZS[:, d, :], op=ALU.mult)\
                        .then_inc(sems["yz_done"], 1)
                need_apart(pool, "put_done", b, 1)
                need(pool, "slots_loaded", b, 0)
                pool.wait_ge(slots_zeroed, 16)
                for t in range(NT):
                    g.indirect_dma_start(
                        out=slot_x, out_offset=bass.IndirectOffsetOnAxis(ap=put_i[:, t:t + 1], axis=0),
                        in_=XN[:, t, :], in_offset=None, bounds_check=SLOTS - 1, oob_is_err=False)\
                        .then_inc(sems["scattered"], 16)
                need_apart(pool, "slots_stored", b, 16)
                need(pool, "get_done", b, 1)
                for t in range(NT):
                    g.indirect_dma_start(
                        out=YG[:, t, :], out_offset=None, in_=slot_y,
                        in_offset=bass.IndirectOffsetOnAxis(ap=get_i[:, t:t + 1], axis=0))\
                        .then_inc(sems["gathered"], 16)

            row(0)
            with pool.Fori(1, NB) as b:
                row(b)

        @block.scalar
        def _(act):
            s = nc.scalar
            count = [0]

            def inv_root(dst, tmp, src, scale, bias, out_bias, b, sem_name):
                s.activation(tmp, src, ACT.Ln, bias=bias, scale=scale).then_inc(sems["a_step"], 1)
                count[0] += 1
                need(act, "a_step", b, count[0])
                return s.activation(dst, tmp, ACT.Exp, bias=out_bias, scale=-0.5)

            LOG_EXP = "natural_log_exp_and_others"
            act.wait_ge(weights_in, W_ALL)
            act.wait_ge(consts_done, CONSTS)
            s.preload_act_table_set(LOG_EXP)
            s.activation(nega[:, :, :], nega[:, :, :], ACT.Exp).then_inc(setup_a, 1)
            s.activation(SQ[:, 0:NI, :], kn[:, :, :], ACT.Square).then_inc(setup_a, 1)
            act.wait_ge(setup_v, 3)
            s.activation(ln2[:, 0:NI], n2[:, 0:NI], ACT.Ln, scale=N2_SCALE).then_inc(setup_a, 1)
            act.wait_ge(setup_a, 3)
            s.activation(rn[:, 0:NI], ln2[:, 0:NI], ACT.Exp, bias=rnb[:, 0:1], scale=-0.5).then_inc(setup_a, 1)
            act.wait_ge(setup_pe, 1)
            s.activation(knT[:, :], PS[:, 6, :], ACT.Copy).then_inc(setup_a, 1)

            def norm_stats(b, k, eps):
                need(act, "mv_done", b, k)
                inv_root(rstd[:, :], lnv[:, :], mv[:, :, 1], 1.0, eps, 0.0, b, None)\
                    .then_inc(sems["rstd_done"], 1)

            def copy_xT(b, k):
                for c in range(NC_):
                    need(act, "xT_ps_done", b, 2 * k + c + 1)
                    s.activation(XT[:, c * CH:(c + 1) * CH], PS[:, 6 + c, :], ACT.Copy)\
                        .then_inc(sems["xT_done"], 1)

            def row(b):
                count[0] = 0
                s.preload_act_table_set(LOG_EXP)
                norm_stats(b, 1, eps_a[:, 0:1])
                need(act, "xln_done", b, 1)
                s.activation(SQ[:, :, :], XL[:, :, :], ACT.Square).then_inc(sems["sqA_done"], 1)
                need(act, "n2_done", b, 1)
                inv_root(rn[:, :], ln2[:, :], n2[:, :], N2_SCALE, 0.0, rnb[:, 0:1], b, None)\
                    .then_inc(sems["rn_done"], 1)
                for c in range(NC_):
                    need(act, "qT_ps_done", b, c + 1)
                    s.activation(XT[:, c * CH:(c + 1) * CH], PS[:, 6 + c, :], ACT.Copy)\
                        .then_inc(sems["qT_done"], 1)
                for c in range(NC_):
                    need(act, "clip_done", b, c + 1)
                    s.activation(L1[:, c], SC[:, c], ACT.Ln, bias=1.0).then_inc(sems["a_step"], 1)
                    count[0] += 1
                    s.activation(L2[:, c], SC[:, c], ACT.Ln, bias=1.0, scale=-1.0)\
                        .then_inc(sems["logs_done"], 1)
                for c in range(NC_):
                    need(act, "dlog_done", b, c + 1)
                    s.activation(L2[:, c], L1[:, c], ACT.Tanh, scale=0.25).then_inc(sems["a_step"], 1)
                    count[0] += 1
                    need(act, "a_step", b, count[0])
                    s.activation(SC[:, c], L2[:, c], ACT.Arctan).then_inc(sems["atan_done"], 1)
                    need(act, "atan_done", b, c + 1)
                    s.activation(L1[:, c], SC[:, c], ACT.Square, bias=half[:, 0:1], scale=2.0 / math.pi)\
                        .then_inc(sems["a_step"], 1)
                    count[0] += 1
                    need(act, "a_step", b, count[0])
                    s.activation(L2[:, c], L1[:, c], ACT.Square).then_inc(sems["t4_done"], 1)
                for c in range(NC_):
                    need(act, "xo_ps_done", b, c + 1)
                    s.activation(SQ[:, TPC * c:TPC * (c + 1), :].rearrange("p a b -> p (a b)"),
                                 PS[:, 4 + c, :], ACT.Square).then_inc(sems["sqX_done"], 1)
                s.preload_act_table_set(LOG_EXP)
                need(act, "n2_done", b, 2)
                inv_root(rn[:, :], ln2[:, :], n2[:, :], N2_SCALE, 0.0, rnb[:, 0:1], b, None)\
                    .then_inc(sems["rn_done"], 1)
                norm_stats(b, 2, eps_l[:, 0:1])
                copy_xT(b, 0)
                need(act, "m_done", b, 1)
                s.activation(gw2[:, :], m2[:, :], ACT.Exp).then_inc(sems["ex_done"], 1)
                need(act, "g3T_ps_done", b, 1)
                s.activation(g3T[:, :], g3T_ps[0:3 * E, :], ACT.Copy).then_inc(sems["g3T_done"], 1)
                j = 0
                for c in range(NC_):
                    for e in range(E):
                        for f in range(NFB):
                            need(act, "z_ps_done", b, j + 1)
                            if j >= 2:
                                need(act, "hg_done", b, j - 1)
                            s.activation(HR[:, j % 2, :], PS[:, j % 2, :], ACT.Relu,
                                         bias=b1_s[:, e, f:f + 1]).then_inc(sems["relu_done"], 1)
                            j += 1
                    need(act, "oB_acc_done", b, j)
                    s.activation(OT[:, c, :], PS[:, 4 + c, :], ACT.Copy).then_inc(sems["oT_done"], 1)
                norm_stats(b, 3, eps_l[:, 0:1])
                copy_xT(b, 1)
                k = 0
                for c in range(NC_):
                    for d in range(2 * ND):
                        need(act, "xz_ps_done", b, k + 1)
                        if d < ND:
                            s.activation(XS[:, d, TAPS - 1 + c * CH:TAPS - 1 + (c + 1) * CH],
                                         PS[:, k % 4, :], ACT.Copy).then_inc(sems["xs_done"], 1)
                        else:
                            s.activation(ZS[:, d - ND, c * CH:(c + 1) * CH], PS[:, k % 4, :], ACT.Silu)\
                                .then_inc(sems["silz_done"], 1)
                        k += 1
                for d in range(ND):
                    need(act, "conv_done", b, d + 1)
                    s.activation(XA[:, d, :], XC[:, d, :], ACT.Silu).then_inc(sems["xa_done"], 1)
                s.preload_act_table_set(LOG_EXP)
                k = 0
                for d in range(ND):
                    for c in range(NC_):
                        need(act, "dt_ps_done", b, k + 1)
                        s.activation(SP_[:, d, c * CH:(c + 1) * CH], PS[:, k % 4, :], ACT.Abs,
                                     bias=bdt_s[:, d:d + 1]).then_inc(sems["abs_done"], 1)
                        k += 1
                    need(act, "abs_done", b, k)
                    s.activation(SP_[:, d, :], SP_[:, d, :], ACT.Exp, scale=-1.0).then_inc(sems["a_step"], 1)
                    count[0] += 1
                    need(act, "a_step", b, count[0])
                    s.activation(SP_[:, d, :], SP_[:, d, :], ACT.Ln, bias=1.0).then_inc(sems["sp_done"], 1)
                need(act, "bs3T_ps_done", b, 1)
                s.activation(bs3T[:, :], bs3T_ps[0:3 * NS, :], ACT.Copy).then_inc(sems["bs3T_done"], 1)
                k = 0
                for d in range(ND):
                    need(act, "dt_done", b, d + 1)
                    for n_ in range(NS):
                        if k >= 2:
                            need(act, "scan_done", b, k - 1)
                        s.activation(dA[:, k % 2, :], DT[:, d, :], ACT.Exp, scale=nega[:, d, n_:n_ + 1])\
                            .then_inc(sems["dA_done"], 1)
                        k += 1
                norm_stats(b, 4, eps_l[:, 0:1])
                copy_xT(b, 2)
                need(act, "m_done", b, 2)
                s.activation(ex[:, :, :], lg[:, :, :], ACT.Exp).then_inc(sems["ex_done"], 1)
                for c in range(2):
                    need(act, "xdT_ps_done", b, c + 1)
                    s.activation(XDT[:, c * CH:(c + 1) * CH], PS[:, 6 + c, :], ACT.Copy)\
                        .then_inc(sems["xdT_done"], 1)
                for e in range(E):
                    need(act, "g_ps_done", b, e + 1)
                    if e >= 2:
                        need(act, "yD_ps_done", b, e - 1)
                    s.activation(GE[:, e % 2].rearrange("p a b -> p (a b)"), PS[:, e % 2, :],
                                 ACT.Gelu_apprx_tanh).then_inc(sems["gelu_done"], 1)
                for c in range(2):
                    need(act, "yD_ps_done", b, 4 * (c + 1))
                    s.activation(YD[:, 4 * c:4 * (c + 1), :].rearrange("p a b -> p (a b)"),
                                 PS[:, 4 + c, :], ACT.Copy).then_inc(sems["yD_done"], 1)
                s.preload_act_table_set(LOG_EXP)
                norm_stats(b, 5, eps_l[:, 0:1])
                assert count[0] == A_STEPS, count[0]

            row(0)
            with act.Fori(1, NB) as b:
                row(b)

        @block.vector
        def _(dve):
            v = nc.vector
            count = [0]
            now = [0]

            def step(ins):
                count[0] += 1
                ins.then_inc(sems["v_step"], 1)
                need(dve, "v_step", now[0], count[0])

            def norm_in(src, k):
                for t in range(NT):
                    ins = v.bn_stats(bst[:, t, :], src[:, t, :])
                step(ins)
                v.memset(held[:, :], 0.0)
                for t in range(NT):
                    ins = v.bn_aggr(mv[:, t, :], bst[:, t, :])
                ins.then_inc(sems["mv_done"], 1)

            def norm_out(dst, src, k, done):
                need(dve, "rstd_done", now[0], k)
                for t in range(NT):
                    ins = v.tensor_scalar(dst[:, t, :], src[:, t, :], mv[:, t, 0:1], rstd[:, t:t + 1],
                                          ALU.subtract, ALU.mult)
                ins.then_inc(sems[done], 1)

            def pick(mx, oh):
                step(v.tensor_reduce(mx[:, :], lg[:, :, :], AX, ALU.max))
                step(v.tensor_tensor(out=t8a[:, :, :], in0=lg[:, :, :], in1=per_tile(mx), op=ALU.is_equal))
                step(v.tensor_tensor(out=t8b[:, :, :], in0=t8a[:, :, :],
                                     in1=first[:, :].unsqueeze(1).to_broadcast([P, NT, E]), op=ALU.mult))
                step(v.tensor_reduce(ms[:, :], t8b[:, :, :], AX, ALU.max))
                step(v.tensor_tensor(out=oh[:, :, :], in0=t8b[:, :, :], in1=per_tile(ms), op=ALU.is_equal))

            def split3(dst, rest, src, last):
                step(v.tensor_copy(dst[0], src))
                step(v.tensor_tensor(out=rest, in0=src, in1=dst[0], op=ALU.subtract))
                step(v.tensor_copy(dst[1], rest))
                step(v.tensor_tensor(out=rest, in0=rest, in1=dst[1], op=ALU.subtract))
                return v.tensor_copy(dst[2], rest)

            v.memset(eps_a[:, :], 1e-12)
            v.memset(eps_l[:, :], 1e-5)
            v.memset(half[:, :], 0.5)
            v.memset(rnb[:, :], RN_BIAS).then_inc(setup_v, 1)
            dve.wait_ge(setup_a, 2)
            v.tensor_scalar(nega[:, :, :], nega[:, :, :], -1.0, None, ALU.mult)
            v.tensor_reduce(ms[:, 0:NI], SQ[:, 0:NI, :], AX, ALU.add).then_inc(setup_v, 1)
            dve.wait_ge(setup_v, 2)
            v.tensor_scalar(n2[:, 0:NI], ms[:, 0:NI], 1e-24, None, ALU.max).then_inc(setup_v, 1)
            dve.wait_ge(setup_a, 4)
            for i in range(NI):
                ins = v.tensor_scalar(kn[:, i, :], kn[:, i, :], rn[:, i:i + 1], None, ALU.mult)
            ins.then_inc(setup_v, 1)
            parts = [b2_p[:, i, :] for i in range(3)]
            ins = []
            v.tensor_copy(parts[0], b2_f[:, :]).then_inc(setup_v, 1)
            dve.wait_ge(setup_v, 5)
            v.tensor_tensor(out=b2_r[:, :], in0=b2_f[:, :], in1=parts[0], op=ALU.subtract).then_inc(setup_v, 1)
            dve.wait_ge(setup_v, 6)
            v.tensor_copy(parts[1], b2_r[:, :]).then_inc(setup_v, 1)
            dve.wait_ge(setup_v, 7)
            v.tensor_tensor(out=b2_r[:, :], in0=b2_r[:, :], in1=parts[1], op=ALU.subtract).then_inc(setup_v, 1)
            dve.wait_ge(setup_v, 8)
            v.tensor_copy(parts[2], b2_r[:, :]).then_inc(setup_v, 1)

            def row(b):
                count[0], now[0] = 0, b
                need(dve, "x_loaded", b, 16)
                norm_in(X, 1)
                norm_out(XL, X, 1, "xh_done")
                need(dve, "sqA_done", b, 1)
                step(v.tensor_reduce(ms[:, :], SQ[:, :, :], AX, ALU.add))
                v.tensor_scalar(n2[:, :], ms[:, :], 1e-24, None, ALU.max).then_inc(sems["n2_done"], 1)
                need(dve, "rn_done", b, 1)
                for t in range(NT):
                    ins = v.tensor_scalar(XL[:, t, :], XL[:, t, :], rn[:, t:t + 1], None, ALU.mult)
                ins.then_inc(sems["qn_done"], 1)
                for c in range(NC_):
                    need(dve, "s_ps_done", b, c + 1)
                    v.tensor_scalar(SC[:, c], PS[:, 0:NI, :], S_MAX, -S_MAX, ALU.min, ALU.max)\
                        .then_inc(sems["clip_done"], 1)
                for c in range(NC_):
                    need(dve, "logs_done", b, c + 1)
                    v.tensor_tensor(out=L1[:, c], in0=L1[:, c], in1=L2[:, c], op=ALU.subtract)\
                        .then_inc(sems["dlog_done"], 1)
                for c in range(NC_):
                    need(dve, "t4_done", b, c + 1)
                    v.tensor_scalar(SC[:, c], SC[:, c], 2.0 / math.pi, 0.5, ALU.mult, ALU.add)
                    step(v.tensor_tensor(out=L2[:, c], in0=L2[:, c], in1=L2[:, c], op=ALU.mult))
                    v.tensor_tensor(out=L1[:, c], in0=L2[:, c], in1=SC[:, c], op=ALU.mult)\
                        .then_inc(sems["bpow_done"], 1)
                for c in range(NC_):
                    need(dve, "sqX_done", b, c + 1)
                    ins = v.tensor_reduce(ms[:, TPC * c:TPC * (c + 1)], SQ[:, TPC * c:TPC * (c + 1), :], AX, ALU.add)
                step(ins)
                v.tensor_scalar(n2[:, :], ms[:, :], 1e-24, None, ALU.max).then_inc(sems["n2_done"], 1)
                need(dve, "rn_done", b, 2)
                need(dve, "p_step", b, 1)
                for t in range(NT):
                    c, r = t // TPC, t % TPC
                    ins = v.scalar_tensor_tensor(out=Y[:, t, :], in0=PS[:, 4 + c, r * P:(r + 1) * P],
                                                 scalar=rn[:, t:t + 1], in1=XB[:, t, :],
                                                 op0=ALU.mult, op1=ALU.add)
                step(ins)
                norm_in(Y, 2)
                need(dve, "out_stored", b, 0)
                norm_out(XN, Y, 2, "ln_done")
                need(dve, "lg_ps_done", b, 1)
                step(v.tensor_tensor(out=lg[:, :, :], in0=PS[:, 6, 0:NT * E].rearrange("p (t e) -> p t e", e=E),
                                     in1=br_bc[:, :].unsqueeze(1).to_broadcast([P, NT, E]), op=ALU.add))
                pick(m1, oh1)
                step(v.scalar_tensor_tensor(out=lg[:, :, :], in0=oh1[:, :, :], scalar=-3.0e38, in1=lg[:, :, :],
                                            op0=ALU.mult, op1=ALU.add))
                pick(m2, oh2)
                v.tensor_tensor(out=m2[:, :], in0=m2[:, :], in1=m1[:, :], op=ALU.subtract)\
                    .then_inc(sems["m_done"], 1)
                need(dve, "ex_done", b, 1)
                step(v.tensor_scalar(gw1[:, :], gw2[:, :], 1.0, None, ALU.add))
                step(v.reciprocal(gw1[:, :], gw1[:, :]))
                step(v.tensor_tensor(out=gw2[:, :], in0=gw2[:, :], in1=gw1[:, :], op=ALU.mult))
                v.tensor_tensor(out=t8a[:, :, :], in0=oh1[:, :, :], in1=per_tile(gw1), op=ALU.mult)
                step(v.tensor_tensor(out=t8b[:, :, :], in0=oh2[:, :, :], in1=per_tile(gw2), op=ALU.mult))
                step(v.tensor_tensor(out=t8a[:, :, :], in0=t8a[:, :, :], in1=t8b[:, :, :], op=ALU.add))
                split3([g3[:, :, i, :] for i in range(3)], t8b[:, :, :], t8a[:, :, :], None)\
                    .then_inc(sems["g3_done"], 1)
                j = 0
                for c in range(NC_):
                    for e in range(E):
                        need(dve, "gate_ps_done", b, E * c + e + 1)
                        for f in range(NFB):
                            need(dve, "relu_done", b, j + 1)
                            if j >= 2:
                                need(dve, "oB_acc_done", b, j - 1)
                            v.tensor_tensor(out=HG[:, j % 2, :], in0=HR[:, j % 2, :], in1=PS[:, 2 + e % 2, :],
                                            op=ALU.mult).then_inc(sems["hg_done"], 1)
                            j += 1
                for c in range(NC_):
                    need(dve, "oB_ps_done", b, c + 1)
                    ins = v.tensor_tensor(out=Y[:, TPC * c:TPC * (c + 1), :].rearrange("p a b -> p (a b)"),
                                          in0=PS[:, 6 + c, :],
                                          in1=XN[:, TPC * c:TPC * (c + 1), :].rearrange("p a b -> p (a b)"),
                                          op=ALU.add)
                ins.then_inc(sems["yB_done"], 1)
                need(dve, "yB_done", b, 1)
                norm_in(Y, 3)
                norm_out(XN, Y, 3, "ln_done")
                for d in range(ND):
                    need(dve, "xs_done", b, 2 * ND)
                    step(v.tensor_scalar(XC[:, d, :], XS[:, d, 0:T], cw_s[:, d, 0:1], cb_s[:, d:d + 1],
                                         ALU.mult, ALU.add))
                    for k in range(1, TAPS):
                        ins = v.scalar_tensor_tensor(out=XC[:, d, :], in0=XS[:, d, k:k + T],
                                                     scalar=cw_s[:, d, k:k + 1], in1=XC[:, d, :],
                                                     op0=ALU.mult, op1=ALU.add)
                        if k < TAPS - 1:
                            step(ins)
                        else:
                            ins.then_inc(sems["conv_done"], 1)
                k = 0
                for d in range(ND):
                    for c in range(NC_):
                        need(dve, "abs_done", b, k + 1)
                        v.tensor_scalar(DT[:, d, c * CH:(c + 1) * CH], PS[:, k % 4, :], bdt_s[:, d:d + 1], 0.0,
                                        ALU.add, ALU.max).then_inc(sems["vrel_done"], 1)
                        k += 1
                need(dve, "bs_ps_done", b, 1)
                step(v.tensor_copy(bsr[:, :, :], PS[:, 6, 0:NT * NS].rearrange("p (t n) -> p t n", n=NS)))
                split3([bs3[:, :, i, :] for i in range(3)], bsr[:, :, :], bsr[:, :, :], None)\
                    .then_inc(sems["bs3_done"], 1)
                k = 0
                for d in range(ND):
                    for n_ in range(NS):
                        need(dve, "dA_done", b, k + 1)
                        need(dve, "bc_ps_done", b, k + 1)
                        if k >= 2:
                            need(dve, "y_acc_done", b, k - 1)
                        bank = 2 * (k % 2)
                        v.tensor_tensor_scan(HS[:, k % 2, :], dA[:, k % 2, :],
                                             PS[:, bank:bank + 2, :].rearrange("p a b -> p (a b)"),
                                             0.0, ALU.mult, ALU.add).then_inc(sems["scan_done"], 1)
                        k += 1
                    need(dve, "y_acc_done", b, k)
                    v.scalar_tensor_tensor(out=XC[:, d, :], in0=XA[:, d, :], scalar=dsk[:, d:d + 1],
                                           in1=PS[:, 4:6, :].rearrange("p a b -> p (a b)"),
                                           op0=ALU.mult, op1=ALU.add).then_inc(sems["yx_done"], 1)
                for c in range(NC_):
                    need(dve, "oC_ps_done", b, c + 1)
                    ins = v.tensor_tensor(out=Y[:, TPC * c:TPC * (c + 1), :].rearrange("p a b -> p (a b)"),
                                          in0=PS[:, 6 + c, :],
                                          in1=XN[:, TPC * c:TPC * (c + 1), :].rearrange("p a b -> p (a b)"),
                                          op=ALU.add)
                ins.then_inc(sems["yC_done"], 1)
                need(dve, "yC_done", b, 1)
                norm_in(Y, 4)
                norm_out(XN, Y, 4, "ln_done")
                need(dve, "lg_ps_done", b, 2)
                step(v.tensor_copy(lg[:, :, :], PS[:, 6, 0:NT * E].rearrange("p (t e) -> p t e", e=E)))
                pick(m1, oh1)
                v.tensor_copy(maskb[:, :, :], oh1[:, :, :]).then_inc(sems["mask_done"], 1)
                v.tensor_tensor(out=lg[:, :, :], in0=lg[:, :, :], in1=per_tile(m1), op=ALU.subtract)\
                    .then_inc(sems["m_done"], 1)
                step(v.tensor_tensor(out=t8a[:, :, :], in0=oh1[:, :, :],
                                     in1=base128[:, :].unsqueeze(1).to_broadcast([P, NT, E]), op=ALU.mult))
                step(v.tensor_reduce(slot[:, :], t8a[:, :, :], AX, ALU.add))
                need(dve, "pos_ps_done", b, 1)
                step(v.tensor_tensor(out=t8b[:, :, :], in0=oh1[:, :, :],
                                     in1=PS[:, 7, 0:NT * E].rearrange("p (t e) -> p t e", e=E), op=ALU.mult))
                step(v.tensor_reduce(pos[:, :], t8b[:, :, :], AX, ALU.add))
                v.tensor_tensor(out=slot[:, :], in0=slot[:, :], in1=pos[:, :], op=ALU.add)
                step(v.tensor_scalar(over[:, :], pos[:, :], float(CAP), None, ALU.is_ge))
                step(v.scalar_tensor_tensor(out=ms[:, :], in0=over[:, :], scalar=float(SLOTS), in1=slot[:, :],
                                            op0=ALU.mult, op1=ALU.add))
                v.tensor_copy(put_i[:, :], ms[:, :]).then_inc(sems["put_done"], 1)
                step(v.tensor_scalar(m2[:, :], slot[:, :], float(SLOTS - 1), None, ALU.min))
                v.tensor_copy(get_i[:, :], m2[:, :]).then_inc(sems["get_done"], 1)
                need(dve, "ex_done", b, 2)
                step(v.tensor_reduce(gw1[:, :], ex[:, :, :], AX, ALU.add))
                step(v.reciprocal(gw1[:, :], gw1[:, :]))
                step(v.tensor_scalar(gw2[:, :], over[:, :], -1.0, 1.0, ALU.mult, ALU.add))
                step(v.tensor_tensor(out=gk[:, :], in0=gw1[:, :], in1=gw2[:, :], op=ALU.mult))
                need(dve, "gathered", b, 16 * NT)
                for t in range(NT):
                    ins = v.scalar_tensor_tensor(out=Y[:, t, :], in0=YG[:, t, :], scalar=gk[:, t:t + 1],
                                                 in1=XN[:, t, :], op0=ALU.mult, op1=ALU.add)
                ins.then_inc(sems["yF_done"], 1)
                need(dve, "yF_done", b, 1)
                norm_in(Y, 5)
                norm_out(XN, Y, 5, "ln_done")
                assert count[0] == V_STEPS, count[0]

            row(0)
            with dve.Fori(1, NB) as b:
                row(b)

        @block.tensor
        def _(pe):
            m = nc.tensor

            pe.wait_ge(consts_done, CONSTS)
            pe.wait_ge(setup_v, 9)
            pe.wait_ge(weights_in, W_ALL)
            for i in range(NI):
                ins = m.transpose(PS[:, 6, i * P:(i + 1) * P], kn[:, i, :], ident[:, :])
            ins.then_inc(setup_pe, 1)
            pe.wait_ge(setup_a, 5)

            def turn_x(b, src, done, wait_name, wait_k):
                need(pe, wait_name, b, wait_k)
                for t in range(NT):
                    c, r = t // TPC, t % TPC
                    ins = m.transpose(PS[:, 6 + c, r * P:(r + 1) * P], src[:, t, :], ident[:, :])
                    if r == TPC - 1:
                        ins.then_inc(sems[done], 1)

            def logits(b, w, k, xT_k):
                need(pe, "xT_done", b, xT_k)
                for t in range(NT):
                    ins = m.matmul(PS[:, 6, t * E:(t + 1) * E], XT[:, t * P:(t + 1) * P], w[:, :],
                                   start=True, stop=True)
                ins.then_inc(sems["lg_ps_done"], 1)

            def row(b):
                turn_x(b, XL, "qT_ps_done", "qn_done", 1)
                for c in range(NC_):
                    need(pe, "qT_done", b, c + 1)
                    if c:
                        need(pe, "clip_done", b, c)
                    for i in range(NI):
                        ins = m.matmul(PS[:, i, :], knT[:, i * P:(i + 1) * P], XT[:, c * CH:(c + 1) * CH],
                                       start=True, stop=True)
                    ins.then_inc(sems["s_ps_done"], 1)
                for c in range(NC_):
                    need(pe, "bpow_done", b, c + 1)
                    for r in range(TPC):
                        for i in range(NI):
                            ins = m.matmul(PS[:, 4 + c, r * P:(r + 1) * P], L1[:, c, i, r * P:(r + 1) * P],
                                           qw[:, i, :], start=(i == 0), stop=(i == NI - 1))
                    ins.then_inc(sems["xo_ps_done"], 1)
                turn_x(b, XN, "xT_ps_done", "ln_done", 1)
                logits(b, wr_s, 1, 2)
                need(pe, "g3_done", b, 1)
                for t in range(NT):
                    ins = m.transpose(g3T_ps[0:3 * E, t * P:(t + 1) * P],
                                      g3[:, t].rearrange("p a e -> p (a e)"), identb[:, :])
                ins.then_inc(sems["g3T_ps_done"], 1)
                need(pe, "g3T_done", b, 1)

                def up(j):
                    c, e, f = j // (E * NFB), j // NFB % E, j % NFB
                    if j >= 2:
                        need(pe, "relu_done", b, j - 1)
                    m.matmul(PS[:, j % 2, :], w1b_s[:, e, f * P:(f + 1) * P], XT[:, c * CH:(c + 1) * CH],
                             start=True, stop=True).then_inc(sems["z_ps_done"], 1)
                    if f == 0:
                        ge = E * c + e
                        if ge >= 2:
                            need(pe, "hg_done", b, NFB * (ge - 1))
                        m.matmul(PS[:, 2 + e % 2, :], sel_gate[:, e, :], g3T[:, c * CH:(c + 1) * CH],
                                 start=True, stop=True).then_inc(sems["gate_ps_done"], 1)

                def down(j):
                    c, e, f = j // (E * NFB), j // NFB % E, j % NFB
                    if j % (E * NFB) == 0:
                        for i in range(3):
                            m.matmul(PS[:, 4 + c, :], b2_p[:, i, :], g3T[:, c * CH:(c + 1) * CH],
                                     start=(i == 0), stop=False)
                    need(pe, "hg_done", b, j + 1)
                    m.matmul(PS[:, 4 + c, :], w2b_s[:, e, f, :], HG[:, j % 2, :],
                             start=False, stop=(j % (E * NFB) == E * NFB - 1)).then_inc(sems["oB_acc_done"], 1)

                n_j = NC_ * E * NFB
                up(0)
                up(1)
                for j in range(n_j):
                    down(j)
                    if j + 2 < n_j:
                        up(j + 2)
                    if (j + 1) % (E * NFB) == 0:
                        c = j // (E * NFB)
                        need(pe, "oT_done", b, c + 1)
                        for r in range(TPC):
                            ins = m.transpose(PS[:, 6 + c, r * P:(r + 1) * P], OT[:, c, r * P:(r + 1) * P],
                                              ident[:, :])
                        ins.then_inc(sems["oB_ps_done"], 1)
                turn_x(b, XN, "xT_ps_done", "ln_done", 2)
                k = 0
                for c in range(NC_):
                    need(pe, "xT_done", b, 4)
                    for d in range(2 * ND):
                        if k >= 4:
                            need(pe, "xs_done", b, 2)
                            need(pe, "silz_done", b, max(k - 5, 0) if k >= 6 else 0)
                        m.matmul(PS[:, k % 4, :], win_s[:, d * P:(d + 1) * P], XT[:, c * CH:(c + 1) * CH],
                                 start=True, stop=True).then_inc(sems["xz_ps_done"], 1)
                        k += 1
                need(pe, "xa_done", b, ND)
                need(pe, "silz_done", b, 4)
                k = 0
                for d in range(ND):
                    for c in range(NC_):
                        for i in range(ND):
                            ins = m.matmul(PS[:, k % 4, :], wdt_s[:, i, d * P:(d + 1) * P],
                                           XA[:, i, c * CH:(c + 1) * CH], start=(i == 0), stop=(i == ND - 1))
                        ins.then_inc(sems["dt_ps_done"], 1)
                        k += 1
                for t in range(NT):
                    for i in range(ND):
                        ins = m.matmul(PS[:, 6, t * NS:(t + 1) * NS], XA[:, i, t * P:(t + 1) * P], wx_s[:, i, :],
                                       start=(i == 0), stop=(i == ND - 1))
                ins.then_inc(sems["bs_ps_done"], 1)
                need_apart(pe, "bs3_done", b, 1)
                for t in range(NT):
                    ins = m.transpose(bs3T_ps[0:3 * NS, t * P:(t + 1) * P],
                                      bs3[:, t].rearrange("p a n -> p (a n)"), identb[:, :])
                ins.then_inc(sems["bs3T_ps_done"], 1)
                need(pe, "bs3T_done", b, 1)
                need(pe, "vrel_done", b, 4)

                def spread(k):
                    if k >= 2:
                        need(pe, "scan_done", b, k - 1)
                    for c in range(NC_):
                        ins = m.matmul(PS[:, 2 * (k % 2) + c, :], sel_bs[:, k % NS, :],
                                       bs3T[:, c * CH:(c + 1) * CH], start=True, stop=True)
                    ins.then_inc(sems["bc_ps_done"], 1)

                spread(0)
                for k in range(ND * NS):
                    if k + 1 < ND * NS:
                        spread(k + 1)
                    if k == NS:
                        need(pe, "yx_done", b, 1)
                    need(pe, "scan_done", b, k + 1)
                    for c in range(NC_):
                        ins = m.matmul(PS[:, 4 + c, :], ident[:, :], HS[:, k % 2, c * CH:(c + 1) * CH],
                                       start=(k % NS == 0), stop=(k % NS == NS - 1))
                    ins.then_inc(sems["y_acc_done"], 1)
                need(pe, "yz_done", b, ND)
                for t in range(NT):
                    c, r = t // TPC, t % TPC
                    for i in range(ND):
                        ins = m.matmul(PS[:, 6 + c, r * P:(r + 1) * P], XC[:, i, t * P:(t + 1) * P],
                                       wout_s[:, i, :], start=(i == 0), stop=(i == ND - 1))
                    if r == TPC - 1:
                        ins.then_inc(sems["oC_ps_done"], 1)
                turn_x(b, XN, "xT_ps_done", "ln_done", 3)
                logits(b, wg_s, 2, 6)
                need(pe, "mask_done", b, 1)
                pos_ps = PS[:, 7, 0:NT * E].rearrange("p (t e) -> p t e", e=E)
                m.matmul(pos_ps, before[:, :], maskb[:, :, :], start=True, stop=False, skip_group_check=True)
                for t in range(NT - 1):
                    ins = m.matmul(pos_ps[:, t + 1:NT, :], onesb[:, :],
                                   maskb[:, t:t + 1, :].to_broadcast([P, NT - 1 - t, E]),
                                   start=False, stop=(t == NT - 2), skip_group_check=True)
                ins.then_inc(sems["pos_ps_done"], 1)
                need(pe, "put_done", b, 1)
                turn_xd = XD
                need(pe, "slots_loaded", b, 16)
                for t in range(E):
                    c, r = t // TPC, t % TPC
                    ins = m.transpose(PS[:, 6 + c, r * P:(r + 1) * P], turn_xd[:, t, :], ident[:, :])
                    if r == TPC - 1:
                        ins.then_inc(sems["xdT_ps_done"], 1)

                def expert_up(e):
                    need(pe, "xdT_done", b, e // TPC + 1)
                    if e >= 2:
                        need(pe, "gelu_done", b, e - 1)
                    for f in range(NFD):
                        ins = m.matmul(PS[:, e % 2, f * P:(f + 1) * P], w1d_s[:, e, f * P:(f + 1) * P],
                                       XDT[:, e * P:(e + 1) * P], start=True, stop=True)
                    ins.then_inc(sems["g_ps_done"], 1)

                expert_up(0)
                for e in range(E):
                    if e + 1 < E:
                        expert_up(e + 1)
                    need(pe, "gelu_done", b, e + 1)
                    c, r = e // TPC, e % TPC
                    for f in range(NFD):
                        ins = m.matmul(PS[:, 4 + c, r * P:(r + 1) * P], GE[:, e % 2, f, :], w2d_s[:, e, f, :],
                                       start=(f == 0), stop=(f == NFD - 1))
                    ins.then_inc(sems["yD_ps_done"], 1)

            row(0)
            with pe.Fori(1, NB) as b:
                row(b)


_INS = [
    "L0_attn_hidden_states", "L0_attn_ln_weight", "L0_attn_ln_bias", "L0_attn_k_weight", "L0_attn_q_weight",
    "L0_attn_bias", "L0_ffn_Wr", "L0_ffn_br", "L0_ffn_W1", "L0_ffn_b1", "L0_ffn_W2", "L0_ffn_b2",
    "L1_attn_W_in", "L1_attn_conv_w", "L1_attn_conv_b", "L1_attn_A_log", "L1_attn_D", "L1_attn_W_x",
    "L1_attn_W_dt", "L1_attn_b_dt", "L1_attn_W_out", "L1_ffn_Wg", "L1_ffn_W1", "L1_ffn_W2",
]
_OUTS = [((8, 1024, 128), "float32")]


def kernel(**inputs):
    import numpy as _np
    import concourse.bacc as _bacc
    from concourse import mybir as _mybir
    from concourse.bass_utils import run_bass_kernel_spmd as _run

    nc = _bacc.Bacc("TRN2", target_bir_lowering=False, num_devices=1)
    arrays, args = {}, []
    for name in _INS:
        a = _np.ascontiguousarray(inputs[name])
        arrays[f"in_{name}_dram"] = a
        args.append(nc.dram_tensor(f"in_{name}_dram", a.shape, _mybir.dt.from_np(a.dtype), kind="ExternalInput").ap())
    for i, (shape, dtype) in enumerate(_OUTS):
        dt = _mybir.dt.from_np(_np.dtype(dtype))
        args.append(nc.dram_tensor(f"out_{i}_dram", shape, dt, kind="ExternalOutput").ap())
    build_layer_stack(nc, *args)
    r = _run(nc, [arrays], core_ids=[0])
    got = tuple(r.results[0][f"out_{i}_dram"] for i in range(len(_OUTS)))
    return got[0]
```

```python
import math
from contextlib import ExitStack

import concourse.bass as bass
from concourse import mybir


CONSTS = 17


def build_layer_stack(
    nc: bass.Bass,
    x_in, ln_w, ln_b, k_w, q_w, l0_bias,
    wr, br, w1b, b1b, w2b, b2b,
    w_in, conv_w, conv_b, a_log, d_skip, w_x, w_dt, b_dt, w_out,
    wg, w1d, w2d,
    out,
):
    fp32, bf16, u32 = mybir.dt.float32, mybir.dt.bfloat16, mybir.dt.uint32
    ACT = mybir.ActivationFunctionType
    ALU = mybir.AluOpType
    AX = mybir.AxisListType.X

    P = 128
    NB, T, H = x_in.shape
    NT = T // P
    CH = 512
    NC_ = T // CH
    TPC = CH // P
    I = k_w.shape[0]
    NI = I // P
    E = wr.shape[1]
    FB = w1b.shape[2]
    NFB = FB // P
    DI = w_in.shape[1] // 2
    ND = DI // P
    NS = a_log.shape[1]
    TAPS = conv_w.shape[2]
    FD = w1d.shape[2]
    NFD = FD // P
    CAP = T // E
    SLOTS = E * CAP
    assert CAP == P and H == P and NC_ == 2

    S_MAX = 1.0 - 1e-6
    N2_SCALE = 2.0 ** 16
    RN_BIAS = 0.5 * math.log(N2_SCALE)

    slot_x = nc.dram_tensor("slot_x", (SLOTS, H), fp32, kind="Internal").ap()
    slot_y = nc.dram_tensor("slot_y", (SLOTS, H), fp32, kind="Internal").ap()

    ctx = ExitStack()
    with ctx:
        def sb(name, shape, dt=fp32):
            return ctx.enter_context(nc.sbuf_tensor(name, shape, dt))

        per, sems = {}, {}

        def sem(name, per_row=0):
            sems[name] = ctx.enter_context(nc.semaphore(name))
            per[name] = per_row
            return sems[name]

        def need(eng, name, b, k):
            if k or not isinstance(b, int) or b:
                eng.wait_ge(sems[name], b * per[name] + k)

        ident = sb("ident", [P, P])
        identb = sb("identb", [P, P], bf16)
        onesb = sb("onesb", [P, P], bf16)
        before = sb("before", [P, P], bf16)
        sel_gate = sb("sel_gate", [3 * E, E, P], bf16)
        sel_bs = sb("sel_bs", [3 * NS, NS, P], bf16)
        first = sb("first", [P, E])
        base128 = sb("base128", [P, E])
        lnw_bc = sb("lnw_bc", [P, H])
        lnb_bc = sb("lnb_bc", [P, H])
        bias_bc = sb("bias_bc", [P, H])
        br_bc = sb("br_bc", [P, E])
        knT = sb("knT", [P, I])
        qw = sb("qw", [P, NI, H])
        wr_s = sb("wr_s", [P, E])
        w1b_s = sb("w1b_s", [P, E, FB])
        b1_s = sb("b1_s", [P, E, NFB])
        w2b_s = sb("w2b_s", [P, E, NFB, H])
        b2_p = sb("b2_p", [3 * E, 3, H], bf16)
        win_s = sb("win_s", [P, 2 * DI])
        cw_s = sb("cw_s", [P, ND, TAPS])
        cb_s = sb("cb_s", [P, ND])
        nega = sb("nega", [P, ND, NS])
        dsk = sb("dsk", [P, ND])
        wx_s = sb("wx_s", [P, ND, NS])
        wdt_s = sb("wdt_s", [P, ND, DI])
        bdt_s = sb("bdt_s", [P, ND])
        wout_s = sb("wout_s", [P, ND, H])
        wg_s = sb("wg_s", [P, E])
        w1d_s = sb("w1d_s", [P, E, FD])
        w2d_s = sb("w2d_s", [P, E, NFD, H])
        X = sb("X", [P, NT, H])
        XL = sb("XL", [P, NT, H])
        SQ = sb("SQ", [P, NT, H])
        X1 = sb("X1", [P, NT, H])
        X2 = sb("X2", [P, NT, H])
        X3 = sb("X3", [P, NT, H])
        Y2 = sb("Y2", [P, NT, H])
        XD = sb("XD", [P, NT, H])
        YD = Y2
        XT1 = sb("XT1", [P, T])
        XT2 = sb("XT2", [P, T])
        XDT = XT1[:, 0:SLOTS]
        OT = SQ[:, :, :].rearrange("p (c r) h -> p c (r h)", c=NC_)
        WIDE = NC_ * NI * CH
        wide = sb("wide", [P, 3 * WIDE])

        def of_a(n):
            return wide[:, n * WIDE:(n + 1) * WIDE].rearrange("p (c i t) -> p c i t", c=NC_, i=NI)

        SC, L1, L2 = of_a(0), of_a(1), of_a(2)
        b2_f, b2_r = wide[0:3 * E, 0:H], wide[0:3 * E, H:2 * H]
        kn = wide[:, 2 * H:(2 + NI) * H].rearrange("p (n h) -> p n h", n=NI)
        N_H, N_A = 8, 3
        HS = wide[:, 0:N_H * T].rearrange("p (n t) -> p n t", n=N_H)
        dA = wide[:, N_H * T:(N_H + N_A) * T].rearrange("p (n t) -> p n t", n=N_A)
        hidden = sb("hidden", [P, 4, CH])
        HR, HG = hidden[:, 0:2, :], hidden[:, 2:4, :]
        g3 = sb("g3", [P, NT, 3, E], bf16)
        g3T = sb("g3T", [3 * E, T], bf16)
        XS = sb("XS", [P, ND, TAPS - 1 + T])
        YX = XS[:, :, TAPS - 1:]
        ZS = sb("ZS", [P, ND, T])
        XA = sb("XA", [P, ND, T])
        DT = sb("DT", [P, ND, T])
        SP_ = hidden[:, :, :].rearrange("p a t -> p (a t)").rearrange("p (d t) -> p d t", d=ND)
        bsr = sb("bsr", [P, NT, NS])
        bs3 = sb("bs3", [P, NT, 3, NS], bf16)
        bs3T = sb("bs3T", [3 * NS, T], bf16)
        GE = SP_[:, 0, :].rearrange("p (k f s) -> p k f s", k=2, f=NFD)
        maskb = sb("maskb", [P, NT, E], bf16)
        put_i = sb("put_i", [P, NT], u32)
        get_i = sb("get_i", [P, NT], u32)
        eps_a = sb("eps_a", [P, 1])
        eps_l = sb("eps_l", [P, 1])
        half = sb("half", [P, 1])
        rnb = sb("rnb", [P, 1])
        held = sb("held", [P, 1])
        held_p = sb("held_p", [P, 1])

        def small(tag):
            shapes = {"bst": [P, NT, 6], "mv": [P, NT, 2]}
            shapes.update({n_: [P, NT] for n_ in ("lnv", "rstd", "n2", "ln2", "rn", "m1", "m2", "ms", "w1", "w2",
                                                  "pos", "slot", "over", "gk")})
            shapes.update({n_: [P, NT, E] for n_ in ("lg", "t8a", "t8b", "oh1", "oh2", "ex")})
            return {n_: sb(n_ + tag, shape) for n_, shape in shapes.items()}

        S1, S2 = small("1"), small("2")
        n2, ln2, rn, ms = S1["n2"], S1["ln2"], S1["rn"], S1["ms"]

        PS = ctx.enter_context(nc.psum_tensor("PS", [P, 8, CH], fp32))
        Z0, GATE, ACC = 0, 2, 3
        YB, SPR = 4, 6
        g3T_ps = PS[:, 3, :].bitcast(bf16)
        bs3T_ps = PS[:, 5, :].bitcast(bf16)

        NJ = NC_ * E * NFB
        NK = ND * NS
        QUAD = 4
        NQ = NK // QUAD

        for name, n in (
            ("x_loaded", 16), ("out_stored", 16),
            ("vA", 6), ("vB", 22), ("vC", 12), ("vD", 18),
            ("aA", 8), ("aB", 1), ("aC", 3), ("aD", 1), ("pA", 2), ("pC", NQ * (QUAD - 2)),
            ("mvA_done", 2), ("mvB_done", 1), ("mvC_done", 1), ("mvD_done", 1),
            ("rstdA_done", 2), ("rstdB_done", 1), ("rstdC_done", 1), ("rstdD_done", 1),
            ("x1_done", 1), ("x2_done", 1), ("x3_done", 1), ("x4_done", 1),
            ("xh_done", 1), ("xln_done", 1), ("sqA_done", 1),
            ("n2_done", 2), ("rn_done", 2), ("qn_done", 1), ("qT_ps_done", 2), ("qT_done", 2),
            ("s_ps_done", 4), ("clip_done", 4), ("logs_done", 2), ("dlog_done", 2), ("atan_done", 2),
            ("t4_done", 2), ("bpow_done", 2), ("xo_ps_done", 2), ("sqX_done", 2), ("yA_done", 1),
            ("x1T_ps_done", 2), ("x1T_done", 2), ("lgB_ps_done", 1), ("mB_done", 1), ("exB_done", 1),
            ("g3_done", 1), ("g3T_ps_done", 1), ("g3T_done", 1),
            ("z_ps_done", NJ), ("relu_done", NJ), ("gate_ps_done", 2 * E),
            ("hg_done", NJ), ("oB_acc_done", NJ), ("oT_done", 2), ("oB_ps_done", 2), ("yB_done", 1),
            ("x2T_ps_done", 2), ("x2T_done", 2), ("xz_ps_done", 8), ("xs_done", 4), ("zs_done", 4),
            ("silz_done", 1), ("conv_done", ND), ("xa_done", ND),
            ("dt_ps_done", 4), ("abs_done", 4), ("vrel_done", 4), ("sp_done", ND), ("dt_done", ND),
            ("bs_ps_done", 1), ("bs3_done", 1), ("bs3T_ps_done", 1), ("bs3T_done", 1),
            ("spread_done", NK), ("dA_done", NK), ("scan_done", NK), ("quad_done", NQ), ("y_acc_done", NQ),
            ("yx_done", ND), ("yz_done", ND), ("oC_ps_done", 2), ("yC_done", 1),
            ("x3T_ps_done", 2), ("x3T_done", 2), ("lgD_ps_done", 1), ("mD_done", 1), ("exD_done", 1),
            ("mask_done", 1), ("pos_ps_done", 1), ("put_done", 1), ("get_done", 1),
            ("scattered", 16 * NT), ("slots_loaded", 16), ("xdT_ps_done", 2), ("xdT_done", 2),
            ("g_ps_done", E), ("gelu_done", E), ("yD_ps_done", E), ("yD_done", 2), ("slots_stored", 16),
            ("gathered", 16 * NT), ("yF_done", 1),
        ):
            sem(name, n)
        consts_done = sem("consts_done")
        weights_in = sem("weights_in")
        setup_v = sem("setup_v")
        setup_a = sem("setup_a")
        setup_pe = sem("setup_pe")
        N_WEIGHTS = 23 + 2 * E
        W_ALL = 16 * N_WEIGHTS

        block = ctx.enter_context(nc.Block())

        def need_apart(eng, name, b, k):
            eng.wait_ge(consts_done, CONSTS)
            need(eng, name, b, k)

        def per_tile(ap):
            return ap[:, :].unsqueeze(2).to_broadcast([P, NT, E])

        def per_token(ap, n):
            return ap[:, :].unsqueeze(1).to_broadcast([P, NT, n])

        def flat(ap):
            return ap.rearrange("p a b -> p (a b)")

        def schedule(eng, part):
            def turn(i, has_a, has_b, has_c, has_c1, has_d):
                a, b, c1 = i + 2, i + 1, i + 1
                if has_a:
                    part("load_x", a)
                if has_b or has_c:
                    part("mix_and_scan", b if has_b else None, i if has_c else None)
                if has_c:
                    part("c_out", i)
                if has_b:
                    part("b_out", b)
                if has_a:
                    part("a_norm", a)
                if has_d:
                    part("d_route", i)
                if has_a:
                    part("a_turn", a)
                if has_d:
                    part("d_slots", i)
                if has_a:
                    part("a_scores", a)
                if has_c1:
                    part("c_in", c1)
                if has_a:
                    part("a_angle", a)
                if has_c1:
                    part("c_silu", c1)
                if has_d:
                    part("d_ffn", i)
                if has_a:
                    part("a_mix", a)
                part("log_exp_table", None)
                if has_c1:
                    part("c_delta", c1)
                if has_a:
                    part("a_out", a)
                if has_d:
                    part("d_out", i)
                if has_a:
                    part("b_route", a)

            turn(-2, True, False, False, False, False)
            turn(-1, True, True, False, True, False)
            with eng.Fori(0, NB - 2) as i:
                turn(i, True, True, True, True, True)
            turn(NB - 2, False, True, True, True, True)
            turn(NB - 1, False, False, True, False, True)

        @block.sync
        def _(sp):
            loads = [
                (lnw_bc[:, :], ln_w.partition_broadcast(P)), (lnb_bc[:, :], ln_b.partition_broadcast(P)),
                (bias_bc[:, :], l0_bias.partition_broadcast(P)), (br_bc[:, :], br.partition_broadcast(P)),
                (kn[:, :, :], k_w.rearrange("(n p) h -> p n h", p=P)),
                (qw[:, :, :], q_w.rearrange("(n p) h -> p n h", p=P)),
                (wr_s[:, :], wr), (w1b_s[:, :, :], w1b.rearrange("e d f -> d e f")),
                (b1_s[:, :, :], b1b.rearrange("e (n p) -> p e n", p=P)),
                (b2_f[0:E, :], b2b), (b2_f[E:2 * E, :], b2b), (b2_f[2 * E:3 * E, :], b2b),
                (win_s[:, :], w_in), (cw_s[:, :, :], conv_w.rearrange("(n p) o k -> p n (o k)", p=P)),
                (cb_s[:, :], conv_b.rearrange("(n p) -> p n", p=P)),
                (nega[:, :, :], a_log.rearrange("(n p) s -> p n s", p=P)),
                (dsk[:, :], d_skip.rearrange("(n p) -> p n", p=P)),
                (wx_s[:, :, :], w_x.rearrange("(n p) s -> p n s", p=P)),
                (wdt_s[:, :, :], w_dt.rearrange("(n p) s -> p n s", p=P)),
                (bdt_s[:, :], b_dt.rearrange("(n p) -> p n", p=P)),
                (wout_s[:, :, :], w_out.rearrange("(n p) h -> p n h", p=P)),
                (wg_s[:, :], wg), (w1d_s[:, :, :], w1d.rearrange("e d f -> d e f")),
            ]
            for dst, src in ((w2b_s, w2b), (w2d_s, w2d)):
                loads += [(dst[:, e], src[e].rearrange("(n p) h -> p n h", p=P)) for e in range(E)]
            assert len(loads) == N_WEIGHTS
            for dst, src in loads:
                sp.dma_start(dst, src, allow_slow_non_contiguous=True).then_inc(weights_in, 16)
            sp.wait_ge(consts_done, 1)
            sp.dma_start(slot_x.rearrange("(e p) d -> p e d", p=P), XD[:, :, :])\
                .then_inc(sems["out_stored"], 16)
            sp.wait_ge(sems["out_stored"], 16)

            def part(what, b, *_):
                if what == "load_x":
                    need(sp, "yA_done", b, 0)
                    sp.dma_start(X[:, :, :],
                                 x_in[bass.ds(b, 1), :, :].rearrange("o (k p) d -> p (o k) d", p=P))\
                        .then_inc(sems["x_loaded"], 16)
                elif what == "d_slots":
                    need(sp, "scattered", b, 16 * NT)
                    sp.dma_start(XD[:, :, :], slot_x.rearrange("(e p) d -> p e d", p=P))\
                        .then_inc(sems["slots_loaded"], 16)
                elif what == "d_ffn":
                    need(sp, "yD_done", b, 2)
                    sp.dma_start(slot_y.rearrange("(e p) d -> p e d", p=P), YD[:, :, :])\
                        .then_inc(sems["slots_stored"], 16)
                elif what == "d_out":
                    need(sp, "x4_done", b, 1)
                    sp.dma_start(out[bass.ds(b, 1), :, :].rearrange("o (k p) d -> p (o k) d", p=P),
                                 YD[:, :, :]).then_inc(sems["out_stored"], 16)

            schedule(sp, part)
            sp.wait_ge(sems["out_stored"], 16 * (NB + 1))

        @block.gpsimd
        def _(pool):
            g = nc.gpsimd
            n = 0

            def const(ins):
                nonlocal n
                n += 1
                ins.then_inc(consts_done, 1)
                pool.wait_ge(consts_done, n)

            const(g.memset(XD[:, :, :], 0.0))
            const(g.memset(ident[:, :], 0.0))
            const(g.affine_select(out=ident[:, :], in_=ident[:, :], compare_op=ALU.not_equal, fill=1.0,
                                  base=0, pattern=[[-1, P]], channel_multiplier=1))
            const(g.tensor_copy(identb[:, :], ident[:, :]))
            const(g.memset(onesb[:, :], 1.0))
            const(g.affine_select(out=before[:, :], in_=onesb[:, :], compare_op=ALU.is_gt, fill=0.0,
                                  base=0, pattern=[[1, P]], channel_multiplier=-1))
            for tile, count in ((sel_gate, E), (sel_bs, NS)):
                const(g.memset(tile[:, :, :], 0.0))
                for p3 in range(3):
                    const(g.affine_select(out=tile[:, :, :], in_=tile[:, :, :], compare_op=ALU.not_equal,
                                          fill=1.0, base=-p3 * count, pattern=[[-1, count], [0, P]],
                                          channel_multiplier=1))
            const(g.iota(first[:, :], pattern=[[-1, E]], base=E, channel_multiplier=0,
                         allow_small_or_imprecise_dtypes=True))
            const(g.iota(base128[:, :], pattern=[[CAP, E]], base=0, channel_multiplier=0,
                         allow_small_or_imprecise_dtypes=True))
            const(g.memset(XS[:, :, 0:TAPS - 1], 0.0))
            assert n == CONSTS
            pool.wait_ge(weights_in, W_ALL)

            def part(what, b, c=None):
                if what == "a_norm":
                    need(pool, "xh_done", b, 1)
                    g.tensor_tensor(out=XL[:, :, :], in0=XL[:, :, :], in1=per_token(lnw_bc, H), op=ALU.mult)\
                        .then_inc(sems["pA"], 1)
                    need(pool, "pA", b, 1)
                    g.tensor_tensor(out=XL[:, :, :], in0=XL[:, :, :], in1=per_token(lnb_bc, H), op=ALU.add)\
                        .then_inc(sems["xln_done"], 1)
                    g.tensor_tensor(out=X[:, :, :], in0=X[:, :, :], in1=per_token(bias_bc, H), op=ALU.add)\
                        .then_inc(sems["pA"], 1)
                elif what == "mix_and_scan" and c is not None:
                    steps = 0
                    for q in range(NQ):
                        h0 = QUAD * q % N_H
                        for r in range(1, QUAD):
                            need(pool, "scan_done", c, QUAD * q + r + 1)
                            if r > 1:
                                need(pool, "pC", c, steps)
                            ins = g.tensor_tensor(out=HS[:, h0, :], in0=HS[:, h0, :], in1=HS[:, h0 + r, :],
                                                  op=ALU.add)
                            if r < QUAD - 1:
                                steps += 1
                                ins.then_inc(sems["pC"], 1)
                        ins.then_inc(sems["quad_done"], 1)
                        if q == NQ // ND + 1:
                            gate_z(c, 0)
                elif what == "c_out":
                    gate_z(b, ND - 1)
                elif what == "c_delta":
                    for d in range(ND):
                        need(pool, "sp_done", b, d + 1)
                        need(pool, "vrel_done", b, NC_ * (d + 1))
                        g.tensor_tensor(out=DT[:, d, :], in0=DT[:, d, :], in1=SP_[:, d, :], op=ALU.add)\
                            .then_inc(sems["dt_done"], 1)
                elif what == "d_slots":
                    need(pool, "put_done", b, 1)
                    g.tensor_tensor(out=held_p[:, :], in0=bias_bc[:, 0:1], in1=bias_bc[:, 0:1], op=ALU.add)
                    for t in range(NT):
                        g.indirect_dma_start(
                            out=slot_x, out_offset=bass.IndirectOffsetOnAxis(ap=put_i[:, t:t + 1], axis=0),
                            in_=X3[:, t, :], in_offset=None, bounds_check=SLOTS - 1, oob_is_err=False)\
                            .then_inc(sems["scattered"], 16)
                elif what == "d_ffn":
                    need_apart(pool, "slots_stored", b, 16)
                    need(pool, "get_done", b, 1)
                    for t in range(NT):
                        g.indirect_dma_start(
                            out=XD[:, t, :], out_offset=None, in_=slot_y,
                            in_offset=bass.IndirectOffsetOnAxis(ap=get_i[:, t:t + 1], axis=0))\
                            .then_inc(sems["gathered"], 16)

            def gate_z(b, d):
                need(pool, "yx_done", b, d + 1)
                g.tensor_tensor(out=YX[:, d, :], in0=YX[:, d, :], in1=ZS[:, d, :], op=ALU.mult)\
                    .then_inc(sems["yz_done"], 1)

            schedule(pool, part)

        @block.scalar
        def _(act):
            s = nc.scalar
            LOG_EXP = "natural_log_exp_and_others"

            def inv_root(dst, tmp, src, scale, bias, out_bias, step, b, k):
                s.activation(tmp, src, ACT.Ln, bias=bias, scale=scale).then_inc(sems[step], 1)
                need(act, step, b, k)
                return s.activation(dst, tmp, ACT.Exp, bias=out_bias, scale=-0.5)

            act.wait_ge(weights_in, W_ALL)
            act.wait_ge(consts_done, CONSTS)
            s.preload_act_table_set(LOG_EXP)
            s.activation(nega[:, :, :], nega[:, :, :], ACT.Exp).then_inc(setup_a, 1)
            s.activation(SQ[:, 0:NI, :], kn[:, :, :], ACT.Square).then_inc(setup_a, 1)
            act.wait_ge(setup_v, 3)
            s.activation(ln2[:, 0:NI], n2[:, 0:NI], ACT.Ln, scale=N2_SCALE).then_inc(setup_a, 1)
            act.wait_ge(setup_a, 3)
            s.activation(rn[:, 0:NI], ln2[:, 0:NI], ACT.Exp, bias=rnb[:, 0:1], scale=-0.5).then_inc(setup_a, 1)
            act.wait_ge(setup_pe, 1)
            s.activation(knT[:, :], PS[:, 6, :], ACT.Copy).then_inc(setup_a, 1)

            def rstd(small, block_name, b, k, eps, step_k):
                need(act, f"mv{block_name}_done", b, k)
                inv_root(small["rstd"][:, :], small["lnv"][:, :], small["mv"][:, :, 1], 1.0, eps[:, 0:1], 0.0,
                         f"a{block_name}", b, step_k).then_inc(sems[f"rstd{block_name}_done"], 1)

            def copy_turned(dst, bank, b, ps_name, done):
                for c in range(NC_):
                    need(act, ps_name, b, c + 1)
                    s.activation(dst[:, c * CH:(c + 1) * CH], PS[:, bank + c, :], ACT.Copy)\
                        .then_inc(sems[done], 1)

            def decay(c, k):
                d, n_ = k // NS, k % NS
                if n_ == 0:
                    need(act, "dt_done", c, d + 1)
                if k >= N_A:
                    need(act, "scan_done", c, k - N_A + 1)
                s.activation(dA[:, k % N_A, :], DT[:, d, :], ACT.Exp, scale=nega[:, d, n_:n_ + 1])\
                    .then_inc(sems["dA_done"], 1)

            def part(what, b, c=None):
                if what == "mix_and_scan":
                    if c is not None:
                        need(act, "dt_done", c, ND)
                        decay(c, 0)
                        decay(c, 1)
                    for j in range(NJ):
                        if b is not None:
                            e, f = j // NFB % E, j % NFB
                            need(act, "z_ps_done", b, j + 1)
                            if j >= 2:
                                need(act, "hg_done", b, j - 1)
                            s.activation(HR[:, j % 2, :], PS[:, Z0 + j % 2, :], ACT.Relu,
                                         bias=b1_s[:, e, f:f + 1]).then_inc(sems["relu_done"], 1)
                        if c is not None and j + 2 < NK:
                            decay(c, j + 2)
                        if b is not None and j == E * NFB + 2:
                            copy_acc(b, 0)
                    if b is not None:
                        copy_acc(b, 1)
                elif what == "log_exp_table":
                    s.preload_act_table_set(LOG_EXP)
                elif what == "c_out":
                    rstd(S2, "C", b, 1, eps_l, 3)
                elif what == "b_out":
                    rstd(S1, "B", b, 1, eps_l, 1)
                elif what == "a_norm":
                    rstd(S1, "A", b, 1, eps_a, 1)
                    need(act, "xln_done", b, 1)
                    s.activation(SQ[:, :, :], XL[:, :, :], ACT.Square).then_inc(sems["sqA_done"], 1)
                    need(act, "n2_done", b, 1)
                    inv_root(rn[:, :], ln2[:, :], n2[:, :], N2_SCALE, 0.0, rnb[:, 0:1], "aA", b, 2)\
                        .then_inc(sems["rn_done"], 1)
                elif what == "a_turn":
                    copy_turned(XT1, 0, b, "qT_ps_done", "qT_done")
                elif what == "a_scores":
                    for h in range(NC_):
                        need(act, "clip_done", b, 2 * (h + 1))
                        s.activation(L1[:, h], SC[:, h], ACT.Ln, bias=1.0)
                        s.activation(L2[:, h], SC[:, h], ACT.Ln, bias=1.0, scale=-1.0)\
                            .then_inc(sems["logs_done"], 1)
                elif what == "a_angle":
                    for h in range(NC_):
                        need(act, "dlog_done", b, h + 1)
                        s.activation(L2[:, h], L1[:, h], ACT.Tanh, scale=0.25).then_inc(sems["aA"], 1)
                        need(act, "aA", b, 3 + 2 * h)
                        s.activation(SC[:, h], L2[:, h], ACT.Arctan).then_inc(sems["atan_done"], 1)
                        need(act, "atan_done", b, h + 1)
                        s.activation(L1[:, h], SC[:, h], ACT.Square, bias=half[:, 0:1], scale=2.0 / math.pi)\
                            .then_inc(sems["aA"], 1)
                        need(act, "aA", b, 4 + 2 * h)
                        s.activation(L2[:, h], L1[:, h], ACT.Square).then_inc(sems["t4_done"], 1)
                elif what == "a_mix":
                    for h in range(NC_):
                        need(act, "xo_ps_done", b, h + 1)
                        s.activation(flat(SQ[:, TPC * h:TPC * (h + 1), :]), PS[:, 2 + h, :], ACT.Square)\
                            .then_inc(sems["sqX_done"], 1)
                elif what == "a_out":
                    need(act, "n2_done", b, 2)
                    inv_root(rn[:, :], ln2[:, :], n2[:, :], N2_SCALE, 0.0, rnb[:, 0:1], "aA", b, 7)\
                        .then_inc(sems["rn_done"], 1)
                    rstd(S1, "A", b, 2, eps_l, 8)
                elif what == "b_route":
                    copy_turned(XT1, 0, b, "x1T_ps_done", "x1T_done")
                    need(act, "mB_done", b, 1)
                    s.activation(S1["w2"][:, :], S1["m2"][:, :], ACT.Exp).then_inc(sems["exB_done"], 1)
                    need(act, "g3T_ps_done", b, 1)
                    s.activation(g3T[:, :], g3T_ps[0:3 * E, :], ACT.Copy).then_inc(sems["g3T_done"], 1)
                elif what == "c_in":
                    need(act, "lgD_ps_done", b, 0)
                    copy_turned(XT2, 4, b, "x2T_ps_done", "x2T_done")
                    k = 0
                    for h in range(NC_):
                        for d in range(2 * ND):
                            need(act, "xz_ps_done", b, k + 1)
                            dst = (XS[:, d, TAPS - 1 + h * CH:TAPS - 1 + (h + 1) * CH] if d < ND
                                   else ZS[:, d - ND, h * CH:(h + 1) * CH])
                            s.activation(dst, PS[:, 4 + k % 4, :], ACT.Copy)\
                                .then_inc(sems["xs_done" if d < ND else "zs_done"], 1)
                            k += 1
                elif what == "c_silu":
                    need(act, "zs_done", b, 4)
                    s.activation(ZS[:, :, :], ZS[:, :, :], ACT.Silu).then_inc(sems["silz_done"], 1)
                    for d in range(ND):
                        need(act, "conv_done", b, d + 1)
                        s.activation(XA[:, d, :], XA[:, d, :], ACT.Silu).then_inc(sems["xa_done"], 1)
                elif what == "c_delta":
                    k = 0
                    for d in range(ND):
                        for h in range(NC_):
                            need(act, "dt_ps_done", b, k + 1)
                            s.activation(SP_[:, d, h * CH:(h + 1) * CH], PS[:, 4 + k, :], ACT.Abs,
                                         bias=bdt_s[:, d:d + 1]).then_inc(sems["abs_done"], 1)
                            k += 1
                        need(act, "abs_done", b, k)
                        s.activation(SP_[:, d, :], SP_[:, d, :], ACT.Exp, scale=-1.0).then_inc(sems["aC"], 1)
                        need(act, "aC", b, d + 1)
                        s.activation(SP_[:, d, :], SP_[:, d, :], ACT.Ln, bias=1.0).then_inc(sems["sp_done"], 1)
                    need(act, "bs3T_ps_done", b, 1)
                    s.activation(bs3T[:, :], bs3T_ps[0:3 * NS, :], ACT.Copy).then_inc(sems["bs3T_done"], 1)
                elif what == "d_route":
                    copy_turned(XT2, 4, b, "x3T_ps_done", "x3T_done")
                    need(act, "mD_done", b, 1)
                    s.activation(S2["ex"][:, :, :], S2["lg"][:, :, :], ACT.Exp).then_inc(sems["exD_done"], 1)
                elif what == "d_ffn":
                    for h in range(2):
                        need(act, "xdT_ps_done", b, h + 1)
                        s.activation(XDT[:, h * CH:(h + 1) * CH], PS[:, 4 + h, :], ACT.Copy)\
                            .then_inc(sems["xdT_done"], 1)
                    for e in range(E):
                        need(act, "g_ps_done", b, e + 1)
                        if e >= 2:
                            need(act, "yD_ps_done", b, e - 1)
                        s.activation(GE[:, e % 2].rearrange("p a b -> p (a b)"), PS[:, 6 + e % 2, :],
                                     ACT.Gelu_apprx_tanh).then_inc(sems["gelu_done"], 1)
                    for h in range(2):
                        need(act, "yD_ps_done", b, TPC * (h + 1))
                        s.activation(flat(YD[:, TPC * h:TPC * (h + 1), :]), PS[:, 4 + h, :], ACT.Copy)\
                            .then_inc(sems["yD_done"], 1)
                elif what == "d_out":
                    rstd(S2, "D", b, 1, eps_l, 1)

            def copy_acc(b, h):
                need(act, "oB_acc_done", b, E * NFB * (h + 1))
                s.activation(OT[:, h, :], PS[:, ACC, :], ACT.Copy).then_inc(sems["oT_done"], 1)

            schedule(act, part)

        @block.vector
        def _(dve):
            v = nc.vector
            count = {}

            def step(ins, name, b):
                count[name] = count.get(name, 0) + 1
                ins.then_inc(sems[name], 1)
                need(dve, name, b, count[name])

            def norm_in(small, src, block_name, b):
                for t in range(NT):
                    ins = v.bn_stats(small["bst"][:, t, :], src[:, t, :])
                step(ins, "v" + block_name, b)
                v.memset(held[:, :], 0.0)
                for t in range(NT):
                    ins = v.bn_aggr(small["mv"][:, t, :], small["bst"][:, t, :])
                ins.then_inc(sems[f"mv{block_name}_done"], 1)

            def norm_out(small, dst, src, block_name, b, k, done):
                need(dve, f"rstd{block_name}_done", b, k)
                for t in range(NT):
                    ins = v.tensor_scalar(dst[:, t, :], src[:, t, :], small["mv"][:, t, 0:1],
                                          small["rstd"][:, t:t + 1], ALU.subtract, ALU.mult)
                ins.then_inc(sems[done], 1)

            def pick(S, mx, oh, name, b):
                step(v.tensor_reduce(mx[:, :], S["lg"][:, :, :], AX, ALU.max), name, b)
                step(v.tensor_tensor(out=S["t8a"][:, :, :], in0=S["lg"][:, :, :], in1=per_tile(mx), op=ALU.is_equal),
                     name, b)
                step(v.tensor_tensor(out=S["t8b"][:, :, :], in0=S["t8a"][:, :, :], in1=per_token(first, E),
                                     op=ALU.mult), name, b)
                step(v.tensor_reduce(S["ms"][:, :], S["t8b"][:, :, :], AX, ALU.max), name, b)
                step(v.tensor_tensor(out=oh[:, :, :], in0=S["t8b"][:, :, :], in1=per_tile(S["ms"]), op=ALU.is_equal),
                     name, b)

            def split3(dst, rest, src, name, b):
                step(v.tensor_copy(dst[0], src), name, b)
                step(v.tensor_tensor(out=rest, in0=src, in1=dst[0], op=ALU.subtract), name, b)
                step(v.tensor_copy(dst[1], rest), name, b)
                step(v.tensor_tensor(out=rest, in0=rest, in1=dst[1], op=ALU.subtract), name, b)
                return v.tensor_copy(dst[2], rest)

            v.memset(eps_a[:, :], 1e-12)
            v.memset(eps_l[:, :], 1e-5)
            v.memset(half[:, :], 0.5)
            v.memset(rnb[:, :], RN_BIAS).then_inc(setup_v, 1)
            dve.wait_ge(setup_a, 2)
            v.tensor_scalar(nega[:, :, :], nega[:, :, :], -1.0, None, ALU.mult)
            v.tensor_reduce(ms[:, 0:NI], SQ[:, 0:NI, :], AX, ALU.add).then_inc(setup_v, 1)
            dve.wait_ge(setup_v, 2)
            v.tensor_scalar(n2[:, 0:NI], ms[:, 0:NI], 1e-24, None, ALU.max).then_inc(setup_v, 1)
            dve.wait_ge(setup_a, 4)
            for i in range(NI):
                ins = v.tensor_scalar(kn[:, i, :], kn[:, i, :], rn[:, i:i + 1], None, ALU.mult)
            ins.then_inc(setup_v, 1)
            parts = [b2_p[:, i, :] for i in range(3)]
            v.tensor_copy(parts[0], b2_f[:, :]).then_inc(setup_v, 1)
            dve.wait_ge(setup_v, 5)
            v.tensor_tensor(out=b2_r[:, :], in0=b2_f[:, :], in1=parts[0], op=ALU.subtract).then_inc(setup_v, 1)
            dve.wait_ge(setup_v, 6)
            v.tensor_copy(parts[1], b2_r[:, :]).then_inc(setup_v, 1)
            dve.wait_ge(setup_v, 7)
            v.tensor_tensor(out=b2_r[:, :], in0=b2_r[:, :], in1=parts[1], op=ALU.subtract).then_inc(setup_v, 1)
            dve.wait_ge(setup_v, 8)
            v.tensor_copy(parts[2], b2_r[:, :]).then_inc(setup_v, 1)

            def skip_and_y(b, d):
                need(dve, "y_acc_done", b, NQ // ND * (d + 1))
                v.scalar_tensor_tensor(out=YX[:, d, :], in0=XA[:, d, :], scalar=dsk[:, d:d + 1],
                                       in1=flat(PS[:, YB:YB + 2, :]), op0=ALU.mult, op1=ALU.add)\
                    .then_inc(sems["yx_done"], 1)

            def part(what, b, c=None):
                if what == "mix_and_scan":
                    for j in range(NJ):
                        if c is not None:
                            k = j
                            need(dve, "dA_done", c, k + 1)
                            need(dve, "spread_done", c, k + 1)
                            if k >= N_H:
                                need(dve, "y_acc_done", c, k // QUAD - N_H // QUAD + 1)
                            v.tensor_tensor_scan(HS[:, k % N_H, :], dA[:, k % N_A, :],
                                                 flat(PS[:, SPR:SPR + 2, :]), 0.0, ALU.mult, ALU.add)\
                                .then_inc(sems["scan_done"], 1)
                        if b is not None:
                            need(dve, "gate_ps_done", b, j // NFB + 1)
                            need(dve, "relu_done", b, j + 1)
                            if j >= 2:
                                need(dve, "oB_acc_done", b, j - 1)
                            v.tensor_tensor(out=HG[:, j % 2, :], in0=HR[:, j % 2, :], in1=PS[:, GATE, :],
                                            op=ALU.mult).then_inc(sems["hg_done"], 1)
                        if c is not None and j == NS + QUAD:
                            skip_and_y(c, 0)
                elif what == "c_out":
                    skip_and_y(b, ND - 1)
                    need(dve, "out_stored", b, 16)
                    for h in range(NC_):
                        need(dve, "oC_ps_done", b, h + 1)
                        ins = v.tensor_tensor(out=flat(Y2[:, TPC * h:TPC * (h + 1), :]), in0=PS[:, 6 + h, :],
                                              in1=flat(X2[:, TPC * h:TPC * (h + 1), :]), op=ALU.add)
                    ins.then_inc(sems["yC_done"], 1)
                    need(dve, "yC_done", b, 1)
                    norm_in(S2, Y2, "C", b)
                    norm_out(S2, X3, Y2, "C", b, 1, "x3_done")
                    assert count.pop("vC") == per["vC"]
                elif what == "b_out":
                    for h in range(NC_):
                        need(dve, "oB_ps_done", b, h + 1)
                        ins = v.tensor_tensor(out=flat(XL[:, TPC * h:TPC * (h + 1), :]), in0=PS[:, h, :],
                                              in1=flat(X1[:, TPC * h:TPC * (h + 1), :]), op=ALU.add)
                    ins.then_inc(sems["yB_done"], 1)
                    need(dve, "yB_done", b, 1)
                    norm_in(S1, XL, "B", b)
                    norm_out(S1, X2, XL, "B", b, 1, "x2_done")
                    assert count.pop("vB") == per["vB"]
                elif what == "a_norm":
                    need(dve, "x_loaded", b, 16)
                    norm_in(S1, X, "A", b)
                    norm_out(S1, XL, X, "A", b, 1, "xh_done")
                    need(dve, "sqA_done", b, 1)
                    step(v.tensor_reduce(ms[:, :], SQ[:, :, :], AX, ALU.add), "vA", b)
                    v.tensor_scalar(n2[:, :], ms[:, :], 1e-24, None, ALU.max).then_inc(sems["n2_done"], 1)
                    need(dve, "rn_done", b, 1)
                    for t in range(NT):
                        ins = v.tensor_scalar(XL[:, t, :], XL[:, t, :], rn[:, t:t + 1], None, ALU.mult)
                    ins.then_inc(sems["qn_done"], 1)
                elif what == "a_scores":
                    for u in range(2 * NC_):
                        h, i2 = u // 2, 2 * (u % 2)
                        need(dve, "s_ps_done", b, u + 1)
                        v.tensor_scalar(SC[:, h, i2:i2 + 2, :], PS[:, i2:i2 + 2, :], S_MAX, -S_MAX,
                                        ALU.min, ALU.max).then_inc(sems["clip_done"], 1)
                    for h in range(NC_):
                        need(dve, "logs_done", b, h + 1)
                        v.tensor_tensor(out=L1[:, h], in0=L1[:, h], in1=L2[:, h], op=ALU.subtract)\
                            .then_inc(sems["dlog_done"], 1)
                elif what == "a_mix":
                    for h in range(NC_):
                        need(dve, "t4_done", b, h + 1)
                        v.tensor_scalar(SC[:, h], SC[:, h], 2.0 / math.pi, 0.5, ALU.mult, ALU.add)
                        step(v.tensor_tensor(out=L2[:, h], in0=L2[:, h], in1=L2[:, h], op=ALU.mult), "vA", b)
                        v.tensor_tensor(out=L1[:, h], in0=L2[:, h], in1=SC[:, h], op=ALU.mult)\
                            .then_inc(sems["bpow_done"], 1)
                elif what == "a_out":
                    for h in range(NC_):
                        need(dve, "sqX_done", b, h + 1)
                        ins = v.tensor_reduce(ms[:, TPC * h:TPC * (h + 1)], SQ[:, TPC * h:TPC * (h + 1), :],
                                              AX, ALU.add)
                    step(ins, "vA", b)
                    v.tensor_scalar(n2[:, :], ms[:, :], 1e-24, None, ALU.max).then_inc(sems["n2_done"], 1)
                    need(dve, "rn_done", b, 2)
                    need(dve, "pA", b, 2)
                    for t in range(NT):
                        h, r = t // TPC, t % TPC
                        ins = v.scalar_tensor_tensor(out=XL[:, t, :], in0=PS[:, 2 + h, r * P:(r + 1) * P],
                                                     scalar=rn[:, t:t + 1], in1=X[:, t, :],
                                                     op0=ALU.mult, op1=ALU.add)
                    ins.then_inc(sems["yA_done"], 1)
                    need(dve, "yA_done", b, 1)
                    norm_in(S1, XL, "A", b)
                    norm_out(S1, X1, XL, "A", b, 2, "x1_done")
                    assert count.pop("vA") == per["vA"]
                elif what == "b_route":
                    S, m = S1, "vB"
                    need(dve, "lgB_ps_done", b, 1)
                    step(v.tensor_tensor(out=S["lg"][:, :, :], in0=PS[:, 2, 0:NT * E].rearrange("p (t e) -> p t e", e=E),
                                         in1=per_token(br_bc, E), op=ALU.add), m, b)
                    pick(S, S["m1"], S["oh1"], m, b)
                    step(v.scalar_tensor_tensor(out=S["lg"][:, :, :], in0=S["oh1"][:, :, :], scalar=-3.0e38,
                                                in1=S["lg"][:, :, :], op0=ALU.mult, op1=ALU.add), m, b)
                    pick(S, S["m2"], S["oh2"], m, b)
                    v.tensor_tensor(out=S["m2"][:, :], in0=S["m2"][:, :], in1=S["m1"][:, :], op=ALU.subtract)\
                        .then_inc(sems["mB_done"], 1)
                    need(dve, "exB_done", b, 1)
                    step(v.tensor_scalar(S["w1"][:, :], S["w2"][:, :], 1.0, None, ALU.add), m, b)
                    step(v.reciprocal(S["w1"][:, :], S["w1"][:, :]), m, b)
                    step(v.tensor_tensor(out=S["w2"][:, :], in0=S["w2"][:, :], in1=S["w1"][:, :], op=ALU.mult), m, b)
                    v.tensor_tensor(out=S["t8a"][:, :, :], in0=S["oh1"][:, :, :], in1=per_tile(S["w1"]), op=ALU.mult)
                    step(v.tensor_tensor(out=S["t8b"][:, :, :], in0=S["oh2"][:, :, :], in1=per_tile(S["w2"]),
                                         op=ALU.mult), m, b)
                    step(v.tensor_tensor(out=S["t8a"][:, :, :], in0=S["t8a"][:, :, :], in1=S["t8b"][:, :, :],
                                         op=ALU.add), m, b)
                    split3([g3[:, :, i, :] for i in range(3)], S["t8b"][:, :, :], S["t8a"][:, :, :], m, b)\
                        .then_inc(sems["g3_done"], 1)
                elif what == "c_in":
                    for d in range(ND):
                        need(dve, "xs_done", b, 2 * ND)
                        step(v.tensor_scalar(XA[:, d, :], XS[:, d, 0:T], cw_s[:, d, 0:1], cb_s[:, d:d + 1],
                                             ALU.mult, ALU.add), "vC", b)
                        for k in range(1, TAPS):
                            ins = v.scalar_tensor_tensor(out=XA[:, d, :], in0=XS[:, d, k:k + T],
                                                         scalar=cw_s[:, d, k:k + 1], in1=XA[:, d, :],
                                                         op0=ALU.mult, op1=ALU.add)
                            if k < TAPS - 1:
                                step(ins, "vC", b)
                            else:
                                ins.then_inc(sems["conv_done"], 1)
                elif what == "c_delta":
                    k = 0
                    for d in range(ND):
                        for h in range(NC_):
                            need(dve, "abs_done", b, k + 1)
                            v.tensor_scalar(DT[:, d, h * CH:(h + 1) * CH], PS[:, 4 + k, :], bdt_s[:, d:d + 1],
                                            0.0, ALU.add, ALU.max).then_inc(sems["vrel_done"], 1)
                            k += 1
                    need(dve, "bs_ps_done", b, 1)
                    step(v.tensor_copy(bsr[:, :, :], PS[:, 4, 0:NT * NS].rearrange("p (t n) -> p t n", n=NS)),
                         "vC", b)
                    split3([bs3[:, :, i, :] for i in range(3)], bsr[:, :, :], bsr[:, :, :], "vC", b)\
                        .then_inc(sems["bs3_done"], 1)
                elif what == "d_route":
                    S, m = S2, "vD"
                    need(dve, "lgD_ps_done", b, 1)
                    step(v.tensor_copy(S["lg"][:, :, :], PS[:, 6, 0:NT * E].rearrange("p (t e) -> p t e", e=E)), m, b)
                    pick(S, S["m1"], S["oh1"], m, b)
                    v.tensor_copy(maskb[:, :, :], S["oh1"][:, :, :]).then_inc(sems["mask_done"], 1)
                    v.tensor_tensor(out=S["lg"][:, :, :], in0=S["lg"][:, :, :], in1=per_tile(S["m1"]), op=ALU.subtract)\
                        .then_inc(sems["mD_done"], 1)
                    step(v.tensor_tensor(out=S["t8a"][:, :, :], in0=S["oh1"][:, :, :], in1=per_token(base128, E),
                                         op=ALU.mult), m, b)
                    step(v.tensor_reduce(S["slot"][:, :], S["t8a"][:, :, :], AX, ALU.add), m, b)
                elif what == "d_slots":
                    S, m = S2, "vD"
                    need(dve, "pos_ps_done", b, 1)
                    step(v.tensor_tensor(out=S["t8b"][:, :, :], in0=S["oh1"][:, :, :],
                                         in1=PS[:, 7, 0:NT * E].rearrange("p (t e) -> p t e", e=E),
                                         op=ALU.mult), m, b)
                    step(v.tensor_reduce(S["pos"][:, :], S["t8b"][:, :, :], AX, ALU.add), m, b)
                    v.tensor_tensor(out=S["slot"][:, :], in0=S["slot"][:, :], in1=S["pos"][:, :], op=ALU.add)
                    step(v.tensor_scalar(S["over"][:, :], S["pos"][:, :], float(CAP), None, ALU.is_ge), m, b)
                    step(v.scalar_tensor_tensor(out=S["ms"][:, :], in0=S["over"][:, :], scalar=float(SLOTS),
                                                in1=S["slot"][:, :], op0=ALU.mult, op1=ALU.add), m, b)
                    v.tensor_copy(put_i[:, :], S["ms"][:, :]).then_inc(sems["put_done"], 1)
                    step(v.tensor_scalar(S["m2"][:, :], S["slot"][:, :], float(SLOTS - 1), None, ALU.min), m, b)
                    v.tensor_copy(get_i[:, :], S["m2"][:, :]).then_inc(sems["get_done"], 1)
                    need(dve, "exD_done", b, 1)
                    step(v.tensor_reduce(S["w1"][:, :], S["ex"][:, :, :], AX, ALU.add), m, b)
                    step(v.reciprocal(S["w1"][:, :], S["w1"][:, :]), m, b)
                    step(v.tensor_scalar(S["w2"][:, :], S["over"][:, :], -1.0, 1.0, ALU.mult, ALU.add), m, b)
                    step(v.tensor_tensor(out=S["gk"][:, :], in0=S["w1"][:, :], in1=S["w2"][:, :], op=ALU.mult), m, b)
                elif what == "d_out":
                    need(dve, "gathered", b, 16 * NT)
                    for t in range(NT):
                        ins = v.scalar_tensor_tensor(out=Y2[:, t, :], in0=XD[:, t, :], scalar=S2["gk"][:, t:t + 1],
                                                     in1=X3[:, t, :], op0=ALU.mult, op1=ALU.add)
                    ins.then_inc(sems["yF_done"], 1)
                    need(dve, "yF_done", b, 1)
                    norm_in(S2, Y2, "D", b)
                    norm_out(S2, YD, Y2, "D", b, 1, "x4_done")
                    assert count.pop("vD") == per["vD"]

            schedule(dve, part)

        @block.tensor
        def _(pe):
            m = nc.tensor

            pe.wait_ge(consts_done, CONSTS)
            pe.wait_ge(setup_v, 9)
            pe.wait_ge(weights_in, W_ALL)
            for i in range(NI):
                ins = m.transpose(PS[:, 6, i * P:(i + 1) * P], kn[:, i, :], ident[:, :])
            ins.then_inc(setup_pe, 1)
            pe.wait_ge(setup_a, 5)

            def turn(b, src, bank, done, wait_name, wait_k):
                need(pe, wait_name, b, wait_k)
                for t in range(NT):
                    h, r = t // TPC, t % TPC
                    ins = m.transpose(PS[:, bank + h, r * P:(r + 1) * P], src[:, t, :], ident[:, :])
                    if r == TPC - 1:
                        ins.then_inc(sems[done], 1)

            def logits(b, xT, w, bank, xT_done, done):
                need(pe, xT_done, b, 2)
                for t in range(NT):
                    ins = m.matmul(PS[:, bank, t * E:(t + 1) * E], xT[:, t * P:(t + 1) * P], w[:, :],
                                   start=True, stop=True)
                ins.then_inc(sems[done], 1)

            def up(b, j):
                h, e, f = j // (E * NFB), j // NFB % E, j % NFB
                if j >= 2:
                    need(pe, "relu_done", b, j - 1)
                m.matmul(PS[:, Z0 + j % 2, :], w1b_s[:, e, f * P:(f + 1) * P], XT1[:, h * CH:(h + 1) * CH],
                         start=True, stop=True).then_inc(sems["z_ps_done"], 1)

            def gate(b, j):
                h, e = j // (E * NFB), j // NFB % E
                if j:
                    need(pe, "hg_done", b, j)
                m.matmul(PS[:, GATE, :], sel_gate[:, e, :], g3T[:, h * CH:(h + 1) * CH],
                         start=True, stop=True).then_inc(sems["gate_ps_done"], 1)

            def down(b, j):
                h, e, f = j // (E * NFB), j // NFB % E, j % NFB
                if j % (E * NFB) == 0:
                    if h:
                        need(pe, "oT_done", b, h)
                    for i in range(3):
                        m.matmul(PS[:, ACC, :], b2_p[:, i, :], g3T[:, h * CH:(h + 1) * CH],
                                 start=(i == 0), stop=False)
                need(pe, "hg_done", b, j + 1)
                m.matmul(PS[:, ACC, :], w2b_s[:, e, f, :], HG[:, j % 2, :],
                         start=False, stop=(j % (E * NFB) == E * NFB - 1)).then_inc(sems["oB_acc_done"], 1)

            def spread(c, k):
                if k:
                    need(pe, "scan_done", c, k)
                for h in range(NC_):
                    ins = m.matmul(PS[:, SPR + h, :], sel_bs[:, k % NS, :], bs3T[:, h * CH:(h + 1) * CH],
                                   start=True, stop=True)
                ins.then_inc(sems["spread_done"], 1)

            def sum_states(c, q):
                if q == NQ // ND:
                    need(pe, "yx_done", c, 1)
                need(pe, "quad_done", c, q + 1)
                for h in range(NC_):
                    ins = m.matmul(PS[:, YB + h, :], ident[:, :], HS[:, QUAD * q % N_H, h * CH:(h + 1) * CH],
                                   start=(q % (NQ // ND) == 0), stop=(q % (NQ // ND) == NQ // ND - 1))
                ins.then_inc(sems["y_acc_done"], 1)

            def part(what, b, c=None):
                if what == "mix_and_scan":
                    if b is not None:
                        up(b, 0)
                        need(pe, "g3T_done", b, 1)
                        gate(b, 0)
                    if c is not None:
                        need(pe, "bs3T_done", c, 1)
                        need(pe, "vrel_done", c, 4)
                        spread(c, 0)
                    for j in range(NJ):
                        if b is not None:
                            if j + 1 < NJ:
                                up(b, j + 1)
                            if j:
                                down(b, j - 1)
                                if j % NFB == 0:
                                    gate(b, j)
                        if c is not None:
                            if j >= QUAD + 2 and (j - QUAD - 2) % QUAD == 0:
                                sum_states(c, (j - QUAD - 2) // QUAD)
                            if j + 1 < NK:
                                spread(c, j + 1)
                    if b is not None:
                        down(b, NJ - 1)
                    if c is not None:
                        sum_states(c, NQ - 1)
                elif what == "c_out":
                    need(pe, "yz_done", b, ND)
                    for t in range(NT):
                        h, r = t // TPC, t % TPC
                        for i in range(ND):
                            ins = m.matmul(PS[:, 6 + h, r * P:(r + 1) * P], YX[:, i, t * P:(t + 1) * P],
                                           wout_s[:, i, :], start=(i == 0), stop=(i == ND - 1))
                        if r == TPC - 1:
                            ins.then_inc(sems["oC_ps_done"], 1)
                elif what == "b_out":
                    for h in range(NC_):
                        need(pe, "oT_done", b, h + 1)
                        for r in range(TPC):
                            ins = m.transpose(PS[:, h, r * P:(r + 1) * P], OT[:, h, r * P:(r + 1) * P],
                                              ident[:, :])
                        ins.then_inc(sems["oB_ps_done"], 1)
                elif what == "a_turn":
                    turn(b, XL, 0, "qT_ps_done", "qn_done", 1)
                elif what == "a_scores":
                    for u in range(2 * NC_):
                        h, i2 = u // 2, 2 * (u % 2)
                        need(pe, "qT_done", b, 2)
                        if u >= 2:
                            need(pe, "clip_done", b, u - 1)
                        for i in range(i2, i2 + 2):
                            ins = m.matmul(PS[:, i, :], knT[:, i * P:(i + 1) * P], XT1[:, h * CH:(h + 1) * CH],
                                           start=True, stop=True)
                        ins.then_inc(sems["s_ps_done"], 1)
                elif what == "a_mix":
                    for h in range(NC_):
                        need(pe, "bpow_done", b, h + 1)
                        for r in range(TPC):
                            for i in range(NI):
                                ins = m.matmul(PS[:, 2 + h, r * P:(r + 1) * P], L1[:, h, i, r * P:(r + 1) * P],
                                               qw[:, i, :], start=(i == 0), stop=(i == NI - 1))
                        ins.then_inc(sems["xo_ps_done"], 1)
                elif what == "b_route":
                    turn(b, X1, 0, "x1T_ps_done", "x1_done", 1)
                    logits(b, XT1, wr_s, 2, "x1T_done", "lgB_ps_done")
                    need(pe, "g3_done", b, 1)
                    for t in range(NT):
                        ins = m.transpose(g3T_ps[0:3 * E, t * P:(t + 1) * P],
                                          g3[:, t].rearrange("p a e -> p (a e)"), identb[:, :])
                    ins.then_inc(sems["g3T_ps_done"], 1)
                elif what == "c_in":
                    turn(b, X2, 4, "x2T_ps_done", "x2_done", 1)
                    need(pe, "put_done", b, 0)
                    k = 0
                    for h in range(NC_):
                        need(pe, "x2T_done", b, 2)
                        for d in range(2 * ND):
                            if k >= 4:
                                need(pe, "xs_done" if d < ND else "zs_done", b, k % 2 + 1)
                            m.matmul(PS[:, 4 + k % 4, :], win_s[:, d * P:(d + 1) * P],
                                     XT2[:, h * CH:(h + 1) * CH], start=True, stop=True)\
                                .then_inc(sems["xz_ps_done"], 1)
                            k += 1
                elif what == "c_silu":
                    need(pe, "xs_done", b, 4)
                    need(pe, "zs_done", b, 4)
                elif what == "c_delta":
                    need(pe, "xa_done", b, ND)
                    need(pe, "yD_done", b, 0)
                    k = 0
                    for d in range(ND):
                        for h in range(NC_):
                            for i in range(ND):
                                ins = m.matmul(PS[:, 4 + k, :], wdt_s[:, i, d * P:(d + 1) * P],
                                               XA[:, i, h * CH:(h + 1) * CH], start=(i == 0), stop=(i == ND - 1))
                            ins.then_inc(sems["dt_ps_done"], 1)
                            k += 1
                    need(pe, "vrel_done", b, 2)
                    for t in range(NT):
                        for i in range(ND):
                            ins = m.matmul(PS[:, 4, t * NS:(t + 1) * NS], XA[:, i, t * P:(t + 1) * P],
                                           wx_s[:, i, :], start=(i == 0), stop=(i == ND - 1))
                    ins.then_inc(sems["bs_ps_done"], 1)
                    need_apart(pe, "bs3_done", b, 1)
                    for t in range(NT):
                        ins = m.transpose(bs3T_ps[0:3 * NS, t * P:(t + 1) * P],
                                          bs3[:, t].rearrange("p a n -> p (a n)"), identb[:, :])
                    ins.then_inc(sems["bs3T_ps_done"], 1)
                elif what == "d_route":
                    turn(b, X3, 4, "x3T_ps_done", "x3_done", 1)
                    logits(b, XT2, wg_s, 6, "x3T_done", "lgD_ps_done")
                elif what == "d_slots":
                    need(pe, "mask_done", b, 1)
                    pos_ps = PS[:, 7, 0:NT * E].rearrange("p (t e) -> p t e", e=E)
                    m.matmul(pos_ps, before[:, :], maskb[:, :, :], start=True, stop=False, skip_group_check=True)
                    for t in range(NT - 1):
                        ins = m.matmul(pos_ps[:, t + 1:NT, :], onesb[:, :],
                                       maskb[:, t:t + 1, :].to_broadcast([P, NT - 1 - t, E]),
                                       start=False, stop=(t == NT - 2), skip_group_check=True)
                    ins.then_inc(sems["pos_ps_done"], 1)
                elif what == "d_ffn":
                    turn(b, XD, 4, "xdT_ps_done", "slots_loaded", 16)
                    for e in range(E + 1):
                        if e < E:
                            need(pe, "xdT_done", b, 2)
                            if e >= 2:
                                need(pe, "gelu_done", b, e - 1)
                            for f in range(NFD):
                                ins = m.matmul(PS[:, 6 + e % 2, f * P:(f + 1) * P],
                                               w1d_s[:, e, f * P:(f + 1) * P], XDT[:, e * P:(e + 1) * P],
                                               start=True, stop=True)
                            ins.then_inc(sems["g_ps_done"], 1)
                        if e:
                            need(pe, "gelu_done", b, e)
                            h, r = (e - 1) // TPC, (e - 1) % TPC
                            for f in range(NFD):
                                ins = m.matmul(PS[:, 4 + h, r * P:(r + 1) * P], GE[:, (e - 1) % 2, f, :],
                                               w2d_s[:, e - 1, f, :], start=(f == 0), stop=(f == NFD - 1))
                            ins.then_inc(sems["yD_ps_done"], 1)

            schedule(pe, part)


_INS = [
    "L0_attn_hidden_states", "L0_attn_ln_weight", "L0_attn_ln_bias", "L0_attn_k_weight", "L0_attn_q_weight",
    "L0_attn_bias", "L0_ffn_Wr", "L0_ffn_br", "L0_ffn_W1", "L0_ffn_b1", "L0_ffn_W2", "L0_ffn_b2",
    "L1_attn_W_in", "L1_attn_conv_w", "L1_attn_conv_b", "L1_attn_A_log", "L1_attn_D", "L1_attn_W_x",
    "L1_attn_W_dt", "L1_attn_b_dt", "L1_attn_W_out", "L1_ffn_Wg", "L1_ffn_W1", "L1_ffn_W2",
]
_OUTS = [((8, 1024, 128), "float32")]


def kernel(**inputs):
    import numpy as _np
    import concourse.bacc as _bacc
    from concourse import mybir as _mybir
    from concourse.bass_utils import run_bass_kernel_spmd as _run

    nc = _bacc.Bacc("TRN2", target_bir_lowering=False, num_devices=1)
    arrays, args = {}, []
    for name in _INS:
        a = _np.ascontiguousarray(inputs[name])
        arrays[f"in_{name}_dram"] = a
        args.append(nc.dram_tensor(f"in_{name}_dram", a.shape, _mybir.dt.from_np(a.dtype), kind="ExternalInput").ap())
    for i, (shape, dtype) in enumerate(_OUTS):
        dt = _mybir.dt.from_np(_np.dtype(dtype))
        args.append(nc.dram_tensor(f"out_{i}_dram", shape, dt, kind="ExternalOutput").ap())
    build_layer_stack(nc, *args)
    r = _run(nc, [arrays], core_ids=[0])
    got = tuple(r.results[0][f"out_{i}_dram"] for i in range(len(_OUTS)))
    return got[0]
```

```python
import math
from contextlib import ExitStack

import concourse.bass as bass
from concourse import mybir


CONSTS = 17


def build_layer_stack(
    nc: bass.Bass,
    x_in, ln_w, ln_b, k_w, q_w, l0_bias,
    wr, br, w1b, b1b, w2b, b2b,
    w_in, conv_w, conv_b, a_log, d_skip, w_x, w_dt, b_dt, w_out,
    wg, w1d, w2d,
    out,
):
    fp32, bf16, u32 = mybir.dt.float32, mybir.dt.bfloat16, mybir.dt.uint32
    ACT = mybir.ActivationFunctionType
    ALU = mybir.AluOpType
    AX = mybir.AxisListType.X

    P = 128
    NB, T, H = x_in.shape
    NT = T // P
    CH = 512
    NC_ = T // CH
    TPC = CH // P
    I = k_w.shape[0]
    NI = I // P
    E = wr.shape[1]
    FB = w1b.shape[2]
    NFB = FB // P
    DI = w_in.shape[1] // 2
    ND = DI // P
    NS = a_log.shape[1]
    TAPS = conv_w.shape[2]
    FD = w1d.shape[2]
    NFD = FD // P
    CAP = T // E
    SLOTS = E * CAP
    assert CAP == P and H == P and NC_ == 2

    S_MAX = 1.0 - 1e-6
    N2_SCALE = 2.0 ** 16
    RN_BIAS = 0.5 * math.log(N2_SCALE)

    slot_x = nc.dram_tensor("slot_x", (SLOTS, H), fp32, kind="Internal").ap()
    slot_y = nc.dram_tensor("slot_y", (SLOTS, H), fp32, kind="Internal").ap()

    ctx = ExitStack()
    with ctx:
        def sb(name, shape, dt=fp32):
            return ctx.enter_context(nc.sbuf_tensor(name, shape, dt))

        per, sems = {}, {}

        def sem(name, per_row=0):
            sems[name] = ctx.enter_context(nc.semaphore(name))
            per[name] = per_row
            return sems[name]

        def raised(name, b, k):
            return b * per[name] + k

        def need_rows(eng, name, b):
            if not isinstance(b, int) or b:
                eng.wait_ge(sems[name], b * per[name])

        ident = sb("ident", [P, P])
        identb = sb("identb", [P, P], bf16)
        onesb = sb("onesb", [P, P], bf16)
        before = sb("before", [P, P], bf16)
        sel_gate = sb("sel_gate", [3 * E, E, P], bf16)
        sel_bs = sb("sel_bs", [3 * NS, NS, P], bf16)
        first = sb("first", [P, E])
        base128 = sb("base128", [P, E])
        lnw_bc = sb("lnw_bc", [P, H])
        lnb_bc = sb("lnb_bc", [P, H])
        bias_bc = sb("bias_bc", [P, H])
        br_bc = sb("br_bc", [P, E])
        knT = sb("knT", [P, I])
        qw = sb("qw", [P, NI, H])
        wr_s = sb("wr_s", [P, E])
        w1b_s = sb("w1b_s", [P, E, FB])
        b1_s = sb("b1_s", [P, E, NFB])
        w2b_s = sb("w2b_s", [P, E, NFB, H])
        b2_p = sb("b2_p", [3 * E, 3, H], bf16)
        win_s = sb("win_s", [P, 2 * DI])
        cw_s = sb("cw_s", [P, ND, TAPS])
        cb_s = sb("cb_s", [P, ND])
        nega = sb("nega", [P, ND, NS])
        dsk = sb("dsk", [P, ND])
        wx_s = sb("wx_s", [P, ND, NS])
        wdt_s = sb("wdt_s", [P, ND, DI])
        bdt_s = sb("bdt_s", [P, ND])
        wout_s = sb("wout_s", [P, ND, H])
        wg_s = sb("wg_s", [P, E])
        w1d_s = sb("w1d_s", [P, E, FD])
        w2d_s = sb("w2d_s", [P, E, NFD, H])
        X = sb("X", [P, NT, H])
        XL = sb("XL", [P, NT, H])
        SQ = sb("SQ", [P, NT, H])
        X1 = sb("X1", [P, NT, H])
        X2 = sb("X2", [P, NT, H])
        X3 = sb("X3", [P, NT, H])
        Y2 = sb("Y2", [P, NT, H])
        XD = sb("XD", [P, NT, H])
        YD = Y2
        XT1 = sb("XT1", [P, T])
        XT2 = sb("XT2", [P, T])
        XDT = XT1[:, 0:SLOTS]
        SQA = XT2[:, :].rearrange("p (n h) -> p n h", n=NT)
        OT = SQ[:, :, :].rearrange("p (c r) h -> p c (r h)", c=NC_)
        WIDE = NC_ * NI * CH
        wide = sb("wide", [P, 3 * WIDE])

        def of_a(n):
            return wide[:, n * WIDE:(n + 1) * WIDE].rearrange("p (c i t) -> p c i t", c=NC_, i=NI)

        SC, L1, L2 = of_a(0), of_a(1), of_a(2)
        b2_f, b2_r = X3[0:3 * E, 0, :], X3[0:3 * E, 1, :]
        kn = wide[:, 0:NI * H].rearrange("p (n h) -> p n h", n=NI)
        N_H, N_A = 8, 4
        HS = wide[:, 0:N_H * T].rearrange("p (n t) -> p n t", n=N_H)
        dA = wide[:, N_H * T:(N_H + N_A) * T].rearrange("p (n t) -> p n t", n=N_A)
        hidden = sb("hidden", [P, 5, CH])
        HR, HG = hidden[:, 0:2, :], hidden[:, 2:5, :]
        g3 = sb("g3", [P, NT, 3, E], bf16)
        g3T = sb("g3T", [3 * E, T], bf16)
        XT3 = hidden[:, 0:2, :].rearrange("p a t -> p (a t)")
        XS = sb("XS", [P, ND, TAPS - 1 + T])
        YX = XS[:, :, TAPS - 1:]
        ZS = sb("ZS", [P, ND, T])
        XA = sb("XA", [P, ND, T])
        DT = sb("DT", [P, ND, T])
        SP_ = hidden[:, 0:4, :].rearrange("p a t -> p (a t)").rearrange("p (d t) -> p d t", d=ND)
        bsr = sb("bsr", [P, NT, NS])
        bs3 = sb("bs3", [P, NT, 3, NS], bf16)
        bs3T = sb("bs3T", [3 * NS, T], bf16)
        GE = SP_[:, 0, :].rearrange("p (k f s) -> p k f s", k=2, f=NFD)
        maskb = sb("maskb", [P, NT, E], bf16)
        put_i = sb("put_i", [P, NT], u32)
        get_i = sb("get_i", [P, NT], u32)
        eps_a = sb("eps_a", [P, 1])
        eps_l = sb("eps_l", [P, 1])
        t2_bias = sb("t2_bias", [P, 1])
        rnb = sb("rnb", [P, 1])
        held = sb("held", [P, 1])
        held_p = sb("held_p", [P, 2])

        def small(tag):
            shapes = {"bst": [P, NT, 6], "mv": [P, NT, 2], "nmr": [P, NT]}
            shapes.update({n_: [P, NT] for n_ in ("lnv", "rstd", "n2", "ln2", "rn", "m1", "m2", "ms", "w1", "w2",
                                                  "pos", "slot", "over", "gk")})
            shapes.update({n_: [P, NT, E] for n_ in ("lg", "t8a", "t8b", "oh1", "oh2", "ex")})
            return {n_: sb(n_ + tag, shape) for n_, shape in shapes.items()}

        S1, S2 = small("1"), small("2")
        n2, ln2, rn, ms = S1["n2"], S1["ln2"], S1["rn"], S1["ms"]

        PS = ctx.enter_context(nc.psum_tensor("PS", [P, 8, CH], fp32))
        Z0, GATE, ACC = 0, 2, 3

        def in_bank(k):
            return 4 + (k + 2) % 4

        SPR = 4
        g3T_ps = PS[:, 3, :].bitcast(bf16)
        bs3T_ps = PS[:, 5, :].bitcast(bf16)

        NJ = NC_ * E * NFB
        NK = ND * NS
        NY = NS - 1
        LEAD, EXTRA = 2, 0
        RESIDUAL_AT = 26
        D_AT, A_AT = 0, 8

        T2_SCALE = 2.0 / math.pi * (2.0 / math.pi) ** 0.125
        T2_BIAS = 0.5 * (2.0 / math.pi) ** 0.125

        for name, n in (
            ("x_loaded", 16), ("out_stored", 16),
            ("vA", 7), ("vB", 22), ("vC", 12), ("vD", 18),
            ("aA", 8), ("aB", 1), ("aC", 3), ("aD", 1),
            ("mvA_done", 2), ("mvB_done", 1), ("mvC_done", 1), ("mvD_done", 1),
            ("rstdA_done", 2), ("rstdB_done", 1), ("rstdC_done", 1), ("rstdD_done", 1),
            ("x1_done", 1), ("x2_done", 1), ("x3_done", 1), ("x4_done", 1),
            ("xh_done", 1), ("xbias_done", 2), ("nmrA_done", 1), ("nmrC_done", 1), ("nmrD_done", 1), ("xw_done", 1), ("xln_done", 1), ("sqA_done", 1),
            ("n2_done", 2), ("rn_done", 2), ("qn_done", 1), ("qT_ps_done", 2), ("qT_done", 2),
            ("s_ps_done", 4), ("clip_done", 4), ("logs_done", 2), ("dlog_done", 2), ("atan_done", 2),
            ("t4_done", 1), ("bpow_done", 2), ("xo_ps_done", 2), ("sqX_done", 2), ("yA_done", 1),
            ("x1T_ps_done", 2), ("x1T_done", 2), ("lgB_ps_done", 1), ("mB_done", 1), ("exB_done", 1),
            ("g3_done", 1), ("g3T_ps_done", 1), ("g3T_done", 1),
            ("z_ps_done", NJ), ("relu_done", NJ), ("gate_ps_done", 2 * E),
            ("hg_done", NJ), ("oB_acc_done", NJ), ("oT_done", 2), ("oB_ps_done", 2), ("yB_done", 1),
            ("x2T_ps_done", 2), ("x2T_done", 2), ("xs_ps_done", 4), ("z_in_ps_done", 4), ("xs_done", 4), ("zs_done", 4),
            ("silz_done", 1), ("conv_done", ND), ("xa_done", ND),
            ("dt_ps_done", 4), ("abs_done", 4), ("vrel_done", 4), ("sp_done", ND), ("dt_done", ND),
            ("bs_ps_done", 1), ("bs3_done", 1), ("bs3T_ps_done", 1), ("bs3T_done", 1),
            ("spread_done", NK), ("dA_done", NK), ("scan_done", NK), ("y_sum_done", ND * NY),
            ("yx_done", ND), ("yz_done", ND), ("oC_ps_done", 2), ("x2_kept", 1), ("yC_done", 1),
            ("x3T_ps_done", 2), ("x3T_done", 2), ("lgD_ps_done", 1), ("mD_done", 1), ("exD_done", 1),
            ("mask_done", 1), ("pos_ps_done", 1), ("put_done", 1), ("get_done", 1),
            ("scattered", 16 * NT), ("slots_loaded", 16), ("xdT_ps_done", 2), ("xdT_done", 2),
            ("g_ps_done", E), ("gelu_done", E), ("yD_ps_done", E), ("yD_done", 2), ("slots_stored", 16),
            ("gathered", 16 * NT), ("yF_done", 1),
        ):
            sem(name, n)
        consts_done = sem("consts_done")
        pe_sum_done = sem("pe_sum_done")
        weights_in = sem("weights_in")
        first_in = sem("first_in")
        setup_v = sem("setup_v")
        setup_a = sem("setup_a")
        setup_pe = sem("setup_pe")
        slots_zeroed = sem("slots_zeroed")
        N_FIRST, N_WEIGHTS = 7, 16 + 2 * E
        W_ALL = 16 * N_WEIGHTS

        block = ctx.enter_context(nc.Block())

        def need_apart(eng, name, b, k):
            eng.wait_ge(consts_done, CONSTS)
            eng.wait_ge(sems[name], raised(name, b, k))

        def scans_beside(j):
            before_j, after_j = (LEAD + n + min(n // 2, EXTRA) for n in (j, j + 1))
            return range(before_j, after_j)

        def on_pe(k, shared):
            return shared and k >= LEAD and k % 2 == 0 and k % NS != 0

        def pool_adds(k, shared):
            return sum(n % NS != 0 and not on_pe(n, shared) for n in range(max(k, k // NS * NS + 1) + 1))

        def pe_adds(k):
            return sum(on_pe(n, True) for n in range(k + 1))

        def per_tile(ap):
            return ap[:, :].unsqueeze(2).to_broadcast([P, NT, E])

        def per_token(ap, n):
            return ap[:, :].unsqueeze(1).to_broadcast([P, NT, n])

        def flat(ap):
            return ap.rearrange("p a b -> p (a b)")

        def schedule(eng, part):
            def turn(i, has_a, has_b, has_c, has_c1, has_d):
                a, b, c1 = i + 2, i + 1, i + 1
                if has_a:
                    part("load_x", a)
                if isinstance(i, int) and i == -2:
                    part("setup_rest", None)
                part("mix_and_scan", b if has_b else None, i if has_c else None, a if has_a else None,
                     i - 1 if not isinstance(i, int) or i >= 1 else None)
                if has_a:
                    part("a_turn", a)
                if has_c:
                    part("c_out", i)
                if has_b:
                    part("b_turn_back", b)
                if has_c:
                    part("c_norm", i, 0)
                if has_b:
                    part("b_out", b, 0)
                if has_c:
                    part("c_norm", i, 1)
                if has_b:
                    part("b_out", b, 1)
                if has_c:
                    part("c_norm", i, 2)
                if has_a:
                    part("a_scores", a, 0)
                if has_b:
                    part("b_out", b, 2)
                if has_a:
                    part("a_scores", a, 1)
                    part("a_logs", a, 0)
                if has_d:
                    part("d_turn", i)
                if has_c1:
                    part("c_turn", c1)
                if has_d:
                    part("d_route", i)
                if has_a:
                    part("a_logs", a, 1)
                if has_d:
                    part("d_slots", i)
                if has_c1:
                    part("c_in", c1)
                if has_a:
                    part("a_angle", a)
                if has_c1:
                    part("c_conv", c1)
                    part("c_silu", c1)
                if has_d:
                    part("d_slots_turn", i)
                if has_a:
                    part("a_mix", a, 0)
                if has_d:
                    part("d_ffn", i)
                if has_a:
                    part("a_mix", a, 1)
                part("log_exp_table", None)
                if has_a:
                    part("a_out", a, 0)
                if has_c1:
                    part("c_delta", c1, 0)
                if has_d:
                    part("d_gate", i)
                if has_a:
                    part("a_out", a, 1)
                    part("b_turn", a)
                    part("b_logits", a)
                if has_c1:
                    part("c_delta", c1, 1)
                if has_a:
                    part("b_route", a, 0)
                if has_c1:
                    part("scan_ahead", c1, range(0, LEAD // 2))
                if has_a:
                    part("b_route", a, 1)
                if has_c1:
                    part("scan_ahead", c1, range(LEAD // 2, LEAD))

            turn(-2, True, False, False, False, False)
            part("setup_rest_done", None)
            turn(-1, True, True, False, True, False)
            turn(0, True, True, True, True, True)
            with eng.Fori(1, NB - 2) as i:
                turn(i, True, True, True, True, True)
            turn(NB - 2, False, True, True, True, True)
            turn(NB - 1, False, False, True, False, True)
            part("mix_and_scan", None, None, None, NB - 1)

        @block.sync
        def _(sp):
            first_loads = [
                (kn[:, :, :], k_w.rearrange("(n p) h -> p n h", p=P)),
                (lnw_bc[:, :], ln_w.partition_broadcast(P)), (lnb_bc[:, :], ln_b.partition_broadcast(P)),
                (bias_bc[:, :], l0_bias.partition_broadcast(P)), (br_bc[:, :], br.partition_broadcast(P)),
                (qw[:, :, :], q_w.rearrange("(n p) h -> p n h", p=P)),
                (wr_s[:, :], wr),
            ]
            loads = [
                (w1b_s[:, :, :], w1b.rearrange("e d f -> d e f")),
                (b1_s[:, :, :], b1b.rearrange("e (n p) -> p e n", p=P)),
                (b2_f[0:E, :], b2b), (b2_f[E:2 * E, :], b2b), (b2_f[2 * E:3 * E, :], b2b),
                (win_s[:, :], w_in), (cw_s[:, :, :], conv_w.rearrange("(n p) o k -> p n (o k)", p=P)),
                (cb_s[:, :], conv_b.rearrange("(n p) -> p n", p=P)),
                (nega[:, :, :], a_log.rearrange("(n p) s -> p n s", p=P)),
                (dsk[:, :], d_skip.rearrange("(n p) -> p n", p=P)),
                (wx_s[:, :, :], w_x.rearrange("(n p) s -> p n s", p=P)),
                (wdt_s[:, :, :], w_dt.rearrange("(n p) s -> p n s", p=P)),
                (bdt_s[:, :], b_dt.rearrange("(n p) -> p n", p=P)),
                (wout_s[:, :, :], w_out.rearrange("(n p) h -> p n h", p=P)),
                (wg_s[:, :], wg), (w1d_s[:, :, :], w1d.rearrange("e d f -> d e f")),
            ]
            for dst, src in ((w2b_s, w2b), (w2d_s, w2d)):
                loads += [(dst[:, e], src[e].rearrange("(n p) h -> p n h", p=P)) for e in range(E)]
            assert len(first_loads) == N_FIRST and len(loads) == N_WEIGHTS
            for dst, src in first_loads:
                sp.dma_start(dst, src).then_inc(first_in, 16)

            def load_rest():
                for dst, src in loads:
                    sp.dma_start(dst, src, allow_slow_non_contiguous=True).then_inc(weights_in, 16)
                sp.wait_ge(consts_done, 1)
                sp.dma_start(slot_x.rearrange("(e p) d -> p e d", p=P), XD[:, :, :]).then_inc(slots_zeroed, 16)
                sp.wait_ge(slots_zeroed, 16)

            def part(what, b, c=None, a=None, d=None):
                if what == "setup_rest":
                    load_rest()
                elif what == "load_x":
                    need_rows(sp, "yA_done", b)
                    sp.dma_start(X[:, :, :],
                                 x_in[bass.ds(b, 1), :, :].rearrange("o (k p) d -> p (o k) d", p=P))\
                        .then_inc(sems["x_loaded"], 16)
                elif what == "d_slots":
                    sp.wait_ge(sems["scattered"], raised("scattered", b, 16 * NT))
                    sp.dma_start(XD[:, :, :], slot_x.rearrange("(e p) d -> p e d", p=P))\
                        .then_inc(sems["slots_loaded"], 16)
                elif what == "d_ffn":
                    sp.wait_ge(sems["yD_done"], raised("yD_done", b, 2))
                    sp.dma_start(slot_y.rearrange("(e p) d -> p e d", p=P), YD[:, :, :])\
                        .then_inc(sems["slots_stored"], 16)
                elif what == "mix_and_scan" and d is not None:
                    sp.wait_ge(sems["x4_done"], raised("x4_done", d, 1))
                    sp.dma_start(out[bass.ds(d, 1), :, :].rearrange("o (k p) d -> p (o k) d", p=P),
                                 YD[:, :, :]).then_inc(sems["out_stored"], 16)

            schedule(sp, part)
            sp.wait_ge(sems["out_stored"], 16 * NB)

        @block.gpsimd
        def _(pool):
            g = nc.gpsimd
            n = 0

            def const(ins):
                nonlocal n
                n += 1
                ins.then_inc(consts_done, 1)
                pool.wait_ge(consts_done, n)

            const(g.memset(XD[:, :, :], 0.0))
            const(g.memset(ident[:, :], 0.0))
            const(g.affine_select(out=ident[:, :], in_=ident[:, :], compare_op=ALU.not_equal, fill=1.0,
                                  base=0, pattern=[[-1, P]], channel_multiplier=1))
            const(g.tensor_copy(identb[:, :], ident[:, :]))
            const(g.memset(onesb[:, :], 1.0))
            const(g.affine_select(out=before[:, :], in_=onesb[:, :], compare_op=ALU.is_gt, fill=0.0,
                                  base=0, pattern=[[1, P]], channel_multiplier=-1))
            for tile, count in ((sel_gate, E), (sel_bs, NS)):
                const(g.memset(tile[:, :, :], 0.0))
                for p3 in range(3):
                    const(g.affine_select(out=tile[:, :, :], in_=tile[:, :, :], compare_op=ALU.not_equal,
                                          fill=1.0, base=-p3 * count, pattern=[[-1, count], [0, P]],
                                          channel_multiplier=1))
            const(g.iota(first[:, :], pattern=[[-1, E]], base=E, channel_multiplier=0,
                         allow_small_or_imprecise_dtypes=True))
            const(g.iota(base128[:, :], pattern=[[CAP, E]], base=0, channel_multiplier=0,
                         allow_small_or_imprecise_dtypes=True))
            const(g.memset(XS[:, :, 0:TAPS - 1], 0.0))
            assert n == CONSTS
            pool.wait_ge(first_in, 16 * N_FIRST)

            def add_state(c, k, shared=False):
                d, n_ = k // NS, k % NS
                if n_ == 0 or on_pe(k, shared):
                    return
                pool.wait_ge(sems["scan_done"], raised("scan_done", c, k + 1))
                if n_ == 1:
                    first = HS[:, (k - 1) % N_H, :]
                else:
                    pool.wait_ge(sems["y_sum_done"], raised("y_sum_done", c, pool_adds(k, shared) - 1))
                    first = YX[:, d, :]
                g.tensor_tensor(out=YX[:, d, :], in0=first, in1=HS[:, k % N_H, :], op=ALU.add)\
                    .then_inc(sems["y_sum_done"], 1)

            def part(what, b, c=None, a=None, d=None):
                if what == "mix_and_scan" and c is not None:
                    for k in range(LEAD, NK):
                        add_state(c, k, b is None)
                elif what == "scan_ahead":
                    for k in c:
                        add_state(b, k)
                elif what == "c_delta":
                    d = c
                    pool.wait_ge(sems["sp_done"], raised("sp_done", b, d + 1))
                    pool.wait_ge(sems["vrel_done"], raised("vrel_done", b, NC_ * (d + 1)))
                    g.tensor_tensor(out=DT[:, d, :], in0=DT[:, d, :], in1=SP_[:, d, :], op=ALU.add)\
                        .then_inc(sems["dt_done"], 1)
                elif what == "d_slots":
                    pool.wait_ge(sems["put_done"], raised("put_done", b, 1))
                    g.tensor_tensor(out=held_p[:, 0:1], in0=bias_bc[:, 0:1], in1=bias_bc[:, 0:1], op=ALU.add)
                    for t in range(NT):
                        g.indirect_dma_start(
                            out=slot_x, out_offset=bass.IndirectOffsetOnAxis(ap=put_i[:, t:t + 1], axis=0),
                            in_=X3[:, t, :], in_offset=None, bounds_check=SLOTS - 1, oob_is_err=False)\
                            .then_inc(sems["scattered"], 16)
                elif what == "d_ffn":
                    pool.wait_ge(sems["slots_stored"], raised("slots_stored", b, 16))
                    pool.wait_ge(sems["get_done"], raised("get_done", b, 1))
                    g.tensor_tensor(out=held_p[:, 1:2], in0=bias_bc[:, 0:1], in1=bias_bc[:, 0:1], op=ALU.add)
                    for t in range(NT):
                        g.indirect_dma_start(
                            out=XD[:, t, :], out_offset=None, in_=slot_y,
                            in_offset=bass.IndirectOffsetOnAxis(ap=get_i[:, t:t + 1], axis=0))\
                            .then_inc(sems["gathered"], 16)

            schedule(pool, part)

        @block.scalar
        def _(act):
            s = nc.scalar
            LOG_EXP = "natural_log_exp_and_others"

            def inv_root(dst, tmp, src, scale, bias, out_bias, step, b, k):
                s.activation(tmp, src, ACT.Ln, bias=bias, scale=scale).then_inc(sems[step], 1)
                act.wait_ge(sems[step], raised(step, b, k))
                return s.activation(dst, tmp, ACT.Exp, bias=out_bias, scale=-0.5)

            s.preload_act_table_set(LOG_EXP)
            act.wait_ge(first_in, 16 * N_FIRST)
            act.wait_ge(consts_done, CONSTS)
            s.activation(SQ[:, 0:NI, :], kn[:, :, :], ACT.Square).then_inc(setup_a, 1)
            act.wait_ge(setup_v, 3)
            s.activation(ln2[:, 0:NI], n2[:, 0:NI], ACT.Ln, scale=N2_SCALE).then_inc(setup_a, 1)
            act.wait_ge(setup_a, 2)
            s.activation(rn[:, 0:NI], ln2[:, 0:NI], ACT.Exp, bias=rnb[:, 0:1], scale=-0.5).then_inc(setup_a, 1)
            act.wait_ge(setup_pe, 1)
            s.activation(knT[:, :], PS[:, 6, :], ACT.Copy).then_inc(setup_a, 1)

            def rstd(small, block_name, b, k, eps, step_k):
                act.wait_ge(sems[f"mv{block_name}_done"], raised(f"mv{block_name}_done", b, k))
                inv_root(small["rstd"][:, :], small["lnv"][:, :], small["mv"][:, :, 1], 1.0, eps[:, 0:1], 0.0,
                         f"a{block_name}", b, step_k).then_inc(sems[f"rstd{block_name}_done"], 1)

            def norm_out(small, dst, src, block_name, b, n, done):
                act.wait_ge(sems[f"nmr{block_name}_done"], raised(f"nmr{block_name}_done", b, 1))
                for t in range(2 * n, 2 * n + 2) if n is not None else range(NT):
                    ins = s.activation(dst[:, t, :], src[:, t, :], ACT.Identity,
                                       bias=small["nmr"][:, t:t + 1], scale=small["rstd"][:, t:t + 1])
                if n is None or n == 3:
                    ins.then_inc(sems[done], 1)

            def copy_turned(dst, bank, b, ps_name, done):
                for c in range(NC_):
                    act.wait_ge(sems[ps_name], raised(ps_name, b, c + 1))
                    s.activation(dst[:, c * CH:(c + 1) * CH], PS[:, bank + c, :], ACT.Copy)\
                        .then_inc(sems[done], 1)

            def decay(c, k):
                d, n_ = k // NS, k % NS
                if n_ == 0:
                    act.wait_ge(sems["dt_done"], raised("dt_done", c, d + 1))
                if k >= N_A:
                    act.wait_ge(sems["scan_done"], raised("scan_done", c, k - N_A + 1))
                s.activation(dA[:, k % N_A, :], DT[:, d, :], ACT.Exp, scale=nega[:, d, n_:n_ + 1])\
                    .then_inc(sems["dA_done"], 1)

            def part(what, b, c=None, a=None, d=None):
                if what == "setup_rest_done":
                    act.wait_ge(weights_in, W_ALL)
                    s.activation(nega[:, :, :], nega[:, :, :], ACT.Exp).then_inc(setup_a, 1)
                elif what == "mix_and_scan":
                    if c is not None:
                        act.wait_ge(sems["dt_done"], raised("dt_done", c, ND))
                    for j in range(NJ):
                        if b is not None:
                            e, f = j // NFB % E, j % NFB
                            act.wait_ge(sems["z_ps_done"], raised("z_ps_done", b, j + 1))
                            if j >= 2:
                                act.wait_ge(sems["hg_done"], raised("hg_done", b, j - 1))
                            s.activation(HR[:, j % 2, :], PS[:, Z0 + j % 2, :], ACT.Relu,
                                         bias=b1_s[:, e, f:f + 1]).then_inc(sems["relu_done"], 1)
                            if j == E * NFB + 1:
                                copy_acc(b, 0)
                        if c is not None:
                            for k in scans_beside(j):
                                if k + 2 < NK:
                                    decay(c, k + 2)
                        if c is not None and j == RESIDUAL_AT:
                            need_rows(act, "out_stored", c)
                            s.activation(Y2[:, :, :], X2[:, :, :], ACT.Copy).then_inc(sems["x2_kept"], 1)
                        if d is not None and j == D_AT + 8:
                            rstd(S2, "D", d, 1, eps_l, 1)
                        if a is not None and j == A_AT + 4:
                            rstd(S1, "A", a, 1, eps_a, 1)
                        if d is not None and 0 <= j - D_AT - 10 < 4:
                            norm_out(S2, YD, Y2, "D", d, j - D_AT - 10, "x4_done")
                        if a is not None and 0 <= j - A_AT - 6 < 4:
                            norm_out(S1, XL, X, "A", a, j - A_AT - 6, "xh_done")
                        if a is not None and j == A_AT + 16:
                            act.wait_ge(sems["xln_done"], raised("xln_done", a, 1))
                            s.activation(SQA, XL[:, :, :], ACT.Square).then_inc(sems["sqA_done"], 1)
                        if a is not None and j == A_AT + 18:
                            act.wait_ge(sems["n2_done"], raised("n2_done", a, 1))
                            inv_root(rn[:, :], ln2[:, :], n2[:, :], N2_SCALE, 0.0, rnb[:, 0:1], "aA", a, 2)\
                                .then_inc(sems["rn_done"], 1)
                    if b is not None:
                        copy_acc(b, 1)
                elif what == "scan_ahead":
                    if c.start == 0:
                        decay(b, 0)
                        decay(b, 1)
                    for k in c:
                        decay(b, k + 2)
                elif what == "log_exp_table":
                    s.preload_act_table_set(LOG_EXP)
                elif what == "c_norm" and c == 1:
                    rstd(S2, "C", b, 1, eps_l, 3)
                elif what == "c_norm" and c == 2:
                    norm_out(S2, X3, Y2, "C", b, None, "x3_done")
                elif what == "b_out" and c == 1:
                    rstd(S1, "B", b, 1, eps_l, 1)
                elif what == "a_turn":
                    copy_turned(XT1, 2, b, "qT_ps_done", "qT_done")
                elif what == "a_logs":
                    h = c
                    act.wait_ge(sems["clip_done"], raised("clip_done", b, 2 * (h + 1)))
                    s.activation(L1[:, h], SC[:, h], ACT.Ln, bias=1.0)
                    s.activation(L2[:, h], SC[:, h], ACT.Ln, bias=1.0, scale=-1.0)\
                        .then_inc(sems["logs_done"], 1)
                elif what == "a_angle":
                    s.preload_act_table_set("sigmoid_and_others")
                    for h in range(NC_):
                        act.wait_ge(sems["dlog_done"], raised("dlog_done", b, h + 1))
                        s.activation(L2[:, h], L1[:, h], ACT.Tanh, scale=0.25).then_inc(sems["aA"], 1)
                        act.wait_ge(sems["aA"], raised("aA", b, 3 + 2 * h))
                        s.activation(SC[:, h], L2[:, h], ACT.Arctan).then_inc(sems["atan_done"], 1)
                        act.wait_ge(sems["atan_done"], raised("atan_done", b, h + 1))
                        s.activation(L1[:, h], SC[:, h], ACT.Square, bias=t2_bias[:, 0:1], scale=T2_SCALE)\
                            .then_inc(sems["aA"], 1)
                        if h == 0:
                            act.wait_ge(sems["aA"], raised("aA", b, 4))
                            s.activation(L2[:, h], L1[:, h], ACT.Square).then_inc(sems["t4_done"], 1)
                elif what == "a_out" and c == 0:
                    for h in range(NC_):
                        act.wait_ge(sems["xo_ps_done"], raised("xo_ps_done", b, h + 1))
                        s.activation(flat(SQ[:, TPC * h:TPC * (h + 1), :]), PS[:, 2 + h, :], ACT.Square)\
                            .then_inc(sems["sqX_done"], 1)
                    act.wait_ge(sems["n2_done"], raised("n2_done", b, 2))
                    inv_root(rn[:, :], ln2[:, :], n2[:, :], N2_SCALE, 0.0, rnb[:, 0:1], "aA", b, 7)\
                        .then_inc(sems["rn_done"], 1)
                elif what == "a_out":
                    rstd(S1, "A", b, 2, eps_l, 8)
                elif what == "b_turn":
                    copy_turned(XT1, 0, b, "x1T_ps_done", "x1T_done")
                elif what == "b_route" and c == 0:
                    act.wait_ge(sems["mB_done"], raised("mB_done", b, 1))
                    s.activation(S1["w2"][:, :], S1["pos"][:, :], ACT.Exp).then_inc(sems["exB_done"], 1)
                elif what == "b_route":
                    act.wait_ge(sems["g3T_ps_done"], raised("g3T_ps_done", b, 1))
                    s.activation(g3T[:, :], g3T_ps[0:3 * E, :], ACT.Copy).then_inc(sems["g3T_done"], 1)
                elif what == "c_turn":
                    copy_turned(XT2, 6, b, "x2T_ps_done", "x2T_done")
                elif what == "c_conv":
                    for k in range(2 * NC_):
                        act.wait_ge(sems["z_in_ps_done"], raised("z_in_ps_done", b, k + 1))
                        s.activation(ZS[:, k // NC_, k % NC_ * CH:(k % NC_ + 1) * CH],
                                     PS[:, in_bank(k), :], ACT.Copy)\
                            .then_inc(sems["zs_done"], 1)
                elif what == "c_silu":
                    act.wait_ge(sems["zs_done"], raised("zs_done", b, 4))
                    s.activation(ZS[:, :, :], ZS[:, :, :], ACT.Silu).then_inc(sems["silz_done"], 1)
                    for d in range(ND):
                        act.wait_ge(sems["conv_done"], raised("conv_done", b, d + 1))
                        s.activation(XA[:, d, :], XA[:, d, :], ACT.Silu).then_inc(sems["xa_done"], 1)
                elif what == "c_delta":
                    d = c
                    for h in range(NC_):
                        k = NC_ * d + h
                        act.wait_ge(sems["dt_ps_done"], raised("dt_ps_done", b, k + 1))
                        s.activation(SP_[:, d, h * CH:(h + 1) * CH], PS[:, 4 + k, :], ACT.Abs,
                                     bias=bdt_s[:, d:d + 1]).then_inc(sems["abs_done"], 1)
                    act.wait_ge(sems["abs_done"], raised("abs_done", b, NC_ * (d + 1)))
                    s.activation(SP_[:, d, :], SP_[:, d, :], ACT.Exp, scale=-1.0).then_inc(sems["aC"], 1)
                    act.wait_ge(sems["aC"], raised("aC", b, d + 1))
                    s.activation(SP_[:, d, :], SP_[:, d, :], ACT.Ln, bias=1.0).then_inc(sems["sp_done"], 1)
                    if d == ND - 1:
                        act.wait_ge(sems["bs3T_ps_done"], raised("bs3T_ps_done", b, 1))
                        s.activation(bs3T[:, :], bs3T_ps[0:3 * NS, :], ACT.Copy).then_inc(sems["bs3T_done"], 1)
                elif what == "d_turn":
                    copy_turned(XT3, 4, b, "x3T_ps_done", "x3T_done")
                elif what == "d_gate":
                    act.wait_ge(sems["mD_done"], raised("mD_done", b, 1))
                    s.activation(S2["ex"][:, :, :], S2["lg"][:, :, :], ACT.Exp).then_inc(sems["exD_done"], 1)
                elif what == "d_slots_turn":
                    for h in range(2):
                        act.wait_ge(sems["xdT_ps_done"], raised("xdT_ps_done", b, h + 1))
                        s.activation(XDT[:, h * CH:(h + 1) * CH], PS[:, 4 + h, :], ACT.Copy)\
                            .then_inc(sems["xdT_done"], 1)
                elif what == "d_ffn":
                    for e in range(E):
                        act.wait_ge(sems["g_ps_done"], raised("g_ps_done", b, e + 1))
                        if e >= 2:
                            act.wait_ge(sems["yD_ps_done"], raised("yD_ps_done", b, e - 1))
                        s.activation(GE[:, e % 2].rearrange("p a b -> p (a b)"), PS[:, 6 + e % 2, :],
                                     ACT.Gelu_apprx_tanh).then_inc(sems["gelu_done"], 1)
                    for h in range(2):
                        act.wait_ge(sems["yD_ps_done"], raised("yD_ps_done", b, TPC * (h + 1)))
                        s.activation(flat(YD[:, TPC * h:TPC * (h + 1), :]), PS[:, 4 + h, :], ACT.Copy)\
                            .then_inc(sems["yD_done"], 1)

            def copy_acc(b, h):
                act.wait_ge(sems["oB_acc_done"], raised("oB_acc_done", b, E * NFB * (h + 1)))
                s.activation(OT[:, h, :], PS[:, ACC, :], ACT.Copy).then_inc(sems["oT_done"], 1)

            schedule(act, part)

        @block.vector
        def _(dve):
            v = nc.vector
            count = {}

            def step(ins, name, b):
                count[name] = count.get(name, 0) + 1
                ins.then_inc(sems[name], 1)
                dve.wait_ge(sems[name], raised(name, b, count[name]))

            def norm_in(small, src, block_name, b, tiles=range(NT)):
                for t in tiles:
                    ins = v.bn_stats(small["bst"][:, t, :], src[:, t, :])
                if tiles.stop < NT:
                    return
                step(ins, "v" + block_name, b)
                v.memset(held[:, :], 0.0)
                for t in range(NT):
                    ins = v.bn_aggr(small["mv"][:, t, :], small["bst"][:, t, :])
                ins.then_inc(sems[f"mv{block_name}_done"], 1)

            def norm_out(small, dst, src, block_name, b, k, done, tiles=range(NT)):
                dve.wait_ge(sems[f"rstd{block_name}_done"], raised(f"rstd{block_name}_done", b, k))
                for t in tiles:
                    ins = v.tensor_scalar(dst[:, t, :], src[:, t, :], small["mv"][:, t, 0:1],
                                          small["rstd"][:, t:t + 1], ALU.subtract, ALU.mult)
                if tiles.stop == NT:
                    ins.then_inc(sems[done], 1)

            def largest(S, mx, name, b):
                step(v.tensor_reduce(mx[:, :], S["lg"][:, :, :], AX, ALU.max), name, b)

            def first_place(S, mx, oh, name, b):
                step(v.tensor_tensor(out=S["t8a"][:, :, :], in0=S["lg"][:, :, :], in1=per_tile(mx), op=ALU.is_equal),
                     name, b)
                step(v.tensor_tensor(out=S["t8b"][:, :, :], in0=S["t8a"][:, :, :], in1=per_token(first, E),
                                     op=ALU.mult), name, b)
                step(v.tensor_reduce(S["ms"][:, :], S["t8b"][:, :, :], AX, ALU.max), name, b)
                step(v.tensor_tensor(out=oh[:, :, :], in0=S["t8b"][:, :, :], in1=per_tile(S["ms"]), op=ALU.is_equal),
                     name, b)

            def split3(dst, rest, src, name, b):
                step(v.tensor_copy(dst[0], src), name, b)
                step(v.tensor_tensor(out=rest, in0=src, in1=dst[0], op=ALU.subtract), name, b)
                step(v.tensor_copy(dst[1], rest), name, b)
                step(v.tensor_tensor(out=rest, in0=rest, in1=dst[1], op=ALU.subtract), name, b)
                return v.tensor_copy(dst[2], rest)

            v.memset(eps_a[:, :], 1e-12)
            v.memset(eps_l[:, :], 1e-5)
            v.memset(t2_bias[:, :], T2_BIAS)
            v.memset(rnb[:, :], RN_BIAS).then_inc(setup_v, 1)
            dve.wait_ge(setup_a, 1)
            v.tensor_reduce(ms[:, 0:NI], SQ[:, 0:NI, :], AX, ALU.add).then_inc(setup_v, 1)
            dve.wait_ge(setup_v, 2)
            v.tensor_scalar(n2[:, 0:NI], ms[:, 0:NI], 1e-24, None, ALU.max).then_inc(setup_v, 1)
            dve.wait_ge(setup_a, 3)
            dve.wait_ge(consts_done, CONSTS)
            for i in range(NI):
                ins = v.tensor_scalar(kn[:, i, :], kn[:, i, :], rn[:, i:i + 1], None, ALU.mult)
            ins.then_inc(setup_v, 1)

            def setup_rest():
                dve.wait_ge(setup_a, 5)
                v.tensor_scalar(nega[:, :, :], nega[:, :, :], -1.0, None, ALU.mult)
                parts = [b2_p[:, i, :] for i in range(3)]
                v.tensor_copy(parts[0], b2_f[:, :]).then_inc(setup_v, 1)
                dve.wait_ge(setup_v, 5)
                v.tensor_tensor(out=b2_r[:, :], in0=b2_f[:, :], in1=parts[0], op=ALU.subtract).then_inc(setup_v, 1)
                dve.wait_ge(setup_v, 6)
                v.tensor_copy(parts[1], b2_r[:, :]).then_inc(setup_v, 1)
                dve.wait_ge(setup_v, 7)
                v.tensor_tensor(out=b2_r[:, :], in0=b2_r[:, :], in1=parts[1], op=ALU.subtract).then_inc(setup_v, 1)
                dve.wait_ge(setup_v, 8)
                v.tensor_copy(parts[2], b2_r[:, :]).then_inc(setup_v, 1)

            def skip(c, d, shared):
                dve.wait_ge(sems["y_sum_done"], raised("y_sum_done", c, pool_adds(NS * d + NS - 1, shared)))
                ins = v.scalar_tensor_tensor(out=YX[:, d, :], in0=XA[:, d, :], scalar=dsk[:, d:d + 1],
                                             in1=YX[:, d, :], op0=ALU.mult, op1=ALU.add)
                if shared:
                    ins.then_inc(setup_v, 1)
                    dve.wait_ge(setup_v, 10 + d)
                    dve.wait_ge(pe_sum_done, pe_adds(NS * d + NS - 1))
                    ins = v.tensor_tensor(out=YX[:, d, :], in0=YX[:, d, :], in1=flat(PS[:, 2 * d:2 * d + 2, :]),
                                          op=ALU.add)
                ins.then_inc(sems["yx_done"], 1)

            def gate_z(c, d):
                dve.wait_ge(sems["yx_done"], raised("yx_done", c, d + 1))
                v.tensor_tensor(out=YX[:, d, :], in0=YX[:, d, :], in1=ZS[:, d, :], op=ALU.mult)\
                    .then_inc(sems["yz_done"], 1)

            def scan(c, k, shared=False):
                if k < NK:
                    dve.wait_ge(sems["dA_done"], raised("dA_done", c, k + 1))
                    dve.wait_ge(sems["spread_done"], raised("spread_done", c, k + 1))
                    if k >= N_H:
                        if on_pe(k - N_H, shared):
                            dve.wait_ge(pe_sum_done, pe_adds(k - N_H))
                        else:
                            dve.wait_ge(sems["y_sum_done"], raised("y_sum_done", c, pool_adds(k - N_H, shared)))
                    bank = SPR + 2 * (k % 2)
                    v.tensor_tensor_scan(HS[:, k % N_H, :], dA[:, k % N_A, :],
                                         flat(PS[:, bank:bank + 2, :]), 0.0, ALU.mult, ALU.add)\
                        .then_inc(sems["scan_done"], 1)
                if k == NS + NS // 2:
                    skip(c, 0, shared)
                    gate_z(c, 0)

            def minus_mean(small, block_name, b):
                dve.wait_ge(sems[f"rstd{block_name}_done"], raised(f"rstd{block_name}_done", b, 1))
                v.scalar_tensor_tensor(out=small["nmr"][:, :], in0=small["mv"][:, :, 0], scalar=-1.0,
                                       in1=small["rstd"][:, :], op0=ALU.mult, op1=ALU.mult)\
                    .then_inc(sems[f"nmr{block_name}_done"], 1)

            def d_out(d, n):
                if n < 4:
                    dve.wait_ge(sems["gathered"], raised("gathered", d, 16 * NT))
                    for t in range(2 * n, 2 * n + 2):
                        ins = v.scalar_tensor_tensor(out=Y2[:, t, :], in0=XD[:, t, :],
                                                     scalar=S2["gk"][:, t:t + 1],
                                                     in1=X3[:, t, :], op0=ALU.mult, op1=ALU.add)
                    if n == 3:
                        ins.then_inc(sems["yF_done"], 1)
                elif n < 8:
                    dve.wait_ge(sems["yF_done"], raised("yF_done", d, 1))
                    norm_in(S2, Y2, "D", d, range(2 * n - 8, 2 * n - 6))
                elif n == 9:
                    minus_mean(S2, "D", d)

            def a_norm(a, n):
                if n < 4:
                    dve.wait_ge(sems["x_loaded"], raised("x_loaded", a, 16))
                    norm_in(S1, X, "A", a, range(2 * n, 2 * n + 2))
                elif n == 5:
                    minus_mean(S1, "A", a)
                elif n in (11, 12, 13, 14):
                    dve.wait_ge(sems["xh_done"], raised("xh_done", a, 1))
                    h, row = n % 2, lnw_bc if n < 13 else lnb_bc
                    if n == 13:
                        dve.wait_ge(sems["xw_done"], raised("xw_done", a, 1))
                    x = XL[:, TPC * (1 - h):TPC * (2 - h), :]
                    ins = v.tensor_tensor(out=x, in0=x, in1=row[:, :].unsqueeze(1).to_broadcast([P, TPC, H]),
                                          op=ALU.mult if n < 13 else ALU.add)
                    if h == 0:
                        ins.then_inc(sems["xw_done" if n < 13 else "xln_done"], 1)
                elif n in (15, 16):
                    x = X[:, TPC * (n - 15):TPC * (n - 14), :]
                    v.tensor_tensor(out=x, in0=x, in1=bias_bc[:, :].unsqueeze(1).to_broadcast([P, TPC, H]),
                                    op=ALU.add).then_inc(sems["xbias_done"], 1)
                elif n == 17:
                    dve.wait_ge(sems["sqA_done"], raised("sqA_done", a, 1))
                    step(v.tensor_reduce(ms[:, :], SQA, AX, ALU.add), "vA", a)
                    v.tensor_scalar(n2[:, :], ms[:, :], 1e-24, None, ALU.max).then_inc(sems["n2_done"], 1)
                elif 19 <= n < 23:
                    dve.wait_ge(sems["rn_done"], raised("rn_done", a, 1))
                    for t in range(2 * n - 38, 2 * n - 36):
                        ins = v.tensor_scalar(XL[:, t, :], XL[:, t, :], rn[:, t:t + 1], None, ALU.mult)
                    if n == 22:
                        ins.then_inc(sems["qn_done"], 1)

            def part(what, b, c=None, a=None, d=None):
                if what == "setup_rest_done":
                    setup_rest()
                elif what == "mix_and_scan":
                    for j in range(NJ):
                        if c is not None:
                            scan(c, scans_beside(j)[0], b is None)
                        if b is not None:
                            dve.wait_ge(sems["gate_ps_done"], raised("gate_ps_done", b, j // NFB + 1))
                            dve.wait_ge(sems["relu_done"], raised("relu_done", b, j + 1))
                            if j >= 3:
                                dve.wait_ge(sems["oB_acc_done"], raised("oB_acc_done", b, j - 2))
                            v.tensor_tensor(out=HG[:, j % 3, :], in0=HR[:, j % 2, :], in1=PS[:, GATE, :],
                                            op=ALU.mult).then_inc(sems["hg_done"], 1)
                        if c is not None:
                            for k in scans_beside(j)[1:]:
                                scan(c, k, b is None)
                            if j == NJ - 1:
                                skip(c, ND - 1, b is None)
                                gate_z(c, ND - 1)
                        if d is not None and j >= D_AT:
                            d_out(d, j - D_AT)
                        if a is not None and j >= A_AT:
                            a_norm(a, j - A_AT)
                    if d is not None:
                        assert count.pop("vD") == per["vD"]
                elif what == "scan_ahead":
                    for k in c:
                        scan(b, k)
                elif what == "c_norm" and c == 0:
                    dve.wait_ge(sems["x2_kept"], raised("x2_kept", b, 1))
                    for h in range(NC_):
                        dve.wait_ge(sems["oC_ps_done"], raised("oC_ps_done", b, h + 1))
                        y = flat(Y2[:, TPC * h:TPC * (h + 1), :])
                        ins = v.tensor_tensor(out=y, in0=PS[:, 6 + h, :], in1=y, op=ALU.add)
                    ins.then_inc(sems["yC_done"], 1)
                elif what == "c_norm" and c == 1:
                    dve.wait_ge(sems["yC_done"], raised("yC_done", b, 1))
                    norm_in(S2, Y2, "C", b)
                elif what == "c_norm":
                    minus_mean(S2, "C", b)
                    assert count.pop("vC") == per["vC"]
                elif what == "b_out" and c == 0:
                    for h in range(NC_):
                        dve.wait_ge(sems["oB_ps_done"], raised("oB_ps_done", b, h + 1))
                        x = flat(X1[:, TPC * h:TPC * (h + 1), :])
                        ins = v.tensor_tensor(out=x, in0=PS[:, h, :], in1=x, op=ALU.add)
                    ins.then_inc(sems["yB_done"], 1)
                elif what == "b_out" and c == 1:
                    dve.wait_ge(sems["yB_done"], raised("yB_done", b, 1))
                    norm_in(S1, X1, "B", b)
                elif what == "b_out":
                    norm_out(S1, X2, X1, "B", b, 1, "x2_done")
                    assert count.pop("vB") == per["vB"]
                elif what == "a_scores":
                    h = c
                    for u in (2 * h, 2 * h + 1):
                        i2, bank = 2 * (u % 2), 2 - 2 * (u % 2)
                        dve.wait_ge(sems["s_ps_done"], raised("s_ps_done", b, u + 1))
                        v.tensor_scalar(SC[:, h, i2:i2 + 2, :], PS[:, bank:bank + 2, :], S_MAX, -S_MAX,
                                        ALU.min, ALU.max).then_inc(sems["clip_done"], 1)
                elif what == "a_logs":
                    h = c
                    dve.wait_ge(sems["logs_done"], raised("logs_done", b, h + 1))
                    v.tensor_tensor(out=L1[:, h], in0=L1[:, h], in1=L2[:, h], op=ALU.subtract)\
                        .then_inc(sems["dlog_done"], 1)
                elif what == "a_mix":
                    for h in (c,):
                        if h == 0:
                            dve.wait_ge(sems["t4_done"], raised("t4_done", b, 1))
                        else:
                            dve.wait_ge(sems["aA"], raised("aA", b, 6))
                            step(v.tensor_tensor(out=L2[:, h], in0=L1[:, h], in1=L1[:, h], op=ALU.mult), "vA", b)
                        step(v.tensor_tensor(out=L2[:, h], in0=L2[:, h], in1=L2[:, h], op=ALU.mult), "vA", b)
                        v.scalar_tensor_tensor(out=L1[:, h], in0=SC[:, h], scalar=math.pi / 4, in1=L2[:, h],
                                               op0=ALU.add, op1=ALU.mult).then_inc(sems["bpow_done"], 1)
                elif what == "a_out" and c == 0:
                    for h in range(NC_):
                        dve.wait_ge(sems["sqX_done"], raised("sqX_done", b, h + 1))
                        ins = v.tensor_reduce(ms[:, TPC * h:TPC * (h + 1)], SQ[:, TPC * h:TPC * (h + 1), :],
                                              AX, ALU.add)
                    step(ins, "vA", b)
                    v.tensor_scalar(n2[:, :], ms[:, :], 1e-24, None, ALU.max).then_inc(sems["n2_done"], 1)
                    dve.wait_ge(sems["rn_done"], raised("rn_done", b, 2))
                    dve.wait_ge(sems["xbias_done"], raised("xbias_done", b, 2))
                    for t in range(NT):
                        h, r = t // TPC, t % TPC
                        ins = v.scalar_tensor_tensor(out=XL[:, t, :], in0=PS[:, 2 + h, r * P:(r + 1) * P],
                                                     scalar=rn[:, t:t + 1], in1=X[:, t, :],
                                                     op0=ALU.mult, op1=ALU.add)
                    ins.then_inc(sems["yA_done"], 1)
                    dve.wait_ge(sems["yA_done"], raised("yA_done", b, 1))
                    norm_in(S1, XL, "A", b)
                elif what == "a_out":
                    norm_out(S1, X1, XL, "A", b, 2, "x1_done")
                    assert count.pop("vA") == per["vA"]
                elif what == "b_route" and c == 0:
                    S, m = S1, "vB"
                    dve.wait_ge(sems["lgB_ps_done"], raised("lgB_ps_done", b, 1))
                    step(v.tensor_tensor(out=S["lg"][:, :, :],
                                         in0=PS[:, 2, 0:NT * E].rearrange("p (t e) -> p t e", e=E),
                                         in1=per_token(br_bc, E), op=ALU.add), m, b)
                    largest(S, S["m1"], m, b)
                    first_place(S, S["m1"], S["oh1"], m, b)
                    step(v.scalar_tensor_tensor(out=S["lg"][:, :, :], in0=S["oh1"][:, :, :], scalar=-3.0e38,
                                                in1=S["lg"][:, :, :], op0=ALU.mult, op1=ALU.add), m, b)
                    largest(S, S["m2"], m, b)
                    v.tensor_tensor(out=S["pos"][:, :], in0=S["m2"][:, :], in1=S["m1"][:, :], op=ALU.subtract)\
                        .then_inc(sems["mB_done"], 1)
                    first_place(S, S["m2"], S["oh2"], m, b)
                elif what == "b_route":
                    S, m = S1, "vB"
                    dve.wait_ge(sems["exB_done"], raised("exB_done", b, 1))
                    step(v.tensor_scalar(S["w1"][:, :], S["w2"][:, :], 1.0, None, ALU.add), m, b)
                    step(v.reciprocal(S["w1"][:, :], S["w1"][:, :]), m, b)
                    step(v.tensor_tensor(out=S["w2"][:, :], in0=S["w2"][:, :], in1=S["w1"][:, :], op=ALU.mult), m, b)
                    v.tensor_tensor(out=S["t8a"][:, :, :], in0=S["oh1"][:, :, :], in1=per_tile(S["w1"]), op=ALU.mult)
                    step(v.tensor_tensor(out=S["t8b"][:, :, :], in0=S["oh2"][:, :, :], in1=per_tile(S["w2"]),
                                         op=ALU.mult), m, b)
                    step(v.tensor_tensor(out=S["t8a"][:, :, :], in0=S["t8a"][:, :, :], in1=S["t8b"][:, :, :],
                                         op=ALU.add), m, b)
                    split3([g3[:, :, i, :] for i in range(3)], S["t8b"][:, :, :], S["t8a"][:, :, :], m, b)\
                        .then_inc(sems["g3_done"], 1)
                elif what == "c_in":
                    for d in range(ND):
                        for h in range(NC_):
                            dve.wait_ge(sems["xs_ps_done"], raised("xs_ps_done", b, NC_ * d + h + 1))
                            v.tensor_copy(XS[:, d, TAPS - 1 + h * CH:TAPS - 1 + (h + 1) * CH],
                                          PS[:, in_bank(NC_ * d + h), :]).then_inc(sems["xs_done"], 1)
                elif what == "c_conv":
                    for d in range(ND):
                        dve.wait_ge(sems["xs_done"], raised("xs_done", b, ND * NC_))
                        step(v.tensor_scalar(XA[:, d, :], XS[:, d, 0:T], cw_s[:, d, 0:1], cb_s[:, d:d + 1],
                                             ALU.mult, ALU.add), "vC", b)
                        for k in range(1, TAPS):
                            ins = v.scalar_tensor_tensor(out=XA[:, d, :], in0=XS[:, d, k:k + T],
                                                         scalar=cw_s[:, d, k:k + 1], in1=XA[:, d, :],
                                                         op0=ALU.mult, op1=ALU.add)
                            if k < TAPS - 1:
                                step(ins, "vC", b)
                            else:
                                ins.then_inc(sems["conv_done"], 1)
                elif what == "c_delta":
                    d = c
                    for h in range(NC_):
                        k = NC_ * d + h
                        dve.wait_ge(sems["abs_done"], raised("abs_done", b, k + 1))
                        v.tensor_scalar(DT[:, d, h * CH:(h + 1) * CH], PS[:, 4 + k, :], bdt_s[:, d:d + 1],
                                        0.0, ALU.add, ALU.max).then_inc(sems["vrel_done"], 1)
                    if d == ND - 1:
                        dve.wait_ge(sems["bs_ps_done"], raised("bs_ps_done", b, 1))
                        step(v.tensor_copy(bsr[:, :, :],
                                           PS[:, 4, 0:NT * NS].rearrange("p (t n) -> p t n", n=NS)), "vC", b)
                        split3([bs3[:, :, i, :] for i in range(3)], bsr[:, :, :], bsr[:, :, :], "vC", b)\
                            .then_inc(sems["bs3_done"], 1)
                elif what == "d_route":
                    S, m = S2, "vD"
                    dve.wait_ge(sems["lgD_ps_done"], raised("lgD_ps_done", b, 1))
                    step(v.tensor_copy(S["lg"][:, :, :], PS[:, 4, 0:NT * E].rearrange("p (t e) -> p t e", e=E)), m, b)
                    largest(S, S["m1"], m, b)
                    first_place(S, S["m1"], S["oh1"], m, b)
                    v.tensor_copy(maskb[:, :, :], S["oh1"][:, :, :]).then_inc(sems["mask_done"], 1)
                    v.tensor_tensor(out=S["lg"][:, :, :], in0=S["lg"][:, :, :], in1=per_tile(S["m1"]), op=ALU.subtract)\
                        .then_inc(sems["mD_done"], 1)
                    step(v.tensor_tensor(out=S["t8a"][:, :, :], in0=S["oh1"][:, :, :], in1=per_token(base128, E),
                                         op=ALU.mult), m, b)
                    step(v.tensor_reduce(S["slot"][:, :], S["t8a"][:, :, :], AX, ALU.add), m, b)
                elif what == "d_slots":
                    S, m = S2, "vD"
                    dve.wait_ge(sems["pos_ps_done"], raised("pos_ps_done", b, 1))
                    step(v.tensor_tensor(out=S["t8b"][:, :, :], in0=S["oh1"][:, :, :],
                                         in1=PS[:, 5, 0:NT * E].rearrange("p (t e) -> p t e", e=E),
                                         op=ALU.mult), m, b)
                    step(v.tensor_reduce(S["pos"][:, :], S["t8b"][:, :, :], AX, ALU.add), m, b)
                    v.tensor_tensor(out=S["slot"][:, :], in0=S["slot"][:, :], in1=S["pos"][:, :], op=ALU.add)
                    step(v.tensor_scalar(S["over"][:, :], S["pos"][:, :], float(CAP), None, ALU.is_ge), m, b)
                    step(v.scalar_tensor_tensor(out=S["ms"][:, :], in0=S["over"][:, :], scalar=float(SLOTS),
                                                in1=S["slot"][:, :], op0=ALU.mult, op1=ALU.add), m, b)
                    v.tensor_copy(put_i[:, :], S["ms"][:, :]).then_inc(sems["put_done"], 1)
                    step(v.tensor_scalar(S["m2"][:, :], S["slot"][:, :], float(SLOTS - 1), None, ALU.min), m, b)
                    v.tensor_copy(get_i[:, :], S["m2"][:, :]).then_inc(sems["get_done"], 1)
                elif what == "d_gate":
                    S, m = S2, "vD"
                    dve.wait_ge(sems["exD_done"], raised("exD_done", b, 1))
                    step(v.tensor_reduce(S["w1"][:, :], S["ex"][:, :, :], AX, ALU.add), m, b)
                    step(v.reciprocal(S["w1"][:, :], S["w1"][:, :]), m, b)
                    step(v.tensor_scalar(S["w2"][:, :], S["over"][:, :], -1.0, 1.0, ALU.mult, ALU.add), m, b)
                    step(v.tensor_tensor(out=S["gk"][:, :], in0=S["w1"][:, :], in1=S["w2"][:, :], op=ALU.mult), m, b)

            schedule(dve, part)

        @block.tensor
        def _(pe):
            m = nc.tensor

            pe.wait_ge(consts_done, CONSTS)
            pe.wait_ge(setup_v, 4)
            pe.wait_ge(first_in, 16 * N_FIRST)
            for i in range(NI):
                ins = m.transpose(PS[:, 6, i * P:(i + 1) * P], kn[:, i, :], ident[:, :])
            ins.then_inc(setup_pe, 1)
            pe.wait_ge(setup_a, 4)

            def turn(b, src, bank, done, wait_name, wait_k):
                pe.wait_ge(sems[wait_name], raised(wait_name, b, wait_k))
                for t in range(NT):
                    h, r = t // TPC, t % TPC
                    ins = m.transpose(PS[:, bank + h, r * P:(r + 1) * P], src[:, t, :], ident[:, :])
                    if r == TPC - 1:
                        ins.then_inc(sems[done], 1)

            def logits(b, xT, w, bank, xT_done, done):
                pe.wait_ge(sems[xT_done], raised(xT_done, b, 2))
                for t in range(NT):
                    ins = m.matmul(PS[:, bank, t * E:(t + 1) * E], xT[:, t * P:(t + 1) * P], w[:, :],
                                   start=True, stop=True)
                ins.then_inc(sems[done], 1)

            def up(b, j):
                h, e, f = j // (E * NFB), j // NFB % E, j % NFB
                if j >= 2:
                    pe.wait_ge(sems["relu_done"], raised("relu_done", b, j - 1))
                m.matmul(PS[:, Z0 + j % 2, :], w1b_s[:, e, f * P:(f + 1) * P], XT1[:, h * CH:(h + 1) * CH],
                         start=True, stop=True).then_inc(sems["z_ps_done"], 1)

            def gate(b, j):
                h, e = j // (E * NFB), j // NFB % E
                if j:
                    pe.wait_ge(sems["hg_done"], raised("hg_done", b, j))
                m.matmul(PS[:, GATE, :], sel_gate[:, e, :], g3T[:, h * CH:(h + 1) * CH],
                         start=True, stop=True).then_inc(sems["gate_ps_done"], 1)

            def down(b, j):
                h, e, f = j // (E * NFB), j // NFB % E, j % NFB
                if j % (E * NFB) == 0:
                    if h:
                        pe.wait_ge(sems["oT_done"], raised("oT_done", b, h))
                    for i in range(3):
                        m.matmul(PS[:, ACC, :], b2_p[:, i, :], g3T[:, h * CH:(h + 1) * CH],
                                 start=(i == 0), stop=False)
                pe.wait_ge(sems["hg_done"], raised("hg_done", b, j + 1))
                m.matmul(PS[:, ACC, :], w2b_s[:, e, f, :], HG[:, j % 3, :],
                         start=False, stop=(j % (E * NFB) == E * NFB - 1)).then_inc(sems["oB_acc_done"], 1)

            def spread(c, k):
                if k >= 2:
                    pe.wait_ge(sems["scan_done"], raised("scan_done", c, k - 1))
                for h in range(NC_):
                    ins = m.matmul(PS[:, SPR + 2 * (k % 2) + h, :], sel_bs[:, k % NS, :],
                                   bs3T[:, h * CH:(h + 1) * CH], start=True, stop=True)
                ins.then_inc(sems["spread_done"], 1)

            def spread_ahead(c, k, shared=False):
                if k + 1 < NK:
                    spread(c, k + 1)
                done = k - 1
                if done < NK and on_pe(done, shared):
                    pe.wait_ge(sems["scan_done"], raised("scan_done", c, done + 1))
                    d = done // NS
                    peers = [n for n in range(NS * d, NS * (d + 1)) if on_pe(n, True)]
                    for h in range(NC_):
                        ins = m.matmul(PS[:, 2 * d + h, :], ident[:, :], HS[:, done % N_H, h * CH:(h + 1) * CH],
                                       start=(done == peers[0]), stop=(done == peers[-1]))
                    ins.then_inc(pe_sum_done, 1)

            def part(what, b, c=None, a=None, d=None):
                if what == "setup_rest_done":
                    pe.wait_ge(weights_in, W_ALL)
                    pe.wait_ge(setup_v, 9)
                elif what == "mix_and_scan":
                    if b is not None:
                        pe.wait_ge(sems["g3T_done"], raised("g3T_done", b, 1))
                        gate(b, 0)
                    for j in range(NJ):
                        if b is not None:
                            if j + 1 < NJ:
                                up(b, j + 1)
                        if c is not None and len(scans_beside(j)) > 1:
                            spread_ahead(c, scans_beside(j)[0], b is None)
                        if b is not None and j >= 2:
                            down(b, j - 2)
                            if j % NFB == 0:
                                gate(b, j)
                        if c is not None:
                            spread_ahead(c, scans_beside(j)[-1], b is None)
                    if b is not None:
                        down(b, NJ - 2)
                        down(b, NJ - 1)
                elif what == "scan_ahead":
                    if c.start == 0:
                        pe.wait_ge(sems["bs3T_done"], raised("bs3T_done", b, 1))
                        pe.wait_ge(sems["vrel_done"], raised("vrel_done", b, 4))
                        spread(b, 0)
                    for k in c:
                        spread_ahead(b, k)
                elif what == "c_out":
                    pe.wait_ge(sems["yz_done"], raised("yz_done", b, ND))
                    for t in range(NT):
                        h, r = t // TPC, t % TPC
                        for i in range(ND):
                            ins = m.matmul(PS[:, 6 + h, r * P:(r + 1) * P], YX[:, i, t * P:(t + 1) * P],
                                           wout_s[:, i, :], start=(i == 0), stop=(i == ND - 1))
                        if r == TPC - 1:
                            ins.then_inc(sems["oC_ps_done"], 1)
                elif what == "b_turn_back":
                    for h in range(NC_):
                        pe.wait_ge(sems["oT_done"], raised("oT_done", b, h + 1))
                        for r in range(TPC):
                            ins = m.transpose(PS[:, h, r * P:(r + 1) * P], OT[:, h, r * P:(r + 1) * P],
                                              ident[:, :])
                        ins.then_inc(sems["oB_ps_done"], 1)
                elif what == "a_turn":
                    need_rows(pe, "oT_done", b)
                    turn(b, XL, 2, "qT_ps_done", "qn_done", 1)
                elif what == "a_scores":
                    h = c
                    need_rows(pe, "yB_done", b)
                    for u in (2 * h, 2 * h + 1):
                        i2, bank = 2 * (u % 2), 2 - 2 * (u % 2)
                        pe.wait_ge(sems["qT_done"], raised("qT_done", b, 2))
                        if u >= 2:
                            pe.wait_ge(sems["clip_done"], raised("clip_done", b, u - 1))
                        for i in range(i2, i2 + 2):
                            ins = m.matmul(PS[:, bank + i - i2, :], knT[:, i * P:(i + 1) * P], XT1[:, h * CH:(h + 1) * CH],
                                           start=True, stop=True)
                        ins.then_inc(sems["s_ps_done"], 1)
                elif what == "a_mix":
                    for h in (c,):
                        pe.wait_ge(sems["bpow_done"], raised("bpow_done", b, h + 1))
                        for r in range(TPC):
                            for i in range(NI):
                                ins = m.matmul(PS[:, 2 + h, r * P:(r + 1) * P], L1[:, h, i, r * P:(r + 1) * P],
                                               qw[:, i, :], start=(i == 0), stop=(i == NI - 1))
                        ins.then_inc(sems["xo_ps_done"], 1)
                elif what == "b_turn":
                    turn(b, X1, 0, "x1T_ps_done", "x1_done", 1)
                elif what == "b_logits":
                    logits(b, XT1, wr_s, 2, "x1T_done", "lgB_ps_done")
                elif what == "b_route" and c == 1:
                    pe.wait_ge(weights_in, W_ALL)
                    up(b, 0)
                    pe.wait_ge(sems["g3_done"], raised("g3_done", b, 1))
                    for t in range(NT):
                        ins = m.transpose(g3T_ps[0:3 * E, t * P:(t + 1) * P],
                                          g3[:, t].rearrange("p a e -> p (a e)"), identb[:, :])
                    ins.then_inc(sems["g3T_ps_done"], 1)
                elif what == "c_turn":
                    turn(b, X2, 6, "x2T_ps_done", "x2_done", 1)
                elif what == "c_in":
                    pe.wait_ge(sems["x2T_done"], raised("x2T_done", b, 2))
                    for what_in, first_d, done in (("xs", 0, "xs_ps_done"), ("z", ND, "z_in_ps_done")):
                        for k in range(ND * NC_):
                            if what_in == "xs" and k == 2:
                                need_rows(pe, "put_done", b)
                            if what_in == "z":
                                pe.wait_ge(sems["xs_done"], raised("xs_done", b, k + 1))
                            d, h = first_d + k // NC_, k % NC_
                            m.matmul(PS[:, in_bank(k), :], win_s[:, d * P:(d + 1) * P],
                                     XT2[:, h * CH:(h + 1) * CH], start=True, stop=True)\
                                .then_inc(sems[done], 1)
                    pe.wait_ge(sems["zs_done"], raised("zs_done", b, 4))
                elif what == "c_delta" and c == 0:
                    need_rows(pe, "yD_done", b)
                    pe.wait_ge(sems["xa_done"], raised("xa_done", b, ND))
                    for d in range(ND):
                        for h in range(NC_):
                            for i in range(ND):
                                ins = m.matmul(PS[:, 4 + NC_ * d + h, :], wdt_s[:, i, d * P:(d + 1) * P],
                                               XA[:, i, h * CH:(h + 1) * CH], start=(i == 0), stop=(i == ND - 1))
                            ins.then_inc(sems["dt_ps_done"], 1)
                    pe.wait_ge(sems["vrel_done"], raised("vrel_done", b, 2))
                    for t in range(NT):
                        for i in range(ND):
                            ins = m.matmul(PS[:, 4, t * NS:(t + 1) * NS], XA[:, i, t * P:(t + 1) * P],
                                           wx_s[:, i, :], start=(i == 0), stop=(i == ND - 1))
                    ins.then_inc(sems["bs_ps_done"], 1)
                elif what == "c_delta":
                    need_apart(pe, "bs3_done", b, 1)
                    for t in range(NT):
                        ins = m.transpose(bs3T_ps[0:3 * NS, t * P:(t + 1) * P],
                                          bs3[:, t].rearrange("p a n -> p (a n)"), identb[:, :])
                    ins.then_inc(sems["bs3T_ps_done"], 1)
                elif what == "d_turn":
                    turn(b, X3, 4, "x3T_ps_done", "x3_done", 1)
                elif what == "d_route":
                    logits(b, XT3, wg_s, 4, "x3T_done", "lgD_ps_done")
                elif what == "d_slots":
                    pe.wait_ge(sems["mask_done"], raised("mask_done", b, 1))
                    pos_ps = PS[:, 5, 0:NT * E].rearrange("p (t e) -> p t e", e=E)
                    m.matmul(pos_ps, before[:, :], maskb[:, :, :], start=True, stop=False, skip_group_check=True)
                    for t in range(NT - 1):
                        ins = m.matmul(pos_ps[:, t + 1:NT, :], onesb[:, :],
                                       maskb[:, t:t + 1, :].to_broadcast([P, NT - 1 - t, E]),
                                       start=False, stop=(t == NT - 2), skip_group_check=True)
                    ins.then_inc(sems["pos_ps_done"], 1)
                elif what == "d_slots_turn":
                    turn(b, XD, 4, "xdT_ps_done", "slots_loaded", 16)
                elif what == "d_ffn":
                    for e in range(E + 1):
                        if e < E:
                            pe.wait_ge(sems["xdT_done"], raised("xdT_done", b, 2))
                            if e >= 2:
                                pe.wait_ge(sems["gelu_done"], raised("gelu_done", b, e - 1))
                            for f in range(NFD):
                                ins = m.matmul(PS[:, 6 + e % 2, f * P:(f + 1) * P],
                                               w1d_s[:, e, f * P:(f + 1) * P], XDT[:, e * P:(e + 1) * P],
                                               start=True, stop=True)
                            ins.then_inc(sems["g_ps_done"], 1)
                        if e:
                            pe.wait_ge(sems["gelu_done"], raised("gelu_done", b, e))
                            h, r = (e - 1) // TPC, (e - 1) % TPC
                            for f in range(NFD):
                                ins = m.matmul(PS[:, 4 + h, r * P:(r + 1) * P], GE[:, (e - 1) % 2, f, :],
                                               w2d_s[:, e - 1, f, :], start=(f == 0), stop=(f == NFD - 1))
                            ins.then_inc(sems["yD_ps_done"], 1)

            schedule(pe, part)


_INS = [
    "L0_attn_hidden_states", "L0_attn_ln_weight", "L0_attn_ln_bias", "L0_attn_k_weight", "L0_attn_q_weight",
    "L0_attn_bias", "L0_ffn_Wr", "L0_ffn_br", "L0_ffn_W1", "L0_ffn_b1", "L0_ffn_W2", "L0_ffn_b2",
    "L1_attn_W_in", "L1_attn_conv_w", "L1_attn_conv_b", "L1_attn_A_log", "L1_attn_D", "L1_attn_W_x",
    "L1_attn_W_dt", "L1_attn_b_dt", "L1_attn_W_out", "L1_ffn_Wg", "L1_ffn_W1", "L1_ffn_W2",
]
_OUTS = [((8, 1024, 128), "float32")]


def kernel(**inputs):
    import numpy as _np
    import concourse.bacc as _bacc
    from concourse import mybir as _mybir
    from concourse.bass_utils import run_bass_kernel_spmd as _run

    nc = _bacc.Bacc("TRN2", target_bir_lowering=False, num_devices=1)
    arrays, args = {}, []
    for name in _INS:
        a = _np.ascontiguousarray(inputs[name])
        arrays[f"in_{name}_dram"] = a
        args.append(nc.dram_tensor(f"in_{name}_dram", a.shape, _mybir.dt.from_np(a.dtype), kind="ExternalInput").ap())
    for i, (shape, dtype) in enumerate(_OUTS):
        dt = _mybir.dt.from_np(_np.dtype(dtype))
        args.append(nc.dram_tensor(f"out_{i}_dram", shape, dt, kind="ExternalOutput").ap())
    build_layer_stack(nc, *args)
    r = _run(nc, [arrays], core_ids=[0])
    got = tuple(r.results[0][f"out_{i}_dram"] for i in range(len(_OUTS)))
    return got[0]
```
